# Optimizing a Trainium2 kernel written in Bass

```python
import numpy as np
import jax
import jax.numpy as jnp

def _softmax(x, axis=-1):
    return jax.nn.softmax(x, axis=axis)

def _gelu(x):
    return jax.nn.gelu(x, approximate=True)

def _silu(x):
    return jax.nn.silu(x)

def _sigmoid(x):
    return jax.nn.sigmoid(x)

def _layernorm(x, axis=-1, eps=1e-05):
    m = jnp.mean(x, axis=axis, keepdims=True)
    v = jnp.var(x, axis=axis, keepdims=True)
    return (x - m) / jnp.sqrt(v + eps)

def _scatter_add(tgt, idx, src, axis=0):
    return tgt.at[idx].add(src)

def _segment_sum(src, seg, n):
    return jax.ops.segment_sum(src, seg, n)
kernel_name = 'mk_conv_preact_d4_conv_nchw1024_r4_f8f649'

def setup_inputs(seed: int=0):
    np.random.seed(seed)
    _w = jnp.asarray

    def _rec_inputs():
        import jax
        import jax.numpy as jnp
        _gk = jax.random.key(seed)
        x = -0.0002023 + 1 * jax.random.normal(jax.random.fold_in(_gk, 1), (32, 256, 14, 14), jnp.float32)
        return x
    x = _rec_inputs()

    def _L0_conv_setup():
        import jax, jax.numpy as jnp
        from jax import lax
        import numpy as np
        B, INP, WIDTH, OUTP, E, H = (32, 256, 64, 256, 8, 14)
        EPS = 1e-05

        def _route(x, w, b):
            return jax.nn.sigmoid(x.mean(axis=(2, 3)) @ w + b)

        def _cond_conv(x, w, rw, stride=1, padding=0, dilation=1, groups=1):
            Bn, Cin, Hh, Ww = x.shape
            _, Cout, Cin_g, kh, kw = w.shape
            cw = jnp.einsum('be,eoikl->boikl', rw, w).reshape(Bn * Cout, Cin_g, kh, kw)
            out = lax.conv_general_dilated(x.reshape(1, Bn * Cin, Hh, Ww), cw, window_strides=(stride, stride), padding=[(padding, padding), (padding, padding)], rhs_dilation=(dilation, dilation), feature_group_count=Bn * groups, dimension_numbers=('NCHW', 'OIHW', 'NCHW'))
            return out.reshape(Bn, Cout, out.shape[2], out.shape[3])

        def _bn(x, g, b, m, v):
            inv = lax.rsqrt(v + EPS) * g
            return x * inv[None, :, None, None] + (b - m * inv)[None, :, None, None]
        key = jax.random.key(seed)
        ks = jax.random.split(key, 12)
        n = lambda k, s, sc=0.05: jax.random.normal(k, s, jnp.float32) * sc
        return {'x': jax.random.normal(ks[0], (B, INP, H, H), jnp.float32), 'w1': n(ks[1], (E, WIDTH, INP, 1, 1)), 'w2': n(ks[2], (E, WIDTH, WIDTH, 3, 3)), 'w3': n(ks[3], (E, OUTP, WIDTH, 1, 1)), 'r1_w': n(ks[4], (INP, E)), 'r1_b': jnp.zeros((E,), jnp.float32), 'r2_w': n(ks[5], (WIDTH, E)), 'r2_b': jnp.zeros((E,), jnp.float32), 'r3_w': n(ks[6], (WIDTH, E)), 'r3_b': jnp.zeros((E,), jnp.float32), 'bn1_g': jax.random.uniform(ks[7], (WIDTH,), jnp.float32, 0.5, 1.5), 'bn1_b': n(ks[8], (WIDTH,), 0.1), 'bn1_m': jnp.zeros((WIDTH,), jnp.float32), 'bn1_v': jnp.ones((WIDTH,), jnp.float32), 'bn2_g': jax.random.uniform(ks[9], (WIDTH,), jnp.float32, 0.5, 1.5), 'bn2_b': n(ks[10], (WIDTH,), 0.1), 'bn2_m': jnp.zeros((WIDTH,), jnp.float32), 'bn2_v': jnp.ones((WIDTH,), jnp.float32), 'bn3_g': jax.random.uniform(ks[11], (OUTP,), jnp.float32, 0.5, 1.5), 'bn3_b': jnp.zeros((OUTP,), jnp.float32), 'bn3_m': jnp.zeros((OUTP,), jnp.float32), 'bn3_v': jnp.ones((OUTP,), jnp.float32)}
    _L0_conv_all = _L0_conv_setup()
    _L0_conv_in = {k: v for k, v in _L0_conv_all.items() if k in ('w1', 'w2', 'w3', 'r1_w', 'r1_b', 'r2_w', 'r2_b', 'r3_w', 'r3_b', 'bn1_g', 'bn1_b', 'bn1_m', 'bn1_v', 'bn2_g', 'bn2_b', 'bn2_m', 'bn2_v', 'bn3_g', 'bn3_b', 'bn3_m', 'bn3_v')}
    del _L0_conv_all

    def _L1_conv_setup():
        import jax, jax.numpy as jnp
        import numpy as np
        from jax import lax
        C1 = 256
        C2 = 256
        D_STATE = 8
        HEADS = 2
        D_INNER = 256
        D_HEAD = D_INNER // HEADS

        def _mobius_perm(mobius, H, W):
            ys, xs = jnp.meshgrid(jnp.linspace(-1.0, 1.0, H), jnp.linspace(-1.0, 1.0, W), indexing='ij')
            z = (xs + 1j * ys).reshape(-1).astype(jnp.complex64)
            perms = []
            for h in range(mobius.shape[0]):
                a, b, c, d = (mobius[h, 0], mobius[h, 1], mobius[h, 2], mobius[h, 3])
                s = jnp.sqrt(jnp.clip(jnp.abs(a * d - b * c), 0.001))
                a, b, c, d = (a / s, b / s, c / s, d / s)
                w = (a * z + b) / (c * z + d + 1e-06)
                score = jnp.real(w) + 1.3 * jnp.imag(w)
                perms.append(jnp.argsort(score))
            return jnp.stack(perms, 0)

        def _gather_last(v, idx):
            return jnp.take_along_axis(v, jnp.broadcast_to(idx, v.shape[:-1] + (idx.shape[-1],)), axis=-1)

        def _selective_scan(x, dt, A, Bt, Ct, D):
            Bsz, Hh, Dh, N = x.shape
            S = A.shape[-1]
            dA = jnp.exp(dt[:, :, None, :] * A[None, :, :, None])
            dB = dt[:, :, None, :] * Bt

            def step(h, inp):
                dA_t, dB_t, x_t, C_t = inp
                h = dA_t[:, :, None, :] * h + dB_t[:, :, None, :] * x_t[..., None]
                y_t = jnp.einsum('bhds,bhs->bhd', h, C_t)
                return (h, y_t)
            h0 = jnp.zeros((Bsz, Hh, Dh, S), x.dtype)
            inputs = (jnp.moveaxis(dA, -1, 0), jnp.moveaxis(dB, -1, 0), jnp.moveaxis(x, -1, 0), jnp.moveaxis(Ct, -1, 0))
            _, ys = lax.scan(step, h0, inputs)
            return jnp.moveaxis(ys, 0, -1) + D[None, :, None, None] * x
        key = jax.random.key(seed)
        ks = jax.random.split(key, 8)
        S = D_STATE
        x = jax.random.normal(ks[0], (8, C1, 32, 32), jnp.float32)
        in_proj_w = jax.random.normal(ks[1], (3 * D_INNER, C1), jnp.float32) / np.sqrt(C1)
        in_proj_b = jnp.zeros((3 * D_INNER,), jnp.float32)
        dw_w = jax.random.normal(ks[2], (D_INNER, 1, 3), jnp.float32) / np.sqrt(3.0)
        dw_b = jnp.zeros((D_INNER,), jnp.float32)
        dbc_w = jax.random.normal(ks[3], (HEADS * (1 + 2 * S), D_INNER), jnp.float32) / np.sqrt(D_INNER)
        dbc_b = jnp.zeros((HEADS * (1 + 2 * S),), jnp.float32)
        A_log = jnp.log(jnp.tile(jnp.arange(1, S + 1, dtype=jnp.float32), (HEADS, 1)))
        Dparam = jnp.ones((HEADS,), jnp.float32)
        mobius = jnp.tile(jnp.array([[1.0, 0.0, 0.0, 1.0]], jnp.float32), (HEADS, 1)) + 0.05 * jax.random.normal(ks[4], (HEADS, 4), jnp.float32)
        out_proj_w = jax.random.normal(ks[5], (C2, D_INNER), jnp.float32) / np.sqrt(D_INNER)
        out_proj_b = jnp.zeros((C2,), jnp.float32)
        return dict(x=x, in_proj_w=in_proj_w, in_proj_b=in_proj_b, dw_w=dw_w, dw_b=dw_b, dbc_w=dbc_w, dbc_b=dbc_b, A_log=A_log, Dparam=Dparam, mobius=mobius, out_proj_w=out_proj_w, out_proj_b=out_proj_b)
    _L1_conv_all = _L1_conv_setup()
    _L1_conv_in = {k: v for k, v in _L1_conv_all.items() if k in ('in_proj_w', 'in_proj_b', 'dw_w', 'dw_b', 'dbc_w', 'dbc_b', 'A_log', 'Dparam', 'mobius', 'out_proj_w', 'out_proj_b')}
    del _L1_conv_all

    def _L2_conv_setup():
        import jax, jax.numpy as jnp
        import numpy as np
        EPS = 1e-05

        def _bn(x, g, b, m, v):
            s = (g / jnp.sqrt(v + EPS))[None, :, None, None]
            return (x - m[None, :, None, None]) * s + b[None, :, None, None]

        def _conv1x1(x, w, b):
            return jnp.einsum('bihw,oi->bohw', x, w) + b[None, :, None, None]

        def _conv3x3(x, w, b):
            y = jax.lax.conv_general_dilated(x, w, (1, 1), ((1, 1), (1, 1)), dimension_numbers=('NCHW', 'OIHW', 'NCHW'))
            return y + b[None, :, None, None]

        def _deform_conv3x3(x, offset, w, b):
            B, C, H, W = x.shape
            off = offset.reshape(B, 9, 2, H, W)
            dy, dx = (off[:, :, 0], off[:, :, 1])
            k = jnp.arange(9)
            ky = (k // 3 - 1).astype(x.dtype)
            kx = (k % 3 - 1).astype(x.dtype)
            hh = jnp.arange(H, dtype=x.dtype)
            ww = jnp.arange(W, dtype=x.dtype)
            py = hh[None, None, :, None] + ky[None, :, None, None] + dy
            px = ww[None, None, None, :] + kx[None, :, None, None] + dx
            y0 = jnp.floor(py)
            x0 = jnp.floor(px)
            ly = py - y0
            lx = px - x0
            y0i = y0.astype(jnp.int32)
            x0i = x0.astype(jnp.int32)
            xf = x.reshape(B, C, H * W)

            def gather(yi, xi):
                valid = (yi >= 0) & (yi < H) & (xi >= 0) & (xi < W)
                idx = jnp.clip(yi, 0, H - 1) * W + jnp.clip(xi, 0, W - 1)
                idx = idx.reshape(B, 1, -1)
                g = jnp.take_along_axis(xf, jnp.broadcast_to(idx, (B, C, idx.shape[-1])), axis=2)
                return g.reshape(B, C, 9, H, W) * valid[:, None].astype(x.dtype)
            v00 = gather(y0i, x0i)
            v01 = gather(y0i, x0i + 1)
            v10 = gather(y0i + 1, x0i)
            v11 = gather(y0i + 1, x0i + 1)
            wy1 = ly[:, None]
            wy0 = 1.0 - wy1
            wx1 = lx[:, None]
            wx0 = 1.0 - wx1
            val = v00 * wy0 * wx0 + v01 * wy0 * wx1 + v10 * wy1 * wx0 + v11 * wy1 * wx1
            Co = w.shape[0]
            return jnp.einsum('bckhw,ock->bohw', val, w.reshape(Co, C, 9)) + b[None, :, None, None]
        key = jax.random.key(seed)
        ks = jax.random.split(key, 24)
        B, Cin, H, W = (16, 256, 32, 32)
        C = 64
        f = jnp.float32
        d = {}
        d['x'] = jax.random.normal(ks[0], (B, Cin, H, W), f)
        d['conv1_w'] = jax.random.normal(ks[1], (C, Cin), f) * (1.0 / np.sqrt(Cin))
        d['conv1_b'] = jax.random.normal(ks[2], (C,), f) * 0.05
        d['bn1_g'] = jax.random.uniform(ks[3], (C,), f, 0.5, 1.5)
        d['bn1_b'] = jax.random.normal(ks[4], (C,), f) * 0.05
        d['bn1_m'] = jax.random.normal(ks[5], (C,), f) * 0.05
        d['bn1_v'] = jax.random.uniform(ks[6], (C,), f, 0.5, 1.5)
        d['off_w'] = jax.random.normal(ks[7], (18, C, 3, 3), f) * 0.01
        d['off_b'] = jax.random.normal(ks[8], (18,), f) * 0.01
        d['dconv_w'] = jax.random.normal(ks[9], (C, C, 3, 3), f) * (1.0 / np.sqrt(9 * C))
        d['dconv_b'] = jax.random.normal(ks[10], (C,), f) * 0.05
        d['bn2_g'] = jax.random.uniform(ks[11], (C,), f, 0.5, 1.5)
        d['bn2_b'] = jax.random.normal(ks[12], (C,), f) * 0.05
        d['bn2_m'] = jax.random.normal(ks[13], (C,), f) * 0.05
        d['bn2_v'] = jax.random.uniform(ks[14], (C,), f, 0.5, 1.5)
        d['conv2_w'] = jax.random.normal(ks[15], (4 * C, C), f) * (1.0 / np.sqrt(C))
        d['conv2_b'] = jax.random.normal(ks[16], (4 * C,), f) * 0.05
        d['bn3_g'] = jax.random.uniform(ks[17], (4 * C,), f, 0.5, 1.5)
        d['bn3_b'] = jax.random.normal(ks[18], (4 * C,), f) * 0.05
        d['bn3_m'] = jax.random.normal(ks[19], (4 * C,), f) * 0.05
        d['bn3_v'] = jax.random.uniform(ks[20], (4 * C,), f, 0.5, 1.5)
        return d
    _L2_conv_all = _L2_conv_setup()
    _L2_conv_in = {k: v for k, v in _L2_conv_all.items() if k in ('conv1_w', 'conv1_b', 'bn1_g', 'bn1_b', 'bn1_m', 'bn1_v', 'off_w', 'off_b', 'dconv_w', 'dconv_b', 'bn2_g', 'bn2_b', 'bn2_m', 'bn2_v', 'conv2_w', 'conv2_b', 'bn3_g', 'bn3_b', 'bn3_m', 'bn3_v')}
    del _L2_conv_all

    def _L3_conv_setup():
        import jax, jax.numpy as jnp
        import numpy as np
        CP = 1.0
        DP = 2
        EPS = 1e-05

        def kerv2d(x, w, stride, padding):
            y = jax.lax.conv_general_dilated(x, w, window_strides=(stride, stride), padding=[(padding, padding), (padding, padding)], dimension_numbers=('NCHW', 'OIHW', 'NCHW'))
            return (y + CP) ** DP

        def bn(x, g, b, m, v):
            inv = g / jnp.sqrt(v + EPS)
            return x * inv[None, :, None, None] + (b - m * inv)[None, :, None, None]
        key = jax.random.key(seed)
        ks = jax.random.split(key, 4)
        C_in, C_mid = (256, 64)
        d = {'x': jax.random.normal(ks[0], (32, C_in, 14, 14), jnp.float32), 'w1': jax.random.normal(ks[1], (C_mid, C_in, 1, 1), jnp.float32) * 0.03, 'w2': jax.random.normal(ks[2], (C_mid, C_mid, 3, 3), jnp.float32) * 0.02, 'w3': jax.random.normal(ks[3], (C_in, C_mid, 1, 1), jnp.float32) * 0.03}
        for i, c in zip((1, 2, 3), (C_mid, C_mid, C_in)):
            d[f'g{i}'] = jnp.ones((c,), jnp.float32)
            d[f'b{i}'] = jnp.zeros((c,), jnp.float32)
            d[f'm{i}'] = jnp.zeros((c,), jnp.float32)
            d[f'v{i}'] = jnp.ones((c,), jnp.float32)
        return d
    _L3_conv_all = _L3_conv_setup()
    _L3_conv_in = {k: v for k, v in _L3_conv_all.items() if k in ('w1', 'w2', 'w3', 'g1', 'b1', 'm1', 'v1', 'g2', 'b2', 'm2', 'v2', 'g3', 'b3', 'm3', 'v3')}
    del _L3_conv_all
    return {'x': x, 'L0_conv_w1': _L0_conv_in['w1'], 'L0_conv_w2': _L0_conv_in['w2'], 'L0_conv_w3': _L0_conv_in['w3'], 'L0_conv_r1_w': _L0_conv_in['r1_w'], 'L0_conv_r1_b': _L0_conv_in['r1_b'], 'L0_conv_r2_w': _L0_conv_in['r2_w'], 'L0_conv_r2_b': _L0_conv_in['r2_b'], 'L0_conv_r3_w': _L0_conv_in['r3_w'], 'L0_conv_r3_b': _L0_conv_in['r3_b'], 'L0_conv_bn1_g': _L0_conv_in['bn1_g'], 'L0_conv_bn1_b': _L0_conv_in['bn1_b'], 'L0_conv_bn1_m': _L0_conv_in['bn1_m'], 'L0_conv_bn1_v': _L0_conv_in['bn1_v'], 'L0_conv_bn2_g': _L0_conv_in['bn2_g'], 'L0_conv_bn2_b': _L0_conv_in['bn2_b'], 'L0_conv_bn2_m': _L0_conv_in['bn2_m'], 'L0_conv_bn2_v': _L0_conv_in['bn2_v'], 'L0_conv_bn3_g': _L0_conv_in['bn3_g'], 'L0_conv_bn3_b': _L0_conv_in['bn3_b'], 'L0_conv_bn3_m': _L0_conv_in['bn3_m'], 'L0_conv_bn3_v': _L0_conv_in['bn3_v'], 'L1_conv_in_proj_w': _L1_conv_in['in_proj_w'], 'L1_conv_in_proj_b': _L1_conv_in['in_proj_b'], 'L1_conv_dw_w': _L1_conv_in['dw_w'], 'L1_conv_dw_b': _L1_conv_in['dw_b'], 'L1_conv_dbc_w': _L1_conv_in['dbc_w'], 'L1_conv_dbc_b': _L1_conv_in['dbc_b'], 'L1_conv_A_log': _L1_conv_in['A_log'], 'L1_conv_Dparam': _L1_conv_in['Dparam'], 'L1_conv_mobius': _L1_conv_in['mobius'], 'L1_conv_out_proj_w': _L1_conv_in['out_proj_w'], 'L1_conv_out_proj_b': _L1_conv_in['out_proj_b'], 'L2_conv_conv1_w': _L2_conv_in['conv1_w'], 'L2_conv_conv1_b': _L2_conv_in['conv1_b'], 'L2_conv_bn1_g': _L2_conv_in['bn1_g'], 'L2_conv_bn1_b': _L2_conv_in['bn1_b'], 'L2_conv_bn1_m': _L2_conv_in['bn1_m'], 'L2_conv_bn1_v': _L2_conv_in['bn1_v'], 'L2_conv_off_w': _L2_conv_in['off_w'], 'L2_conv_off_b': _L2_conv_in['off_b'], 'L2_conv_dconv_w': _L2_conv_in['dconv_w'], 'L2_conv_dconv_b': _L2_conv_in['dconv_b'], 'L2_conv_bn2_g': _L2_conv_in['bn2_g'], 'L2_conv_bn2_b': _L2_conv_in['bn2_b'], 'L2_conv_bn2_m': _L2_conv_in['bn2_m'], 'L2_conv_bn2_v': _L2_conv_in['bn2_v'], 'L2_conv_conv2_w': _L2_conv_in['conv2_w'], 'L2_conv_conv2_b': _L2_conv_in['conv2_b'], 'L2_conv_bn3_g': _L2_conv_in['bn3_g'], 'L2_conv_bn3_b': _L2_conv_in['bn3_b'], 'L2_conv_bn3_m': _L2_conv_in['bn3_m'], 'L2_conv_bn3_v': _L2_conv_in['bn3_v'], 'L3_conv_w1': _L3_conv_in['w1'], 'L3_conv_w2': _L3_conv_in['w2'], 'L3_conv_w3': _L3_conv_in['w3'], 'L3_conv_g1': _L3_conv_in['g1'], 'L3_conv_b1': _L3_conv_in['b1'], 'L3_conv_m1': _L3_conv_in['m1'], 'L3_conv_v1': _L3_conv_in['v1'], 'L3_conv_g2': _L3_conv_in['g2'], 'L3_conv_b2': _L3_conv_in['b2'], 'L3_conv_m2': _L3_conv_in['m2'], 'L3_conv_v2': _L3_conv_in['v2'], 'L3_conv_g3': _L3_conv_in['g3'], 'L3_conv_b3': _L3_conv_in['b3'], 'L3_conv_m3': _L3_conv_in['m3'], 'L3_conv_v3': _L3_conv_in['v3']}

def reference(x, L0_conv_w1, L0_conv_w2, L0_conv_w3, L0_conv_r1_w, L0_conv_r1_b, L0_conv_r2_w, L0_conv_r2_b, L0_conv_r3_w, L0_conv_r3_b, L0_conv_bn1_g, L0_conv_bn1_b, L0_conv_bn1_m, L0_conv_bn1_v, L0_conv_bn2_g, L0_conv_bn2_b, L0_conv_bn2_m, L0_conv_bn2_v, L0_conv_bn3_g, L0_conv_bn3_b, L0_conv_bn3_m, L0_conv_bn3_v, L1_conv_in_proj_w, L1_conv_in_proj_b, L1_conv_dw_w, L1_conv_dw_b, L1_conv_dbc_w, L1_conv_dbc_b, L1_conv_A_log, L1_conv_Dparam, L1_conv_mobius, L1_conv_out_proj_w, L1_conv_out_proj_b, L2_conv_conv1_w, L2_conv_conv1_b, L2_conv_bn1_g, L2_conv_bn1_b, L2_conv_bn1_m, L2_conv_bn1_v, L2_conv_off_w, L2_conv_off_b, L2_conv_dconv_w, L2_conv_dconv_b, L2_conv_bn2_g, L2_conv_bn2_b, L2_conv_bn2_m, L2_conv_bn2_v, L2_conv_conv2_w, L2_conv_conv2_b, L2_conv_bn3_g, L2_conv_bn3_b, L2_conv_bn3_m, L2_conv_bn3_v, L3_conv_w1, L3_conv_w2, L3_conv_w3, L3_conv_g1, L3_conv_b1, L3_conv_m1, L3_conv_v1, L3_conv_g2, L3_conv_b2, L3_conv_m2, L3_conv_v2, L3_conv_g3, L3_conv_b3, L3_conv_m3, L3_conv_v3):
    import jax
    import jax.numpy as jnp

    def _L0_conv_ref(x, w1, w2, w3, r1_w, r1_b, r2_w, r2_b, r3_w, r3_b, bn1_g, bn1_b, bn1_m, bn1_v, bn2_g, bn2_b, bn2_m, bn2_v, bn3_g, bn3_b, bn3_m, bn3_v):
        import jax, jax.numpy as jnp
        from jax import lax
        import numpy as np
        B, INP, WIDTH, OUTP, E, H = (32, 256, 64, 256, 8, 14)
        EPS = 1e-05

        def _route(x, w, b):
            return jax.nn.sigmoid(x.mean(axis=(2, 3)) @ w + b)

        def _cond_conv(x, w, rw, stride=1, padding=0, dilation=1, groups=1):
            Bn, Cin, Hh, Ww = x.shape
            _, Cout, Cin_g, kh, kw = w.shape
            cw = jnp.einsum('be,eoikl->boikl', rw, w).reshape(Bn * Cout, Cin_g, kh, kw)
            out = lax.conv_general_dilated(x.reshape(1, Bn * Cin, Hh, Ww), cw, window_strides=(stride, stride), padding=[(padding, padding), (padding, padding)], rhs_dilation=(dilation, dilation), feature_group_count=Bn * groups, dimension_numbers=('NCHW', 'OIHW', 'NCHW'))
            return out.reshape(Bn, Cout, out.shape[2], out.shape[3])

        def _bn(x, g, b, m, v):
            inv = lax.rsqrt(v + EPS) * g
            return x * inv[None, :, None, None] + (b - m * inv)[None, :, None, None]
        identity = x
        rw1 = _route(x, r1_w, r1_b)
        out = jax.nn.relu(_bn(_cond_conv(x, w1, rw1), bn1_g, bn1_b, bn1_m, bn1_v))
        rw2 = _route(out, r2_w, r2_b)
        out = jax.nn.relu(_bn(_cond_conv(out, w2, rw2, stride=1, padding=1), bn2_g, bn2_b, bn2_m, bn2_v))
        rw3 = _route(out, r3_w, r3_b)
        out = _bn(_cond_conv(out, w3, rw3), bn3_g, bn3_b, bn3_m, bn3_v)
        return jax.nn.relu(out + identity)

    def _L1_conv_ref(x, in_proj_w, in_proj_b, dw_w, dw_b, dbc_w, dbc_b, A_log, Dparam, mobius, out_proj_w, out_proj_b):
        import jax, jax.numpy as jnp
        import numpy as np
        from jax import lax
        C1 = 256
        C2 = 256
        D_STATE = 8
        HEADS = 2
        D_INNER = 256
        D_HEAD = D_INNER // HEADS

        def _mobius_perm(mobius, H, W):
            ys, xs = jnp.meshgrid(jnp.linspace(-1.0, 1.0, H), jnp.linspace(-1.0, 1.0, W), indexing='ij')
            z = (xs + 1j * ys).reshape(-1).astype(jnp.complex64)
            perms = []
            for h in range(mobius.shape[0]):
                a, b, c, d = (mobius[h, 0], mobius[h, 1], mobius[h, 2], mobius[h, 3])
                s = jnp.sqrt(jnp.clip(jnp.abs(a * d - b * c), 0.001))
                a, b, c, d = (a / s, b / s, c / s, d / s)
                w = (a * z + b) / (c * z + d + 1e-06)
                score = jnp.real(w) + 1.3 * jnp.imag(w)
                perms.append(jnp.argsort(score))
            return jnp.stack(perms, 0)

        def _gather_last(v, idx):
            return jnp.take_along_axis(v, jnp.broadcast_to(idx, v.shape[:-1] + (idx.shape[-1],)), axis=-1)

        def _selective_scan(x, dt, A, Bt, Ct, D):
            Bsz, Hh, Dh, N = x.shape
            S = A.shape[-1]
            dA = jnp.exp(dt[:, :, None, :] * A[None, :, :, None])
            dB = dt[:, :, None, :] * Bt

            def step(h, inp):
                dA_t, dB_t, x_t, C_t = inp
                h = dA_t[:, :, None, :] * h + dB_t[:, :, None, :] * x_t[..., None]
                y_t = jnp.einsum('bhds,bhs->bhd', h, C_t)
                return (h, y_t)
            h0 = jnp.zeros((Bsz, Hh, Dh, S), x.dtype)
            inputs = (jnp.moveaxis(dA, -1, 0), jnp.moveaxis(dB, -1, 0), jnp.moveaxis(x, -1, 0), jnp.moveaxis(Ct, -1, 0))
            _, ys = lax.scan(step, h0, inputs)
            return jnp.moveaxis(ys, 0, -1) + D[None, :, None, None] * x
        Bsz, _, H, W = x.shape
        N = H * W
        heads, S = A_log.shape
        d_inner = dw_w.shape[0]
        d_head = d_inner // heads
        xz = jax.nn.silu(jnp.einsum('oc,bchw->bohw', in_proj_w, x) + in_proj_b[None, :, None, None])
        x_ssm, res, gate = jnp.split(xz, 3, axis=1)
        xf = x_ssm.reshape(Bsz, d_inner, N)
        xf = lax.conv_general_dilated(xf, dw_w, (1,), [(1, 1)], dimension_numbers=('NCH', 'OIH', 'NCH'), feature_group_count=d_inner) + dw_b[None, :, None]
        xf = jax.nn.silu(xf)
        x_h = xf.reshape(Bsz, heads, d_head, N)
        perm = _mobius_perm(mobius, H, W)
        x_h = _gather_last(x_h, perm[None, :, None, :])
        dbc = (jnp.einsum('oc,bcn->bon', dbc_w, xf) + dbc_b[None, :, None]).reshape(Bsz, heads, 1 + 2 * S, N)
        dt = jax.nn.softplus(dbc[:, :, 0])
        B_t = dbc[:, :, 1:1 + S]
        C_t = dbc[:, :, 1 + S:]
        dt = _gather_last(dt, perm[None, :, :])
        B_t = _gather_last(B_t, perm[None, :, None, :])
        C_t = _gather_last(C_t, perm[None, :, None, :])
        A = -jnp.exp(A_log)
        y_h = _selective_scan(x_h, dt, A, B_t, C_t, Dparam)
        inv = jnp.argsort(perm, axis=-1)
        y_h = _gather_last(y_h, inv[None, :, None, :])
        y = y_h.reshape(Bsz, d_inner, H, W)
        y = y * jax.nn.silu(gate) + res
        return jax.nn.silu(jnp.einsum('oc,bchw->bohw', out_proj_w, y) + out_proj_b[None, :, None, None])

    def _L2_conv_ref(x, conv1_w, conv1_b, bn1_g, bn1_b, bn1_m, bn1_v, off_w, off_b, dconv_w, dconv_b, bn2_g, bn2_b, bn2_m, bn2_v, conv2_w, conv2_b, bn3_g, bn3_b, bn3_m, bn3_v):
        import jax, jax.numpy as jnp
        import numpy as np
        EPS = 1e-05

        def _bn(x, g, b, m, v):
            s = (g / jnp.sqrt(v + EPS))[None, :, None, None]
            return (x - m[None, :, None, None]) * s + b[None, :, None, None]

        def _conv1x1(x, w, b):
            return jnp.einsum('bihw,oi->bohw', x, w) + b[None, :, None, None]

        def _conv3x3(x, w, b):
            y = jax.lax.conv_general_dilated(x, w, (1, 1), ((1, 1), (1, 1)), dimension_numbers=('NCHW', 'OIHW', 'NCHW'))
            return y + b[None, :, None, None]

        def _deform_conv3x3(x, offset, w, b):
            B, C, H, W = x.shape
            off = offset.reshape(B, 9, 2, H, W)
            dy, dx = (off[:, :, 0], off[:, :, 1])
            k = jnp.arange(9)
            ky = (k // 3 - 1).astype(x.dtype)
            kx = (k % 3 - 1).astype(x.dtype)
            hh = jnp.arange(H, dtype=x.dtype)
            ww = jnp.arange(W, dtype=x.dtype)
            py = hh[None, None, :, None] + ky[None, :, None, None] + dy
            px = ww[None, None, None, :] + kx[None, :, None, None] + dx
            y0 = jnp.floor(py)
            x0 = jnp.floor(px)
            ly = py - y0
            lx = px - x0
            y0i = y0.astype(jnp.int32)
            x0i = x0.astype(jnp.int32)
            xf = x.reshape(B, C, H * W)

            def gather(yi, xi):
                valid = (yi >= 0) & (yi < H) & (xi >= 0) & (xi < W)
                idx = jnp.clip(yi, 0, H - 1) * W + jnp.clip(xi, 0, W - 1)
                idx = idx.reshape(B, 1, -1)
                g = jnp.take_along_axis(xf, jnp.broadcast_to(idx, (B, C, idx.shape[-1])), axis=2)
                return g.reshape(B, C, 9, H, W) * valid[:, None].astype(x.dtype)
            v00 = gather(y0i, x0i)
            v01 = gather(y0i, x0i + 1)
            v10 = gather(y0i + 1, x0i)
            v11 = gather(y0i + 1, x0i + 1)
            wy1 = ly[:, None]
            wy0 = 1.0 - wy1
            wx1 = lx[:, None]
            wx0 = 1.0 - wx1
            val = v00 * wy0 * wx0 + v01 * wy0 * wx1 + v10 * wy1 * wx0 + v11 * wy1 * wx1
            Co = w.shape[0]
            return jnp.einsum('bckhw,ock->bohw', val, w.reshape(Co, C, 9)) + b[None, :, None, None]
        out = jax.nn.relu(_bn(_conv1x1(x, conv1_w, conv1_b), bn1_g, bn1_b, bn1_m, bn1_v))
        offset = _conv3x3(out, off_w, off_b)
        out = _deform_conv3x3(out, offset, dconv_w, dconv_b)
        out = _bn(out, bn2_g, bn2_b, bn2_m, bn2_v)
        out = _conv1x1(out, conv2_w, conv2_b)
        out = jax.nn.relu(_bn(out, bn3_g, bn3_b, bn3_m, bn3_v))
        return out

    def _L3_conv_ref(x, w1, w2, w3, g1, b1, m1, v1, g2, b2, m2, v2, g3, b3, m3, v3):
        import jax, jax.numpy as jnp
        import numpy as np
        CP = 1.0
        DP = 2
        EPS = 1e-05

        def kerv2d(x, w, stride, padding):
            y = jax.lax.conv_general_dilated(x, w, window_strides=(stride, stride), padding=[(padding, padding), (padding, padding)], dimension_numbers=('NCHW', 'OIHW', 'NCHW'))
            return (y + CP) ** DP

        def bn(x, g, b, m, v):
            inv = g / jnp.sqrt(v + EPS)
            return x * inv[None, :, None, None] + (b - m * inv)[None, :, None, None]
        identity = x
        h = bn(kerv2d(x, w1, 1, 0), g1, b1, m1, v1)
        h = bn(kerv2d(h, w2, 1, 1), g2, b2, m2, v2)
        h = bn(kerv2d(h, w3, 1, 0), g3, b3, m3, v3)
        return h + identity

    def _gn(v, G=32, eps=1e-05):
        B_, C_, H_, W_ = v.shape
        g = v.reshape(B_, G, C_ // G, H_, W_)
        m = jnp.mean(g, axis=(2, 3, 4), keepdims=True)
        s = jnp.var(g, axis=(2, 3, 4), keepdims=True)
        return ((g - m) / jnp.sqrt(s + eps)).reshape(v.shape)

    def _ln_c(v, eps=1e-06):
        m = jnp.mean(v, axis=1, keepdims=True)
        s = jnp.var(v, axis=1, keepdims=True)
        return (v - m) / jnp.sqrt(s + eps)

    def _ln_t(v, eps=1e-05):
        m = jnp.mean(v, axis=-1, keepdims=True)
        s = jnp.var(v, axis=-1, keepdims=True)
        return (v - m) / jnp.sqrt(s + eps)

    def _to_tokens(v):
        B_, C_, H_, W_ = v.shape
        return v.reshape(B_, C_, H_ * W_).transpose(0, 2, 1)

    def _from_tokens(t, like):
        B_, C_, H_, W_ = like.shape
        return t.transpose(0, 2, 1).reshape(B_, C_, H_, W_)
    x = x + _L0_conv_ref(_gn(x), L0_conv_w1, L0_conv_w2, L0_conv_w3, L0_conv_r1_w, L0_conv_r1_b, L0_conv_r2_w, L0_conv_r2_b, L0_conv_r3_w, L0_conv_r3_b, L0_conv_bn1_g, L0_conv_bn1_b, L0_conv_bn1_m, L0_conv_bn1_v, L0_conv_bn2_g, L0_conv_bn2_b, L0_conv_bn2_m, L0_conv_bn2_v, L0_conv_bn3_g, L0_conv_bn3_b, L0_conv_bn3_m, L0_conv_bn3_v)
    x = x + _L1_conv_ref(_gn(x), L1_conv_in_proj_w, L1_conv_in_proj_b, L1_conv_dw_w, L1_conv_dw_b, L1_conv_dbc_w, L1_conv_dbc_b, L1_conv_A_log, L1_conv_Dparam, L1_conv_mobius, L1_conv_out_proj_w, L1_conv_out_proj_b)
    x = x + _L2_conv_ref(_gn(x), L2_conv_conv1_w, L2_conv_conv1_b, L2_conv_bn1_g, L2_conv_bn1_b, L2_conv_bn1_m, L2_conv_bn1_v, L2_conv_off_w, L2_conv_off_b, L2_conv_dconv_w, L2_conv_dconv_b, L2_conv_bn2_g, L2_conv_bn2_b, L2_conv_bn2_m, L2_conv_bn2_v, L2_conv_conv2_w, L2_conv_conv2_b, L2_conv_bn3_g, L2_conv_bn3_b, L2_conv_bn3_m, L2_conv_bn3_v)
    x = x + _L3_conv_ref(_gn(x), L3_conv_w1, L3_conv_w2, L3_conv_w3, L3_conv_g1, L3_conv_b1, L3_conv_m1, L3_conv_v1, L3_conv_g2, L3_conv_b2, L3_conv_m2, L3_conv_v2, L3_conv_g3, L3_conv_b3, L3_conv_m3, L3_conv_v3)
    return x

_drawn_inputs = setup_inputs


def setup_inputs(seed=0):
    import zlib

    import numpy as np

    out = dict(_drawn_inputs(seed))
    spreads = {'L0_conv_r1_b': (0.0, 0.733),
     'L0_conv_r2_b': (0.0, 0.8),
     'L0_conv_r3_b': (0.0, 0.739),
     'L0_conv_bn1_m': (0.0, 0.511),
     'L0_conv_bn1_v': (1.0, 0.6),
     'L0_conv_bn2_m': (0.0, 0.479),
     'L0_conv_bn2_v': (1.0, 0.6),
     'L0_conv_bn3_b': (0.0, 0.1),
     'L0_conv_bn3_m': (0.0, 0.1),
     'L0_conv_bn3_v': (1.0, 0.6),
     'L1_conv_in_proj_b': (0.0, 0.425),
     'L1_conv_dw_b': (0.0, 0.8),
     'L1_conv_dbc_b': (0.0, 0.8),
     'L1_conv_Dparam': (1.0, 0.6),
     'L1_conv_out_proj_b': (0.0, 0.305),
     'L3_conv_g1': (1.0, 0.2),
     'L3_conv_b1': (0.0, 0.479),
     'L3_conv_m1': (0.0, 0.452),
     'L3_conv_v1': (1.0, 0.6),
     'L3_conv_g2': (1.0, 0.2),
     'L3_conv_b2': (0.0, 0.463),
     'L3_conv_m2': (0.0, 0.462),
     'L3_conv_v2': (1.0, 0.2),
     'L3_conv_g3': (1.0, 0.2),
     'L3_conv_b3': (0.0, 0.268),
     'L3_conv_m3': (0.0, 0.272),
     'L3_conv_v3': (1.0, 0.2)}
    factors = {'L0_conv_r1_w': 8.0,
     'L0_conv_r2_w': 2.726,
     'L0_conv_bn1_b': 4.01,
     'L0_conv_bn2_b': 3.497,
     'L1_conv_dbc_w': 3.017,
     'L1_conv_A_log': 8.0,
     'L1_conv_mobius': 8.0,
     'L2_conv_conv1_b': 4.657,
     'L2_conv_bn1_b': 5.097,
     'L2_conv_bn1_m': 4.136,
     'L2_conv_off_b': 8.0,
     'L2_conv_dconv_b': 2.98,
     'L2_conv_bn2_b': 3.85,
     'L2_conv_bn2_m': 3.608,
     'L2_conv_conv2_b': 3.512,
     'L2_conv_bn3_b': 3.683,
     'L2_conv_bn3_m': 3.737}
    for name, (base, spread) in spreads.items():
        noise = np.random.default_rng([zlib.crc32(name.encode()), seed]).standard_normal(out[name].shape)
        drawn = base * np.exp(spread * noise) if base else spread * noise
        out[name] = jnp.asarray(drawn.astype(out[name].dtype))
    for name, factor in factors.items():
        out[name] = (out[name] * factor).astype(out[name].dtype)
    return out
```

```python
from contextlib import ExitStack

import concourse.bass as bass
from concourse import mybir

ALU = mybir.AluOpType
ACT = mybir.ActivationFunctionType
AX = mybir.AxisListType
F32 = mybir.dt.float32

BATCH, CH, HW = 32, 256, 14
N = HW * HW
G = 2
GROUPS = BATCH // G
CC = CH // 128
W = G * N
MID = 64
EXPERTS = 8
TAPS = 9
HEADS, STATE = 2, 8
HD = CH // HEADS
DBC = 1 + 2 * STATE
HT = N // 2
HR = HW // 2
HS = HR * (HW + 2)
CHUNK = 14
NCH = N // CHUNK
CPT = NCH // 2
CS = NCH * STATE
PAD = HW + 2
XD = HD + DBC
GN_EPS = 1e-5
BN_EPS = 1e-5
STAGES = 4
(BN_A1, BN_A2, BN_A3, BN_C1, BN_C2, BN_C3, BN_D1, BN_D2, BN_D3) = (0, 1, 2, 4, 5, 6, 8, 9, 10)
NBN = 12
ROW_A, ROW_D, ROW_MOB = 0, HEADS * STATE, HEADS * STATE + HEADS
ROW_BC = ROW_MOB + 4 * HEADS
ROW_R = [ROW_BC + EXPERTS * i for i in range(3)]
ROW_DBC = ROW_BC + 3 * EXPERTS
ROW_OFF = ROW_DBC + HEADS * DBC
ROWS = ROW_OFF + 2 * TAPS


def shape_constants():
    import numpy as np

    f = np.float32
    u = np.arange(HT)
    tok = np.stack([u, HT + u])
    t = np.arange(N)
    i, c = u % CHUNK, u // CHUNK
    tt = np.arange(CHUNK)
    step = np.arange(HW - 1, dtype=f) / f(HW - 1)
    line = np.append(-(f(1) - step) + step, f(1)).astype(f)
    k = np.arange(TAPS)
    sample = np.arange(128)
    grid = np.zeros((128, 2, TAPS, 2), f)
    for m in range(2):
        grid[:, m, :, 0] = (sample // PAD + HR * m)[:, None] + (k // 3 - 1)[None]
        grid[:, m, :, 1] = (sample % PAD)[:, None] + (k % 3 - 1)[None]
    parts_scan = [
        ("self", np.stack([tok[m][:, None] == t[None] for m in range(2)], 1)),
        ("before", np.stack([t[None] < tok[m][:, None] for m in range(2)], 1)),
        ("iota196", np.tile(t, (HT, 1))),
        ("xs", np.tile(line[t % HW], (HT, 1))),
        ("ys", np.tile(line[t // HW], (HT, 1))),
    ]
    parts98 = [
        ("later", (c[:, None] == c[None]) & (i[:, None] > i[None])),
        ("same", c[:, None] == c[None]),
        ("upto", i[:, None] <= tt[None]),
        ("at", i[:, None] == tt[None]),
        ("chunk7", c[:, None] == np.arange(CPT)[None]),
        ("chunk14", np.stack([(tok[m] // CHUNK)[:, None] == np.arange(NCH)[None] for m in range(2)], 1)),
        ("after", np.stack([(tok[m] // CHUNK)[:, None] > np.arange(NCH)[None] for m in range(2)], 1)),
        ("tri0", tok[0][:, None] <= t[None]),
        ("tri1", tok[1][:, None] <= t[None, HT:]),
    ]
    p = np.arange(128)
    parts128 = [
        ("ident", p[:, None] == p[None]),
        ("group", (p[:, None] // 8 == p[None] // 8) / 16.0),
        ("grid", grid),
        ("iota14", np.tile(np.arange(HW), (128, 1))),
    ]
    out = []
    for parts in (parts98, parts128, parts_scan):
        where, at, cols = {}, 0, []
        for name, a in parts:
            a = np.asarray(a, f)
            a = a.reshape(a.shape[0], -1)
            where[name] = (at, at + a.shape[1])
            at += a.shape[1]
            cols.append(a)
        out += [where, np.ascontiguousarray(np.concatenate(cols, 1))]
    return out


class Signal:

    def __init__(self, sem, per=1):
        self.sem, self.per = sem, per

    def count(self, g, k=None):
        return g * self.per + (self.per if k is None else k)


class Chain:

    def __init__(self, sem, per):
        self.sem, self.per, self.at = sem, per, 0

    def step(self):
        self.at += 1
        return 1

    def count(self, g, back=0):
        return g * self.per + self.at - back

    def end(self, what):
        assert self.at == self.per, (what, self.at, self.per)
        self.at = 0


class Banks:

    def __init__(self, tiles, filled, drained, fills):
        assert fills % len(tiles) == 0
        self.tiles, self.nb, self.per = tiles, len(tiles), fills // len(tiles)
        self.sems = filled, drained

    def tile(self, f):
        return self.tiles[f % self.nb]

    def filled(self, f):
        return self.sems[0][f % self.nb]

    def drained(self, f):
        return self.sems[1][f % self.nb]

    def empty(self, g, f):
        return g * self.per + f // self.nb

    def full(self, g, f):
        return self.empty(g, f) + 1


STEPS = (11, 16, 12, 7)
VECTOR_STEPS = (60, 26, 8, 10)
NZERO = 7


def step_order(stages):
    return sorted(((i + 1) / STEPS[s], -s, i) for s in stages for i in range(STEPS[s]))


def for_rounds(eng, steps, chains=()):

    def one(r, stages):
        for _, s, i in step_order(stages):
            steps[-s](i, r + s)
        for s in stages:
            if s in chains:
                chains[s].end((str(eng), s))

    for r in range(STAGES):
        one(r, range(min(r + 1, STAGES)))
    with eng.Fori(STAGES, GROUPS) as r:
        one(r, range(STAGES))
    for r in range(GROUPS, GROUPS + STAGES - 1):
        one(r, range(r - GROUPS + 1, STAGES))


def build(nc, a, out, at98, at128, at_scan):
    ctx = ExitStack()
    with ctx:
        def sb(name, shape):
            return ctx.enter_context(nc.sbuf_tensor(name, shape, F32))

        def sem(name):
            return ctx.enter_context(nc.semaphore(name))

        c98 = sb("c98", [HT, a["c98"].shape[1]])
        c128 = sb("c128", [128, a["c128"].shape[1]])
        bnp = sb("bnp", [128, 5, NBN])
        bn_s = sb("bn_s", [128, NBN])
        bn_b = sb("bn_b", [128, NBN])
        bn_t = sb("bn_t", [128, NBN])
        half = sb("half", [128, NBN])
        rows = sb("rows", [1, ROWS])
        ones = sb("ones", [1, 128])
        rowb = sb("rowb", [128, ROW_BC])
        w1 = sb("w1", [128, EXPERTS, CC * MID])
        w2 = sb("w2", [128, EXPERTS, 6 * MID])
        w3 = sb("w3", [128, EXPERTS, 128])
        r1 = sb("r1", [128, CC, EXPERTS])
        r23 = sb("r23", [MID, 2, EXPERTS])
        inw = sb("inw", [128, CC, 6, 128])
        cvec = sb("cvec", [128, 16])
        dbcw = sb("dbcw", [128, CC, HEADS, DBC])
        outw = sb("outw", [128, CC, 2, 128])
        c1w = sb("c1w", [128, CC, MID])
        offw = sb("offw", [128, 6, 2 * TAPS])
        dcw = sb("dcw", [MID, TAPS * MID])
        c2w = sb("c2w", [MID, CH])
        d1w = sb("d1w", [128, CC, MID])
        d2w = sb("d2w", [128, 6, MID])
        d3w = sb("d3w", [MID, CH])

        def k98(name, *dims):
            lo, hi = (at98 if name in at98 else at_scan)[name]
            v = (c98 if name in at98 else c_scan)[:, lo:hi]
            if len(dims) == 2:
                v = v.rearrange("p (x y) -> p x y", x=dims[0])
            return v

        def k128(name):
            lo, hi = at128[name]
            return c128[:, lo:hi]

        ident = k128("ident")

        X = [sb(f"x{s}", [128, CC, G, N]) for s in range(STAGES)]
        XR = sb("xr", [128, CC, G, N])
        Y = [sb(f"y{s}", [128, CC, G, N]) for s in range(STAGES)]
        OUT = sb("xo", [128, CC, G, N])
        st = [sb(f"st{s}", [128, 4, 6]) for s in range(STAGES)]
        mv = [sb(f"mv{s}", [128, 4, 2]) for s in range(STAGES)]
        gm = [sb(f"gm{s}", [128, 4]) for s in range(STAGES)]
        dm = [sb(f"dm{s}", [128, 4, 2]) for s in range(STAGES)]
        dd = [sb(f"dd{s}", [128, 4, 2]) for s in range(STAGES)]
        dq = [sb(f"dq{s}", [128, 4]) for s in range(STAGES)]
        ve = [sb(f"ve{s}", [128, 4]) for s in range(STAGES)]
        rs = [sb(f"rs{s}", [128, 4]) for s in range(STAGES)]
        a_md = sb("a_md", [128, 4])
        a_mo = sb("a_mo", [128, 4])
        a_e = sb("a_e", [128, G * EXPERTS])
        a_e1 = sb("a_e1", [128, G * EXPERTS])
        a_rw = sb("a_rw", [128, 3, G, EXPERTS])
        a_w1 = sb("a_w1", [128, G, CC, MID])
        a_w2 = sb("a_w2", [128, G, 6, MID])
        a_w3 = sb("a_w3", [128, G, 128])
        a_pad = sb("a_pad", [128, G, PAD, PAD])
        a_sum = sb("a_sum", [128, 2, G])
        a_mean = sb("a_mean", [128, 2, G])
        a_h2 = sb("a_h2", [128, G, N])
        a_t = sb("a_t", [128, CC, W])
        a_u = a_t
        b_xc = sb("b_xc", [128, CC, G, N + 2])
        b_res = sb("b_res", [128, CC, W])
        b_gate = sb("b_gate", [128, CC, W])
        b_xf = sb("b_xf", [128, CC, G, N])
        XT = sb("b_xt", [HT, 2, G, HEADS, XD])
        XP = sb("b_xp", [HT, 2, G, HEADS, XD])
        Q8 = 2 * G * HEADS
        b_ab = sb("b_ab", [HT, Q8])
        b_ex = sb("b_ex", [HT, Q8])
        b_ln = sb("b_ln", [HT, Q8])
        b_u = sb("b_u", [HT, Q8])
        b_wm = sb("b_wm", [HT, Q8])
        b_m = sb("b_m", [HT, Q8])
        b_nu = sb("b_nu", [HT, Q8])
        b_de = sb("b_de", [HT, Q8])
        b_rc = sb("b_rc", [HT, Q8])
        b_sp = sb("b_sp", [HT, Q8])
        dt = sb("b_dt", [HT, Q8])
        dB = sb("b_db", [HT, Q8, STATE])
        rD = sb("b_rd", [HT, Q8, CHUNK])
        DU0 = sb("b_du0", [HT, 4, N])
        DU1 = sb("b_du1", [HT, 4, HT])
        CD = sb("b_cd", [HT, Q8, STATE, CHUNK])
        AD = sb("b_adt", [HT, Q8, STATE, CHUNK])
        EE = sb("b_ee", [HT, Q8, STATE, CHUNK])
        M1 = M2 = AD
        MC = sb("b_mc", [HT, Q8, CHUNK])
        MC2 = sb("b_mc2", [HT, Q8, CHUNK])
        MC3 = sb("b_mc3", [HT, Q8, CHUNK])
        MB = sb("b_mb", [HT, Q8, CPT, CHUNK])
        FF = sb("b_ff", [HT, Q8, STATE])
        UL = sb("b_ul", [HT, Q8, NCH, STATE])
        CR = sb("b_cr", [HT, Q8, NCH, STATE])
        RE = sb("b_re", [CS, 4, N])
        RR = RE
        US = sb("b_us", [CS, 4, HD])
        YT = XT
        b_y1 = sb("b_y1", [128, CC, W])
        b_y2 = b_y1
        b_o = b_gate
        b_A = sb("b_A", [128, HEADS * STATE])
        b_MA = sb("b_MA", [HT, 2, HEADS, NCH, STATE])
        b_De = sb("b_De", [HT, HEADS, CHUNK])
        PM = sb("b_pm", [HT, 2, HEADS, N])
        PT = sb("b_pt", [HT, 2, HEADS, N])
        c_flat = sb("c_pad", [128, G * PAD * PAD + PAD])
        c_pad = c_flat[:, 0:G * PAD * PAD].rearrange("p (b y x) -> p b y x", b=G, y=PAD)
        c_h = sb("c_h", [MID, G, N])
        c_py = sb("c_py", [HS, 4, 2 * TAPS])
        c_df = sb("c_df", [HS, 4 * 2 * TAPS, HW])
        c_ab = c_df
        c_te = c_df[:, :, :].rearrange("p (t b k d) v -> p t b k d v", t=2, b=G, k=TAPS)
        c_wt = sb("c_wt", [HS, 2, G, TAPS, HW, HW])
        c_wm = [sb(f"c_wm{j}", [HT, 2, N]) for j in range(2)]
        c_z = sb("c_z", [HT, 2, G, TAPS * MID])
        c_v = sb("c_v", [MID, W])
        c_o = sb("c_o", [128, CC, W])
        d_sq = sb("d_sq", [MID, W])
        d_pad = sb("d_pad", [128, G, PAD, PAD])
        d_sq2 = d_h2 = sb("d_h2", [MID, W])
        d_sq3 = OUT[:, :, :, :].rearrange("p c b n -> p c (b n)")
        d_t = d_sq3
        s_a = sb("s_a", [128, 16])
        s_w = c_wt[0:HT, 0, 0].rearrange("p k y x -> p (k y x)")[:, 0:1568].rearrange("p (v n) -> p v n", n=N)
        c_scan = c_wt[0:HT, 0, 1].rearrange("p k y x -> p (k y x)")[:, 0:a["c_scan"].shape[1]]
        S = c_wt[0:HT, 1, 0].rearrange("p k y x -> p (k y x)")[:, 0:HEADS * N].rearrange("p (h n) -> p h n", h=HEADS)
        s_half = sb("s_half", [128, 2])
        s_m = sb("s_m", [128, HEADS, 4])
        bn_r = sb("bn_r", [128, NBN])
        s_rank = sb("s_rank", [HT, 2, HEADS, 4])

        ps = [ctx.enter_context(nc.psum_tensor(f"ps{i}", [128, 512], F32)) for i in range(8)]

        def banks(name, which, fills):
            return Banks([ps[i] for i in which], [sem(f"{name}_filled{i}") for i in which],
                         [sem(f"{name}_drained{i}") for i in which], fills)

        A = banks("a", [0], 9)
        B = banks("b", [2, 3, 4], 30)
        C = banks("c", [5], 7)
        CT = banks("ct", [6, 7], 26)
        D = banks("d", [1], 6)

        def sig(name, per=1):
            return Signal(sem(name), per)

        consts_in = sem("consts_in")
        n_consts = [0]
        x_in = sig("x_in", 16 * CC)
        xr_in = sig("xr_in", 16 * CC)
        out_stored = sig("out_stored", 16 * CC)
        x_done = [None] + [sig(f"x{s}_written") for s in range(1, STAGES)] + [sig("out_written")]
        stats = [sig(f"stats{s}") for s in range(STAGES)]
        spread = [sig(f"spread{s}") for s in range(STAGES)]
        rstd = [sig(f"rstd{s}") for s in range(STAGES)]
        normed = [sig(f"normed{s}", 4) for s in range(STAGES)]
        pads_zero = sem("pads_zero")
        setup = sem("setup_done")
        setup_pe = sem("setup_pe")
        setup_v = sem("setup_v")
        setup_p = sem("setup_p")
        setup_s = sem("setup_s")
        setup_r = sem("setup_r")
        setup_a = sem("setup_a")
        b_ff = sig("b_ff_ready")

        a_md_ok = sig("a_md_ready")
        a_mix = sig("a_mixed", 3)
        a_mn = sig("a_mean_ready", 2)
        a_u_ok = sig("a_u_written", 2)

        b_gate_ok = sig("b_gate_written")
        b_dw = sig("b_dwconv")
        b_xf_ok = sig("b_xf_written")
        b_abs = sig("b_abs")
        b_e = sig("b_e")
        b_u_ok = sig("b_u_ready")
        b_l = sig("b_ln")
        b_dt = sig("b_dt_ready")
        b_rd = sig("b_rD_ready")
        b_cd = sig("b_cd_ready")
        b_du = sig("b_du_ready")
        b_ee = sig("b_ee_ready")
        b_mb = sig("b_mb_ready")
        b_ul = sig("b_ul_ready")
        b_cr_ok = sig("b_cr_ready")
        b_y2_ok = sig("b_y2_ready")

        c_df_ok = sig("c_df_ready")
        c_ab_ok = sig("c_ab_ready")
        c_te_ok = sig("c_te_ready")
        c_wt_v = sig("c_wt_by_vector", 2)
        c_wt_p = sig("c_wt_by_pool", 2)

        d_h1 = sig("d_h1_written")
        d_h2_ok = sig("d_h2_written")

        xsrc = a["x"]

        def pair(t, g, c):
            v = t.rearrange("(g b) (c p) n -> c g p b n", b=G, p=128)[c]
            return v[g] if isinstance(g, int) else v[bass.ds(g, 1)].rearrange("o p b n -> (o p) b n")

        def bilinear(tt, t, b):
            te = c_te[:, t, b]
            return tt(c_wt[:, t, b], te[:, :, 0, :].unsqueeze(3).to_broadcast([HS, TAPS, HW, HW]),
                      te[:, :, 1, :].unsqueeze(2).to_broadcast([HS, TAPS, HW, HW]), ALU.mult)

        def in_rows(t):
            return t[0:HT, 0:4 * HS].rearrange("p (r x) -> p r x", x=PAD)[:, :, 0:HW]

        block = ctx.enter_context(nc.Block())
        loads = [(c98[:, :], a["c98"]), (c128[:, :], a["c128"]), (c_scan, a["c_scan"]), (bnp[:, :, :], a["bnp"]), (rows[:, :], a["rows"]),
                 (w1[:, :, :], a["w1"]), (r1[:, :, :], a["r1"]), (r23[:, :, :], a["r23"]),
                 (w2[:, :, :], a["w2"]), (w3[:, :, :], a["w3"]), (inw[:, :, :, :], a["inw"]), (cvec[:, :], a["cvec"]),
                 (dbcw[:, :, :, :], a["dbcw"]), (outw[:, :, :, :], a["outw"]), (c1w[:, :, :], a["c1w"]),
                 (offw[:, :, :], a["offw"]), (dcw[:, :], a["dcw"]), (c2w[:, :], a["c2w"]), (d1w[:, :, :], a["d1w"]),
                 (d2w[:, :, :], a["d2w"]), (d3w[:, :], a["d3w"])]
        ALL_IN = 16 * len(loads)

        @block.sync
        def _(sp):
            for dst, src in loads:
                sp.dma_start(dst, src).then_inc(consts_in, 16)

            def stage0(i, g):
                if i == 0:
                    sp.wait_ge(normed[0].sem, normed[0].count(g, 0))
                    for c in range(CC):
                        sp.dma_start(X[0][:, c, :, :], pair(xsrc, g, c)).then_inc(x_in.sem, 16)
                if i == 1:
                    sp.wait_ge(x_done[1].sem, x_done[1].count(g, 0))
                    for c in range(CC):
                        sp.dma_start(XR[:, c, :, :], pair(xsrc, g, c)).then_inc(xr_in.sem, 16)

            def stage3(i, g):
                if i == STEPS[3] - 1:
                    sp.wait_ge(x_done[4].sem, x_done[4].count(g))
                    for c in range(CC):
                        sp.dma_start(pair(out, g, c), OUT[:, c, :, :]).then_inc(out_stored.sem, 16)

            def idle(i, g):
                return

            for_rounds(sp, [stage0, idle, idle, stage3])
            sp.wait_ge(out_stored.sem, 16 * CC * GROUPS)

        @block.tensor
        def _(pe):
            def mm(o, l, r, start=True, stop=True):
                return nc.tensor.matmul(o, l, r, start=start, stop=stop)

            def group_mean(s, g, bank, f, rhs, ready):
                pe.wait_ge(ready.sem, ready.count(g))
                pe.wait_ge(bank.drained(f), bank.empty(g, f))
                t = bank.tile(f)
                mm(t[:, 0:4], k128("group"), rhs).then_inc(bank.filled(f), 1)

            def route(g, bank, f, mean, ws, b0):
                pe.wait_ge(bank.drained(f), bank.empty(g, f))
                t = bank.tile(f)
                for b in range(G):
                    o = t[:, b * EXPERTS:(b + 1) * EXPERTS]
                    for j, w in enumerate(ws):
                        m = mean[j][:, b:b + 1]
                        mm(o, m.to_broadcast([m.shape[0], 128]), w, start=(j == 0), stop=False)
                    last = mm(o, ones[0:1, :], rows[0:1, b0:b0 + EXPERTS], start=False)
                last.then_inc(bank.filled(f), 1)

            def conv3x3(o, wt, pad):
                for j in range(6):
                    dy, dx = 2 * (j // 3), j % 3
                    last = mm(o, wt(j), pad(dy, dx), start=(j == 0), stop=(j == 5))
                return last

            def stage0(i, g):
                if i == 1:
                    group_mean(0, g, A, 0, mv[0][:, :, 0], stats[0])
                if i == 2:
                    group_mean(0, g, A, 1, dq[0][:, :], spread[0])
                if i == 3:
                    pe.wait_ge(a_md_ok.sem, a_md_ok.count(g))
                    route(g, A, 2, [a_md[:, 2 * c:2 * c + 2] for c in range(CC)],
                          [r1[:, c, :] for c in range(CC)], ROW_R[0])
                if i == 5:
                    pe.wait_ge(a_mix.sem, a_mix.count(g, 1))
                    pe.wait_ge(normed[0].sem, normed[0].count(g))
                    pe.wait_ge(A.drained(3), A.empty(g, 3))
                    t = A.tile(3)
                    for b in range(G):
                        for c in range(CC):
                            last = mm(t[0:MID, b * N:(b + 1) * N], a_w1[:, b, c, :], Y[0][:, c, b, :],
                                      start=(c == 0), stop=(c == CC - 1))
                    last.then_inc(A.filled(3), 1)
                if i == 6:
                    pe.wait_ge(a_mn.sem, a_mn.count(g, 1))
                    route(g, A, 4, [a_mean[0:MID, 0, :]], [r23[:, 0, :]], ROW_R[1])
                if i == 8:
                    pe.wait_ge(a_mix.sem, a_mix.count(g, 2))
                    pe.wait_ge(A.drained(3), A.full(g, 3))
                    pe.wait_ge(A.drained(5), A.empty(g, 5))
                    t = A.tile(5)
                    for b in range(G):
                        last = conv3x3(t[0:MID, b * N:(b + 1) * N], lambda j: a_w2[:, b, j, :],
                                       lambda dy, dx: a_pad[:, b, dy:dy + HW, dx:dx + HW])
                    last.then_inc(A.filled(5), 1)
                if i == 9:
                    pe.wait_ge(a_mn.sem, a_mn.count(g, 2))
                    route(g, A, 6, [a_mean[0:MID, 1, :]], [r23[:, 1, :]], ROW_R[2])
                if i == 10:
                    pe.wait_ge(a_mix.sem, a_mix.count(g, 3))
                    pe.wait_ge(A.drained(5), A.full(g, 5))
                    for m in range(CC):
                        pe.wait_ge(A.drained(7 + m), A.empty(g, 7 + m))
                        t = A.tile(7 + m)
                        for b in range(G):
                            last = mm(t[:, b * N:(b + 1) * N], a_w3[m * MID:(m + 1) * MID, b, :],
                                      a_h2[m * MID:(m + 1) * MID, b, :])
                        last.then_inc(A.filled(7 + m), 1)

            def stage1(i, g):
                if i == 1:
                    group_mean(1, g, B, 0, mv[1][:, :, 0], stats[1])
                if i == 2:
                    group_mean(1, g, B, 1, dq[1][:, :], spread[1])
                if i == 4:
                    pe.wait_ge(normed[1].sem, normed[1].count(g))
                    for m in range(6):
                        pe.wait_ge(B.drained(2 + m), B.empty(g, 2 + m))
                        t = B.tile(2 + m)
                        for c in range(CC):
                            last = mm(t[:, 0:W], inw[:, c, m, :], Y[1][:, c, :, :], start=(c == 0), stop=(c == CC - 1))
                        last.then_inc(B.filled(2 + m), 1)
                if i == 6:
                    pe.wait_ge(b_xf_ok.sem, b_xf_ok.count(g))
                    for k, (tt, b) in enumerate([(tt, b) for tt in range(2) for b in range(G)]):
                        pe.wait_ge(B.drained(8 + k), B.empty(g, 8 + k))
                        t = B.tile(8 + k)
                        cols = slice(tt * HT, (tt + 1) * HT)
                        for h in range(HEADS):
                            nc.tensor.transpose(t[0:HT, h * XD:h * XD + HD], b_xf[:, h, b, cols], ident)
                            o = t[0:HT, h * XD + HD:(h + 1) * XD]
                            for c in range(CC):
                                mm(o, b_xf[:, c, b, cols], dbcw[:, c, h, :], start=(c == 0), stop=False)
                            last = mm(o, ones[0:1, 0:HT],
                                      rows[0:1, ROW_DBC + h * DBC:ROW_DBC + (h + 1) * DBC], start=False)
                        last.then_inc(B.filled(8 + k), 1)
                if i == 7:
                    pe.wait_ge(B.drained(9), B.full(g, 9))
                    pe.wait_ge(B.drained(10), B.full(g, 10))
                    pe.wait_ge(B.drained(11), B.full(g, 11))
                    for k, (tt, b) in enumerate([(tt, b) for tt in range(2) for b in range(G)]):
                        pe.wait_ge(B.drained(12 + k), B.empty(g, 12 + k))
                        t = B.tile(12 + k)
                        for h in range(HEADS):
                            for n in range(2):
                                last = mm(t[0:HT, h * XD:(h + 1) * XD], PM[:, n, h, tt * HT:(tt + 1) * HT],
                                          XT[:, n, b, h, :], start=(n == 0), stop=(n == 1))
                        last.then_inc(B.filled(12 + k), 1)
                if i == 9:
                    pe.wait_ge(b_rd.sem, b_rd.count(g))
                    pe.wait_ge(B.drained(16), B.empty(g, 16))
                    t = B.tile(16)
                    last = mm(t[0:HT, 0:Q8 * CHUNK], k98("later"), rD[:, :, :].rearrange("p q t -> p (q t)"))
                    last.then_inc(B.filled(16), 1)
                    pe.wait_ge(b_du.sem, b_du.count(g))
                    for b in range(G):
                        pe.wait_ge(B.drained(17 + b), B.empty(g, 17 + b))
                        t = B.tile(17 + b)
                        for h in range(HEADS):
                            o = t[0:CS, h * N:(h + 1) * N]
                            mm(o, b_MA[:, 0, h].rearrange("p c s -> p (c s)"), DU0[:, 2 * b + h, :], stop=False)
                            last = mm(o[:, HT:N], b_MA[:, 1, h].rearrange("p c s -> p (c s)"), DU1[:, 2 * b + h, :],
                                      start=False)
                        last.then_inc(B.filled(17 + b), 1)
                    pe.wait_ge(b_cd.sem, b_cd.count(g))
                    for k in range(2):
                        pe.wait_ge(B.drained(19 + k), B.empty(g, 19 + k))
                        t = B.tile(19 + k)
                        last = mm(t[0:HT, 0:448], k98("same"),
                                  CD[:, 4 * k:4 * k + 4].rearrange("p q s t -> p (q s t)"))
                        last.then_inc(B.filled(19 + k), 1)
                if i == 10:
                    pe.wait_ge(b_cr_ok.sem, b_cr_ok.count(g))
                    for b in range(G):
                        pe.wait_ge(B.drained(21 + b), B.empty(g, 21 + b))
                        t = B.tile(21 + b)
                        for h in range(HEADS):
                            for tt in range(2):
                                o = t[0:CS, h * N + tt * HT:h * N + (tt + 1) * HT]
                                last = nc.tensor.transpose(
                                    o, CR[:, tt * 4 + 2 * b + h].rearrange("p c s -> p (c s)"), ident[0:HT, 0:HT])
                        last.then_inc(B.filled(21 + b), 1)
                if i == 11:
                    pe.wait_ge(b_ul.sem, b_ul.count(g))
                    pe.wait_ge(B.drained(23), B.empty(g, 23))
                    t = B.tile(23)
                    for b in range(G):
                        for h in range(HEADS):
                            for tt in range(2):
                                q = tt * 4 + b * 2 + h
                                last = mm(t[0:CS, (2 * b + h) * HD:(2 * b + h + 1) * HD],
                                          UL[:, q].rearrange("p c s -> p (c s)"), XP[:, tt, b, h, 0:HD],
                                          start=(tt == 0), stop=(tt == 1))
                    last.then_inc(B.filled(23), 1)
                if i == 12:
                    pe.wait_ge(b_mb.sem, b_mb.count(g))
                    pe.wait_ge(B.drained(21), B.full(g, 21))
                    pe.wait_ge(B.drained(22), B.full(g, 22))
                    pe.wait_ge(B.drained(23), B.full(g, 23))
                    for tt in range(2):
                        pe.wait_ge(B.drained(24 + tt), B.empty(g, 24 + tt))
                        t = B.tile(24 + tt)
                        for b in range(G):
                            for h in range(HEADS):
                                j = 2 * b + h
                                o = t[0:HT, j * HD:(j + 1) * HD]
                                mm(o, MB[:, tt * 4 + j].rearrange("p c t -> p (c t)"), XP[:, tt, b, h, 0:HD],
                                   stop=False)
                                last = mm(o, RR[:, j, tt * HT:(tt + 1) * HT], US[:, j, :], start=False)
                        last.then_inc(B.filled(24 + tt), 1)
                if i == 13:
                    pe.wait_ge(B.drained(24), B.full(g, 24))
                    pe.wait_ge(B.drained(25), B.full(g, 25))
                    for h in range(HEADS):
                        pe.wait_ge(B.drained(26 + h), B.empty(g, 26 + h))
                        t = B.tile(26 + h)
                        for b in range(G):
                            for tt in range(2):
                                last = mm(t[:, b * N:(b + 1) * N], YT[:, tt, b, h, 0:HD], PT[:, tt, h, :],
                                          start=(tt == 0), stop=(tt == 1))
                        last.then_inc(B.filled(26 + h), 1)
                if i == 15:
                    pe.wait_ge(b_y2_ok.sem, b_y2_ok.count(g))
                    for m in range(CC):
                        pe.wait_ge(B.drained(28 + m), B.empty(g, 28 + m))
                        t = B.tile(28 + m)
                        for c in range(CC):
                            last = mm(t[:, 0:W], outw[:, c, m, :], b_y2[:, c, :], start=(c == 0), stop=(c == CC - 1))
                        last.then_inc(B.filled(28 + m), 1)

            def stage2(i, g):
                if i == 1:
                    group_mean(2, g, C, 0, mv[2][:, :, 0], stats[2])
                if i == 2:
                    group_mean(2, g, C, 1, dq[2][:, :], spread[2])
                if i == 3:
                    pe.wait_ge(normed[2].sem, normed[2].count(g))
                    pe.wait_ge(C.drained(2), C.empty(g, 2))
                    t = C.tile(2)
                    for c in range(CC):
                        last = mm(t[0:MID, 0:W], c1w[:, c, :], Y[2][:, c, :, :], start=(c == 0), stop=(c == CC - 1))
                    last.then_inc(C.filled(2), 1)
                if i == 4:
                    pe.wait_ge(C.drained(2), C.full(g, 2))
                    pe.wait_ge(C.drained(3), C.empty(g, 3))
                    t = C.tile(3)
                    for tt in range(2):
                        for b in range(G):
                            o = t[0:HS, (2 * tt + b) * 2 * TAPS:(2 * tt + b + 1) * 2 * TAPS]
                            for j in range(6):
                                at = (b * PAD + 2 * (j // 3) + HR * tt) * PAD + j % 3
                                mm(o, c_flat[:, at:at + HS], offw[:, j, :], start=(j == 0), stop=False)
                            last = mm(o, ones[0:1, 0:HS], rows[0:1, ROW_OFF:ROW_OFF + 2 * TAPS], start=False)
                    last.then_inc(C.filled(3), 1)
                if i == 5:
                    for k in range(8):
                        tt, b, h = k // 4, k // 2 % 2, k % 2
                        pe.wait_ge(CT.drained(k), CT.empty(g, k))
                        t = CT.tile(k)
                        w = TAPS * MID // 2
                        last = mm(t[0:HT, 0:w], c_h[:, b, tt * HT:(tt + 1) * HT],
                                  dcw[:, h * w:(h + 1) * w])
                        last.then_inc(CT.filled(k), 1)
                if i in (7, 8, 9, 10):
                    units = [range(0, 5), range(5, 9), range(9, 14), range(14, 18)][i - 7]

                    def turn(k):
                        b, tap = k // TAPS, k % TAPS
                        pe.wait_ge(CT.drained(8 + k), CT.empty(g, 8 + k))
                        t = CT.tile(8 + k)
                        for m in range(2):
                            for n in range(2):
                                src = c_wt[:, n, b, tap, HR * m:HR * (m + 1), :].rearrange("p y x -> p (y x)")
                                last = nc.tensor.transpose(t[0:HT, (2 * m + n) * HS:(2 * m + n + 1) * HS], src,
                                                           ident[0:HS, 0:HS])
                        last.then_inc(CT.filled(8 + k), 1)

                    def add(k):
                        b, tap = k // TAPS, k % TAPS
                        pe.wait_ge(CT.drained(8 + k), CT.full(g, 8 + k))
                        t = C.tile(4)
                        for m in range(2):
                            last = mm(t[0:MID, b * N:(b + 1) * N], c_z[:, m, b, tap * MID:(tap + 1) * MID],
                                      c_wm[k % 2][:, m, :], start=(tap == 0 and m == 0), stop=(tap == TAPS - 1 and m == 1))
                        return last

                    if i == 7:
                        pe.wait_ge(CT.drained(6), CT.full(g, 6))
                        pe.wait_ge(CT.drained(7), CT.full(g, 7))
                        pe.wait_ge(C.drained(4), C.empty(g, 4))
                    for k in units:
                        if k in (0, TAPS):
                            if k == 0:
                                pe.wait_ge(c_wt_v.sem, c_wt_v.count(g))
                            else:
                                pe.wait_ge(c_wt_p.sem, c_wt_p.count(g))
                        turn(k)
                        if k:
                            add(k - 1)
                    if i == 10:
                        add(17).then_inc(C.filled(4), 1)
                if i == 11:
                    pe.wait_ge(C.drained(4), C.full(g, 4))
                    for m in range(CC):
                        pe.wait_ge(C.drained(5 + m), C.empty(g, 5 + m))
                        t = C.tile(5 + m)
                        mm(t[:, 0:W], c2w[:, m * 128:(m + 1) * 128], c_v[:, :]).then_inc(C.filled(5 + m), 1)

            def stage3(i, g):
                if i == 1:
                    group_mean(3, g, D, 0, mv[3][:, :, 0], stats[3])
                if i == 2:
                    group_mean(3, g, D, 1, dq[3][:, :], spread[3])
                if i == 3:
                    pe.wait_ge(normed[3].sem, normed[3].count(g))
                    pe.wait_ge(D.drained(2), D.empty(g, 2))
                    t = D.tile(2)
                    for c in range(CC):
                        last = mm(t[0:MID, 0:W], d1w[:, c, :], Y[3][:, c, :, :], start=(c == 0), stop=(c == CC - 1))
                    last.then_inc(D.filled(2), 1)
                if i == 4:
                    pe.wait_ge(d_h1.sem, d_h1.count(g))
                    pe.wait_ge(D.drained(3), D.empty(g, 3))
                    t = D.tile(3)
                    last = conv3x3(t[0:MID, 0:W], lambda j: d2w[:, j, :],
                                   lambda dy, dx: d_pad[:, :, dy:dy + HW, dx:dx + HW])
                    last.then_inc(D.filled(3), 1)
                if i == 6:
                    pe.wait_ge(d_h2_ok.sem, d_h2_ok.count(g))
                    for m in range(CC):
                        pe.wait_ge(D.drained(4 + m), D.empty(g, 4 + m))
                        t = D.tile(4 + m)
                        mm(t[:, 0:W], d3w[:, m * 128:(m + 1) * 128], d_h2[:, :]).then_inc(D.filled(4 + m), 1)

            pe.wait_ge(consts_in, ALL_IN)
            pe.wait_ge(pads_zero, 1)
            mm(ps[0][:, 0:ROW_BC], ones[0:1, :], rows[0:1, 0:ROW_BC]).then_inc(setup_pe, 1)
            pe.wait_ge(setup, 1)
            for h in range(HEADS):
                for n in range(2):
                    for tt in range(2):
                        last = nc.tensor.transpose(ps[1 + h][0:HT, (2 * tt + n) * HT:(2 * tt + n + 1) * HT],
                                                   PM[:, n, h, tt * HT:(tt + 1) * HT], ident[0:HT, 0:HT])
            last.then_inc(setup_pe, 1)
            pe.wait_ge(setup, 2)
            for_rounds(pe, [stage0, stage1, stage2, stage3])

        @block.scalar
        def _(act):
            def fn(o, i, f, **kw):
                return nc.scalar.activation(o, i, f, **kw)

            def halves(g, bank, f, pad, j, sums=None):
                act.wait_ge(bank.filled(f), bank.full(g, f))
                t = bank.tile(f)
                for b in range(G):
                    for h in range(2):
                        part, r0 = slice(h * MID, (h + 1) * MID), 1 - h
                        src = t[0:MID, b * N:(b + 1) * N].rearrange("p (y x) -> p y x", x=HW)
                        kw = {} if sums is None or h else {"accum_out": sums[0:MID, b:b + 1]}
                        last = fn(pad[part, b, r0:r0 + HW, 1:1 + HW], src, ACT.Relu, scale=bn_s[0:MID, j:j + 1],
                                  bias=bn_b[0:MID, j:j + 1], **kw)
                last.then_inc(bank.drained(f), 1)

            def stage0(i, g):
                def exps(f):
                    act.wait_ge(A.filled(f), A.full(g, f))
                    t = A.tile(f)
                    fn(a_e[:, :], t[:, 0:G * EXPERTS], ACT.Exp, scale=-1.0).then_inc(A.drained(f), 1)

                if i == 3:
                    exps(2)
                if i == 5:
                    halves(g, A, 3, a_pad, BN_A1, a_sum[:, 0, :])
                if i == 6:
                    exps(4)
                if i == 8:
                    act.wait_ge(A.filled(5), A.full(g, 5))
                    t = A.tile(5)
                    for b in range(G):
                        fn(a_h2[0:MID, b, :], t[0:MID, b * N:(b + 1) * N], ACT.Relu,
                           scale=bn_s[0:MID, BN_A2:BN_A2 + 1], bias=bn_b[0:MID, BN_A2:BN_A2 + 1],
                           accum_out=a_sum[0:MID, 1, b:b + 1])
                    last = fn(a_h2[MID:128, :, :].rearrange("p b n -> p (b n)"), t[0:MID, 0:W], ACT.Relu,
                              scale=bn_s[0:MID, BN_A2:BN_A2 + 1], bias=bn_b[0:MID, BN_A2:BN_A2 + 1])
                    last.then_inc(A.drained(5), 1)
                if i == 9:
                    exps(6)
                if i == 10:
                    for m in range(CC):
                        act.wait_ge(A.drained(7 + m), A.full(g, 7 + m))
                        fn(a_u[:, m, :], a_t[:, m, :], ACT.Relu, bias=bn_b[:, BN_A3 + m:BN_A3 + m + 1])\
                            .then_inc(a_u_ok.sem, 1)

            def stage1(i, g):
                if i == 4:
                    for m in range(6):
                        act.wait_ge(B.filled(2 + m), B.full(g, 2 + m))
                        t = B.tile(2 + m)
                        if m < 2:
                            o = b_xc[:, m, :, 1:1 + N]
                        else:
                            o = (b_res if m < 4 else b_gate)[:, m % 2, :].rearrange("p (b n) -> p b n", b=G)
                        fn(o, t[:, 0:W].rearrange("p (b n) -> p b n", b=G), ACT.Silu,
                                     bias=cvec[:, m:m + 1]).then_inc(B.drained(2 + m), 1)
                if i == 5:
                    act.wait_ge(B.drained(6), B.full(g, 6))
                    act.wait_ge(B.drained(7), B.full(g, 7))
                    fn(b_gate[:, :, :], b_gate[:, :, :], ACT.Silu).then_inc(b_gate_ok.sem, 1)
                    act.wait_ge(b_dw.sem, b_dw.count(g))
                    fn(b_xf[:, :, :, :], b_xf[:, :, :, :], ACT.Silu).then_inc(b_xf_ok.sem, 1)
                if i in (6, 7):
                    f, dst = ((8, XT), (12, XP))[i - 6]
                    for k in (0, 2):
                        act.wait_ge(B.filled(f + k), B.full(g, f + k))
                        t = B.tile(f + k)
                        fn(dst[:, k // 2, k % 2, :, :],
                                     t[0:HT, 0:HEADS * XD].rearrange("p (h x) -> p h x", h=HEADS), ACT.Copy).then_inc(B.drained(f + k), 1)
                if i == 8:
                    act.wait_ge(B.drained(13), B.full(g, 13))
                    act.wait_ge(B.drained(14), B.full(g, 14))
                    act.wait_ge(B.drained(15), B.full(g, 15))
                    x = XP[:, :, :, :, HD:HD + 1].rearrange("p t b h o -> p (t b h) o")
                    fn(b_ab[:, :].unsqueeze(2), x, ACT.Abs).then_inc(b_abs.sem, 1)
                    act.wait_ge(b_abs.sem, b_abs.count(g))
                    fn(b_ex[:, :], b_ab[:, :], ACT.Exp, scale=-1.0).then_inc(b_e.sem, 1)
                    act.wait_ge(b_u_ok.sem, b_u_ok.count(g))
                    fn(b_ln[:, :], b_u[:, :], ACT.Ln).then_inc(b_l.sem, 1)
                if i == 9:
                    for b in range(G):
                        act.wait_ge(B.filled(17 + b), B.full(g, 17 + b))
                        t = B.tile(17 + b)
                        fn(RE[:, 2 * b:2 * b + 2, :].rearrange("p h n -> p (h n)"), t[0:CS, 0:W], ACT.Exp,
                                     scale=-1.0).then_inc(B.drained(17 + b), 1)
                    act.wait_ge(B.drained(16), B.full(g, 16))
                    fn(EE[:, :, :, :], AD[:, :, :, :], ACT.Exp, scale=-1.0).then_inc(b_ee.sem, 1)
                if i == 11:
                    act.wait_ge(B.filled(23), B.full(g, 23))
                    t = B.tile(23)
                    fn(US[:, :, :].rearrange("p j d -> p (j d)"), t[0:CS, 0:4 * HD], ACT.Copy).then_inc(B.drained(23), 1)
                if i == 12:
                    act.wait_ge(B.filled(24), B.full(g, 24))
                    t = B.tile(24)
                    fn(YT[:, 0, :, :, 0:HD].rearrange("p b h d -> p (b h) d"),
                                 t[0:HT, 0:4 * HD].rearrange("p (j d) -> p j d", d=HD), ACT.Copy).then_inc(B.drained(24), 1)
                if i == 15:
                    for m in range(CC):
                        act.wait_ge(B.filled(28 + m), B.full(g, 28 + m))
                        t = B.tile(28 + m)
                        fn(b_o[:, m, :], t[:, 0:W], ACT.Silu, bias=cvec[:, 14 + m:15 + m]).then_inc(B.drained(28 + m), 1)

            def stage2(i, g):
                if i == 3:
                    act.wait_ge(C.filled(2), C.full(g, 2))
                    t = C.tile(2)
                    fn(c_h[:, :, :].rearrange("p b n -> p (b n)"), t[0:MID, 0:W], ACT.Relu,
                       scale=bn_s[0:MID, BN_C1:BN_C1 + 1], bias=bn_b[0:MID, BN_C1:BN_C1 + 1])
                    halves(g, C, 2, c_pad, BN_C1)
                if i == 4:
                    act.wait_ge(c_df_ok.sem, c_df_ok.count(g))
                    fn(c_ab[:, :, :], c_df[:, :, :], ACT.Abs).then_inc(c_ab_ok.sem, 1)
                    act.wait_ge(c_ab_ok.sem, c_ab_ok.count(g))
                    fn(c_df[:, :, :], c_ab[:, :, :], ACT.Relu,
                       bias=1.0, scale=-1.0).then_inc(c_te_ok.sem, 1)
                if i == 5:
                    for k in range(0, 8, 2):
                        act.wait_ge(CT.filled(k), CT.full(g, k))
                        t = CT.tile(k)
                        w = TAPS * MID // 2
                        fn(c_z[:, k // 4, k // 2 % 2, 0:w], t[0:HT, 0:w], ACT.Copy).then_inc(CT.drained(k), 1)
                if i in (7, 8, 9, 10):
                    for k in ((0, 2, 4), (6, 8), (10, 12), (14, 16))[i - 7]:
                        act.wait_ge(CT.filled(8 + k), CT.full(g, 8 + k))
                        t = CT.tile(8 + k)
                        fn(c_wm[0][:, :, :].rearrange("p m (y x) -> p (m y) x", x=HW), in_rows(t),
                                      ACT.Copy).then_inc(CT.drained(8 + k), 1)
                if i == 11:
                    act.wait_ge(C.filled(4), C.full(g, 4))
                    t = C.tile(4)
                    fn(c_v[:, :], t[0:MID, 0:W], ACT.Identity, scale=bn_s[0:MID, BN_C2:BN_C2 + 1],
                                 bias=bn_b[0:MID, BN_C2:BN_C2 + 1]).then_inc(C.drained(4), 1)
                    for m in range(CC):
                        act.wait_ge(C.filled(5 + m), C.full(g, 5 + m))
                        t = C.tile(5 + m)
                        j = BN_C3 + m
                        fn(c_o[:, m, :], t[:, 0:W], ACT.Relu, scale=bn_s[:, j:j + 1],
                                     bias=bn_b[:, j:j + 1]).then_inc(C.drained(5 + m), 1)

            def stage3(i, g):
                if i == 3:
                    act.wait_ge(D.filled(2), D.full(g, 2))
                    t = D.tile(2)
                    fn(d_sq[:, :], t[0:MID, 0:W], ACT.Square, bias=1.0).then_inc(D.drained(2), 1)
                if i == 5:
                    act.wait_ge(D.filled(3), D.full(g, 3))
                    t = D.tile(3)
                    fn(d_sq2[:, :], t[0:MID, 0:W], ACT.Square, bias=1.0).then_inc(D.drained(3), 1)
                if i == 6:
                    act.wait_ge(out_stored.sem, out_stored.count(g, 0))
                    for m in range(CC):
                        act.wait_ge(D.filled(4 + m), D.full(g, 4 + m))
                        t = D.tile(4 + m)
                        fn(d_sq3[:, m, :], t[:, 0:W], ACT.Square, bias=1.0).then_inc(D.drained(4 + m), 1)

            act.wait_ge(setup_r, 1)
            fn(b_A[:, :], rowb[:, ROW_A:ROW_A + HEADS * STATE], ACT.Exp).then_inc(setup_a, 1)
            act.wait_ge(setup, 2)
            act.wait_ge(pads_zero, NZERO)
            for_rounds(act, [stage0, stage1, stage2, stage3])

        @block.gpsimd
        def _(pool):
            def tt(o, x, y, op):
                return nc.gpsimd.tensor_tensor(out=o, in0=x, in1=y, op=op)

            def rstd_of(s, i, g, bank):
                if i == 2:
                    pool.wait_ge(bank.drained(1), bank.full(g, 1))
                    tt(rs[s][:, :], ve[s][:, :], half[:, 0:4], ALU.pow).then_inc(rstd[s].sem, 1)

            def add_input(s, g, m, x, y):
                ins = tt(X[s][:, m, :, :].rearrange("p b n -> p (b n)"), x, y.rearrange("p b n -> p (b n)"), ALU.add)
                if m == CC - 1:
                    ins.then_inc(x_done[s].sem, 1)

            def stage0(i, g):
                rstd_of(0, i, g, A)
                if i == 10:
                    pool.wait_ge(xr_in.sem, xr_in.count(g))
                    pool.wait_ge(x_done[2].sem, x_done[2].count(g, 0))
                    for m in range(CC):
                        pool.wait_ge(a_u_ok.sem, a_u_ok.count(g, m + 1))
                        add_input(1, g, m, a_u[:, m, :], XR[:, m, :, :])

            def stage1(i, g):
                rstd_of(1, i, g, B)
                if i == 8:
                    pool.wait_ge(B.drained(13), B.full(g, 13))
                    pool.wait_ge(B.drained(14), B.full(g, 14))
                    pool.wait_ge(B.drained(15), B.full(g, 15))
                    for m in range(2):
                        ins = tt(CR[:, 4 * m:4 * m + 4],
                                 XP[:, m, :, :, HD + 1 + STATE:XD].rearrange("p b h s -> p (b h) s").unsqueeze(2)
                                 .to_broadcast([HT, 4, NCH, STATE]),
                                 k98("after", 2, NCH)[:, m].unsqueeze(1).unsqueeze(3)
                                 .to_broadcast([HT, 4, NCH, STATE]), ALU.mult)
                    ins.then_inc(b_cr_ok.sem, 1)
                if i == 10:
                    pool.wait_ge(b_ff.sem, b_ff.count(g))
                    for m in range(2):
                        ins = tt(UL[:, 4 * m:4 * m + 4], FF[:, 4 * m:4 * m + 4].unsqueeze(2)
                                 .to_broadcast([HT, 4, NCH, STATE]),
                                 k98("chunk14", 2, NCH)[:, m].unsqueeze(1).unsqueeze(3)
                                 .to_broadcast([HT, 4, NCH, STATE]), ALU.mult)
                    ins.then_inc(b_ul.sem, 1)
                if i == 13:
                    for h in range(HEADS):
                        pool.wait_ge(B.drained(26 + h), B.full(g, 26 + h))
                        ins = tt(b_y2[:, h, :], b_y1[:, h, :], b_res[:, h, :], ALU.add)
                    ins.then_inc(b_y2_ok.sem, 1)
                if i == 15:
                    pool.wait_ge(x_done[3].sem, x_done[3].count(g, 0))
                    for m in range(CC):
                        pool.wait_ge(B.drained(28 + m), B.full(g, 28 + m))
                        add_input(2, g, m, b_o[:, m, :], X[1][:, m, :, :])

            def stage2(i, g):
                rstd_of(2, i, g, C)
                if i == 6:
                    pool.wait_ge(c_te_ok.sem, c_te_ok.count(g))
                    for t in range(2):
                        bilinear(tt, t, 1).then_inc(c_wt_p.sem, 1)
                if i == 11:
                    pool.wait_ge(x_done[4].sem, x_done[4].count(g, 0))
                    for m in range(CC):
                        pool.wait_ge(C.drained(5 + m), C.full(g, 5 + m))
                        add_input(3, g, m, c_o[:, m, :], X[2][:, m, :, :])

            def stage3(i, g):
                rstd_of(3, i, g, D)

            nc.gpsimd.memset(ones[:, :], 1.0).then_inc(pads_zero, 1)
            nc.gpsimd.memset(half[:, :], -0.5).then_inc(pads_zero, 1)
            nc.gpsimd.memset(s_half[:, :], 0.5).then_inc(pads_zero, 1)
            for t in (a_pad[:, :, :, :], c_flat[:, :], d_pad[:, :, :, :]):
                nc.gpsimd.memset(t, 0.0).then_inc(pads_zero, 1)
            nc.gpsimd.memset(b_xc[:, :, :, :], 0.0).then_inc(pads_zero, 1)
            pool.wait_ge(pads_zero, NZERO)
            pool.wait_ge(setup_p, 1)
            tt(bn_r[:, :], bn_t[:, :], half[:, :], ALU.pow).then_inc(setup_s, 1)
            pool.wait_ge(setup_p, 2)
            tt(s_a[:, 8:10], s_a[:, 6:8], s_half[:, :], ALU.pow).then_inc(setup_s, 1)
            pool.wait_ge(setup, 2)
            for_rounds(pool, [stage0, stage1, stage2, stage3])

        @block.vector
        def _(v):
            def tt(o, x, y, op):
                return nc.vector.tensor_tensor(out=o, in0=x, in1=y, op=op)

            def ts(o, x, s1, s2, op0, op1=None):
                if op1 is None:
                    return nc.vector.tensor_scalar(o, x, s1, None, op0)
                return nc.vector.tensor_scalar(o, x, s1, s2, op0, op1)

            def stt(o, x, s, y, op0, op1):
                return nc.vector.scalar_tensor_tensor(out=o, in0=x, scalar=s, in1=y, op0=op0, op1=op1)

            chains = {s: Chain(sem(f"vector_chain{s}"), n) for s, n in enumerate(VECTOR_STEPS)}

            def norm(s, i, g, bank, ready):
                ch = chains[s]
                if i == 0:
                    v.wait_ge(ready.sem, ready.count(g))
                    for c in range(CC):
                        for b in range(G):
                            nc.vector.bn_stats(st[s][:, 2 * c + b, :], X[s][:, c, b, :]).then_inc(ch.sem, ch.step())
                    v.wait_ge(ch.sem, ch.count(g))
                    tt(mv[s][:, :, 1], st[s][:, :, 2], st[s][:, :, 5], ALU.add).then_inc(ch.sem, ch.step())
                    tt(mv[s][:, :, 0], st[s][:, :, 1], st[s][:, :, 4], ALU.add).then_inc(stats[s].sem, 1)
                if i == 1:
                    v.wait_ge(bank.filled(0), bank.full(g, 0))
                    t = bank.tile(0)
                    nc.vector.tensor_copy(gm[s][:, :], t[:, 0:4]).then_inc(ch.sem, ch.step())
                    even_odd = st[s][:, :, :].rearrange("p j (e k) -> p j e k", e=2)[:, :, :, 1]
                    tt(dm[s][:, :, :], even_odd, t[:, 0:4].unsqueeze(2).to_broadcast([128, 4, 2]),
                                    ALU.subtract).then_inc(bank.drained(0), 1)
                    v.wait_ge(bank.drained(0), bank.full(g, 0))
                    tt(dd[s][:, :, :], dm[s][:, :, :], dm[s][:, :, :], ALU.mult).then_inc(ch.sem, ch.step())
                    v.wait_ge(ch.sem, ch.count(g))
                    tt(ve[s][:, :], dd[s][:, :, 0], dd[s][:, :, 1], ALU.add).then_inc(ch.sem, ch.step())
                    v.wait_ge(ch.sem, ch.count(g))
                    stt(dq[s][:, :], mv[s][:, :, 1], 2.0 / N, ve[s][:, :], ALU.mult, ALU.add)\
                        .then_inc(spread[s].sem, 1)
                if i == 2:
                    v.wait_ge(bank.filled(1), bank.full(g, 1))
                    t = bank.tile(1)
                    ts(ve[s][:, :], t[:, 0:4], GN_EPS, None, ALU.add).then_inc(bank.drained(1), 1)
                if i == 3:
                    v.wait_ge(rstd[s].sem, rstd[s].count(g))
                    for c in range(CC):
                        for b in range(G):
                            j = 2 * c + b
                            ts(Y[s][:, c, b, :], X[s][:, c, b, :], gm[s][:, j:j + 1], rs[s][:, j:j + 1],
                               ALU.subtract, ALU.mult).then_inc(normed[s].sem, 1)

            def stage0(i, g):
                ch = chains[0]
                norm(0, i, g, A, x_in)

                def sigmoid(j, f):
                    v.wait_ge(A.drained(f), A.full(g, f))
                    ts(a_e1[:, :], a_e[:, :], 1.0, None, ALU.add).then_inc(ch.sem, ch.step())
                    v.wait_ge(ch.sem, ch.count(g))
                    nc.vector.reciprocal(a_rw[:, j].rearrange("p b e -> p (b e)"), a_e1[:, :]).then_inc(ch.sem, ch.step())
                    v.wait_ge(ch.sem, ch.count(g))

                def mix(j, ws, outs):
                    for e in range(EXPERTS):
                        for b in range(G):
                            r = a_rw[:, j, b, e:e + 1]
                            if e == 0:
                                ins = ts(outs(b), ws(e), r, None, ALU.mult)
                            else:
                                v.wait_ge(ch.sem, ch.count(g, 1))
                                ins = stt(outs(b), ws(e), r, outs(b), ALU.mult, ALU.add)
                            if e == EXPERTS - 1 and b == G - 1:
                                ins.then_inc(a_mix.sem, 1)
                            else:
                                ins.then_inc(ch.sem, ch.step())

                if i == 3:
                    tt(a_mo[:, :], dm[0][:, :, 0], dm[0][:, :, 1], ALU.add).then_inc(ch.sem, ch.step())
                    v.wait_ge(ch.sem, ch.count(g))
                    stt(a_md[:, :], a_mo[:, :], 0.5, rs[0][:, :], ALU.mult, ALU.mult).then_inc(a_md_ok.sem, 1)
                if i == 4:
                    sigmoid(0, 2)
                    mix(0, lambda e: w1[:, e, :], lambda b: a_w1[:, b].rearrange("p c o -> p (c o)"))
                if i in (5, 8):
                    j = i // 8
                    v.wait_ge(A.drained((3, 5)[j]), A.full(g, (3, 5)[j]))
                    ts(a_mean[0:MID, j, :], a_sum[0:MID, j, :], 1.0 / N, None, ALU.mult).then_inc(a_mn.sem, 1)
                if i == 7:
                    sigmoid(1, 4)
                    mix(1, lambda e: w2[:, e, :], lambda b: a_w2[:, b].rearrange("p j o -> p (j o)"))
                if i == 9:
                    sigmoid(2, 6)
                    mix(2, lambda e: w3[:, e, :], lambda b: a_w3[:, b, :])
                if i == 10:
                    for m in range(CC):
                        v.wait_ge(A.filled(7 + m), A.full(g, 7 + m))
                        t = A.tile(7 + m)
                        stt(a_t[:, m, :], t[:, 0:W], bn_s[:, BN_A3 + m:BN_A3 + m + 1],
                                      Y[0][:, m].rearrange("p b n -> p (b n)"), ALU.mult, ALU.add).then_inc(A.drained(7 + m), 1)

            def stage1(i, g):
                ch = chains[1]
                norm(1, i, g, B, x_done[1])
                if i == 5:
                    v.wait_ge(B.drained(2), B.full(g, 2))
                    v.wait_ge(B.drained(3), B.full(g, 3))
                    for c in range(CC):
                        w = [cvec[:, 6 + 3 * c + j:7 + 3 * c + j] for j in range(3)]
                        ts(b_xf[:, c], b_xc[:, c, :, 0:N], w[0], cvec[:, 12 + c:13 + c], ALU.mult, ALU.add).then_inc(ch.sem, ch.step())
                    for j in (1, 2):
                        for c in range(CC):
                            v.wait_ge(ch.sem, ch.count(g, 1))
                            ins = stt(b_xf[:, c], b_xc[:, c, :, j:j + N], cvec[:, 6 + 3 * c + j:7 + 3 * c + j],
                                      b_xf[:, c], ALU.mult, ALU.add)
                            if j == 1 or c == 0:
                                ins.then_inc(ch.sem, ch.step())
                    ins.then_inc(b_dw.sem, 1)
                if i in (6, 7):
                    f, dst = ((8, XT), (12, XP))[i - 6]
                    for k in (1, 3):
                        v.wait_ge(B.filled(f + k), B.full(g, f + k))
                        t = B.tile(f + k)
                        nc.vector.tensor_copy(
                            dst[:, k // 2, k % 2, :, :],
                            t[0:HT, 0:HEADS * XD].rearrange("p (h x) -> p h x", h=HEADS)).then_inc(B.drained(f + k), 1)
                if i == 8:
                    v.wait_ge(B.drained(13), B.full(g, 13))
                    v.wait_ge(B.drained(14), B.full(g, 14))
                    v.wait_ge(B.drained(15), B.full(g, 15))
                    xp = XP[:, :, :, :, :].rearrange("p t b h x -> p (t b h) x")
                    Cm = xp[:, :, HD + 1 + STATE:XD]
                    at, upto = k98("at"), k98("upto")
                    tt(CD[:, :, :, :], Cm.unsqueeze(3).to_broadcast([HT, Q8, STATE, CHUNK]),
                       at.unsqueeze(1).unsqueeze(1).to_broadcast([HT, Q8, STATE, CHUNK]), ALU.mult)\
                        .then_inc(b_cd.sem, 1)
                    v.wait_ge(b_e.sem, b_e.count(g))
                    ts(b_u[:, :], b_ex[:, :], 1.0, None, ALU.add).then_inc(b_u_ok.sem, 1)
                    v.wait_ge(b_u_ok.sem, b_u_ok.count(g))
                    ts(b_wm[:, :], b_u[:, :], -1.0, None, ALU.add).then_inc(ch.sem, ch.step())
                    v.wait_ge(ch.sem, ch.count(g))
                    ts(b_m[:, :], b_wm[:, :], 0.0, None, ALU.is_equal).then_inc(ch.sem, ch.step())
                    v.wait_ge(ch.sem, ch.count(g))
                    tt(b_de[:, :], b_wm[:, :], b_m[:, :], ALU.add).then_inc(ch.sem, ch.step())
                    v.wait_ge(ch.sem, ch.count(g))
                    nc.vector.reciprocal(b_rc[:, :], b_de[:, :]).then_inc(ch.sem, ch.step())
                    v.wait_ge(b_l.sem, b_l.count(g))
                    tt(b_nu[:, :], b_ln[:, :], b_m[:, :], ALU.add).then_inc(ch.sem, ch.step())
                    v.wait_ge(ch.sem, ch.count(g))
                    tt(b_de[:, :], b_nu[:, :], b_ex[:, :], ALU.mult).then_inc(ch.sem, ch.step())
                    v.wait_ge(ch.sem, ch.count(g))
                    tt(b_sp[:, :], b_de[:, :], b_rc[:, :], ALU.mult).then_inc(ch.sem, ch.step())
                    v.wait_ge(ch.sem, ch.count(g))
                    stt(dt[:, :].unsqueeze(2), xp[:, :, HD:HD + 1], 0.0, b_sp[:, :].unsqueeze(2), ALU.max, ALU.add).then_inc(ch.sem, ch.step())
                    v.wait_ge(ch.sem, ch.count(g))
                    tt(rD[:, :, :], dt[:, :].unsqueeze(2).to_broadcast([HT, Q8, CHUNK]),
                       upto.unsqueeze(1).to_broadcast([HT, Q8, CHUNK]), ALU.mult).then_inc(b_rd.sem, 1)
                    tt(DU0[:, :, :], dt[:, 0:4].unsqueeze(2).to_broadcast([HT, 4, N]),
                       k98("tri0").unsqueeze(1).to_broadcast([HT, 4, N]), ALU.mult)
                    tt(DU1[:, :, :], dt[:, 4:8].unsqueeze(2).to_broadcast([HT, 4, HT]),
                       k98("tri1").unsqueeze(1).to_broadcast([HT, 4, HT]), ALU.mult).then_inc(b_du.sem, 1)
                    tt(dB[:, :, :], xp[:, :, HD + 1:HD + 1 + STATE],
                              dt[:, :].unsqueeze(2).to_broadcast([HT, Q8, STATE]), ALU.mult).then_inc(ch.sem, ch.step())
                if i == 9:
                    v.wait_ge(B.filled(16), B.full(g, 16))
                    t = B.tile(16)
                    D3 = t[0:HT, 0:Q8 * CHUNK].rearrange("p (r h t) -> p h r t", h=HEADS, t=CHUNK)
                    for h in range(HEADS):
                        ins = tt(AD[:, :, :, :].rearrange("p (r h) s t -> p h r s t", h=HEADS)[:, h],
                                 D3[:, h].unsqueeze(2).to_broadcast([HT, 4, STATE, CHUNK]),
                                 b_A[0:HT, h * STATE:(h + 1) * STATE].unsqueeze(1).unsqueeze(3)
                                 .to_broadcast([HT, 4, STATE, CHUNK]), ALU.mult)
                    ins.then_inc(B.drained(16), 1)
                if i == 10:
                    v.wait_ge(b_ee.sem, b_ee.count(g))
                    v.wait_ge(ch.sem, ch.count(g))
                    tt(FF[:, :, :], EE[:, :, :, CHUNK - 1], dB[:, :, :], ALU.mult).then_inc(b_ff.sem, 1)
                    for k in range(2):
                        v.wait_ge(B.filled(19 + k), B.full(g, 19 + k))
                        t = B.tile(19 + k)
                        tt(M1[:, 4 * k:4 * k + 4].rearrange("p q s t -> p (q s t)"),
                                     EE[:, 4 * k:4 * k + 4].rearrange("p q s t -> p (q s t)"), t[0:HT, 0:448],
                                     ALU.mult).then_inc(B.drained(19 + k), 1)
                    v.wait_ge(B.drained(19), B.full(g, 19))
                    v.wait_ge(B.drained(20), B.full(g, 20))
                    tt(M2[:, :, :, :], M1[:, :, :, :],
                              dB[:, :, :].unsqueeze(3).to_broadcast([HT, Q8, STATE, CHUNK]), ALU.mult).then_inc(ch.sem, ch.step())
                    v.wait_ge(ch.sem, ch.count(g))
                    nc.vector.tensor_reduce(MC[:, :, :], M2[:, :, :, :].rearrange("p q s t -> p q t s"),
                                                   AX.X, ALU.add).then_inc(ch.sem, ch.step())
                    v.wait_ge(ch.sem, ch.count(g))
                    tt(MC2[:, :, :], MC[:, :, :],
                              k98("upto").unsqueeze(1).to_broadcast([HT, Q8, CHUNK]), ALU.mult).then_inc(ch.sem, ch.step())
                    v.wait_ge(ch.sem, ch.count(g))
                    tt(MC3[:, :, :].rearrange("p (r h) t -> p r (h t)", h=HEADS),
                              MC2[:, :, :].rearrange("p (r h) t -> p r (h t)", h=HEADS),
                              b_De[:, :, :].rearrange("p h t -> p (h t)").unsqueeze(1)
                              .to_broadcast([HT, 4, HEADS * CHUNK]), ALU.add).then_inc(ch.sem, ch.step())
                    v.wait_ge(ch.sem, ch.count(g))
                    tt(MB[:, :, :, :], MC3[:, :, :].unsqueeze(2).to_broadcast([HT, Q8, CPT, CHUNK]),
                       k98("chunk7").unsqueeze(1).unsqueeze(3).to_broadcast([HT, Q8, CPT, CHUNK]), ALU.mult)\
                        .then_inc(b_mb.sem, 1)
                    v.wait_ge(B.drained(17), B.full(g, 17))
                    v.wait_ge(B.drained(18), B.full(g, 18))
                    for b in range(G):
                        v.wait_ge(B.filled(21 + b), B.full(g, 21 + b))
                        t = B.tile(21 + b)
                        tt(RR[:, 2 * b:2 * b + 2, :].rearrange("p h n -> p (h n)"),
                                     RE[:, 2 * b:2 * b + 2, :].rearrange("p h n -> p (h n)"), t[0:CS, 0:W],
                                     ALU.mult).then_inc(B.drained(21 + b), 1)
                if i == 12:
                    v.wait_ge(B.filled(25), B.full(g, 25))
                    t = B.tile(25)
                    nc.vector.tensor_copy(YT[:, 1, :, :, 0:HD].rearrange("p b h d -> p (b h) d"),
                                                   t[0:HT, 0:4 * HD].rearrange("p (j d) -> p j d", d=HD)).then_inc(B.drained(25), 1)
                if i == 13:
                    v.wait_ge(b_gate_ok.sem, b_gate_ok.count(g))
                    for h in range(HEADS):
                        v.wait_ge(B.filled(26 + h), B.full(g, 26 + h))
                        t = B.tile(26 + h)
                        tt(b_y1[:, h, :], b_gate[:, h, :], t[:, 0:W], ALU.mult).then_inc(B.drained(26 + h), 1)

            def stage2(i, g):
                norm(2, i, g, C, x_done[2])
                if i == 4:
                    v.wait_ge(C.filled(3), C.full(g, 3))
                    t = C.tile(3)
                    J = 2 * TAPS
                    tt(c_py[:, :, :].rearrange("p (m b) j -> p m b j", b=G),
                                 t[0:HS, 0:4 * J].rearrange("p (m b j) -> p m b j", m=2, b=G),
                                 k128("grid")[0:HS].rearrange("p (m j) -> p m j", m=2).unsqueeze(2)
                                 .to_broadcast([HS, 2, G, J]), ALU.add).then_inc(C.drained(3), 1)
                    v.wait_ge(C.drained(3), C.full(g, 3))
                    tt(c_df[:, :, :], c_py[:, :, :].rearrange("p q j -> p (q j)").unsqueeze(2)
                       .to_broadcast([HS, 4 * J, HW]),
                       k128("iota14")[0:HS].unsqueeze(1).to_broadcast([HS, 4 * J, HW]), ALU.subtract).then_inc(c_df_ok.sem, 1)
                if i == 5:
                    for k in range(1, 8, 2):
                        v.wait_ge(CT.filled(k), CT.full(g, k))
                        t = CT.tile(k)
                        w = TAPS * MID // 2
                        nc.vector.tensor_copy(c_z[:, k // 4, k // 2 % 2, w:2 * w], t[0:HT, 0:w]).then_inc(CT.drained(k), 1)
                if i == 6:
                    v.wait_ge(c_te_ok.sem, c_te_ok.count(g))
                    for t in range(2):
                        bilinear(tt, t, 0).then_inc(c_wt_v.sem, 1)
                if i in (7, 8, 9, 10):
                    for k in ((1, 3), (5, 7), (9, 11, 13), (15, 17))[i - 7]:
                        v.wait_ge(CT.filled(8 + k), CT.full(g, 8 + k))
                        t = CT.tile(8 + k)
                        nc.vector.tensor_copy(c_wm[1][:, :, :].rearrange("p m (y x) -> p (m y) x", x=HW),
                                                         in_rows(t)).then_inc(CT.drained(8 + k), 1)

            def stage3(i, g):
                ch = chains[3]
                norm(3, i, g, D, x_done[3])
                if i == 3:
                    v.wait_ge(D.drained(2), D.full(g, 2))
                    for h in range(2):
                        part, r0 = slice(h * MID, (h + 1) * MID), 1 - h
                        last = ts(d_pad[part, :, r0:r0 + HW, 1:1 + HW],
                                  d_sq[:, :].rearrange("p (b y x) -> p b y x", b=G, x=HW),
                                  bn_s[0:MID, BN_D1:BN_D1 + 1], bn_b[0:MID, BN_D1:BN_D1 + 1], ALU.mult, ALU.add)
                    last.then_inc(d_h1.sem, 1)
                if i == 5:
                    v.wait_ge(D.drained(3), D.full(g, 3))
                    ts(d_h2[:, :], d_sq2[:, :], bn_s[0:MID, BN_D2:BN_D2 + 1], bn_b[0:MID, BN_D2:BN_D2 + 1],
                       ALU.mult, ALU.add).then_inc(d_h2_ok.sem, 1)
                if i == 6:
                    for m in range(CC):
                        v.wait_ge(D.drained(4 + m), D.full(g, 4 + m))
                        j = BN_D3 + m
                        stt(d_t[:, m, :], d_sq3[:, m, :], bn_s[:, j:j + 1],
                                   Y[3][:, m].rearrange("p b n -> p (b n)"), ALU.mult, ALU.add).then_inc(ch.sem, ch.step())
                        v.wait_ge(ch.sem, ch.count(g))
                        ins = stt(OUT[:, m].rearrange("p b n -> p (b n)"), d_t[:, m, :], bn_b[:, j:j + 1],
                                  X[3][:, m].rearrange("p b n -> p (b n)"), ALU.add, ALU.add)
                    ins.then_inc(x_done[4].sem, 1)

            at = [0]

            def link(ins):
                ins.then_inc(setup_v, 1)
                at[0] += 1
                v.wait_ge(setup_v, at[0])

            v.wait_ge(consts_in, ALL_IN)
            ts(bn_t[:, :], bnp[:, 3, :], BN_EPS, None, ALU.add).then_inc(setup_p, 1)
            link(tt(bn_b[:, :], bnp[:, 4, :], bnp[:, 2, :], ALU.subtract))
            v.wait_ge(setup_pe, 1)
            nc.vector.tensor_copy(rowb[:, :], ps[0][:, 0:ROW_BC]).then_inc(setup_r, 1)
            v.wait_ge(setup_r, 1)
            v.wait_ge(setup_s, 1)
            link(tt(bn_s[:, :], bnp[:, 0, :], bn_r[:, :], ALU.mult))
            link(tt(bn_b[:, :], bn_b[:, :], bn_s[:, :], ALU.mult))
            link(tt(bn_b[:, :], bn_b[:, :], bnp[:, 1, :], ALU.add))
            mob = rowb[:, ROW_MOB:ROW_BC].rearrange("p (h j) -> p h j", j=4)
            link(tt(s_a[:, 0:2], mob[:, :, 0], mob[:, :, 3], ALU.mult))
            link(tt(s_a[:, 2:4], mob[:, :, 1], mob[:, :, 2], ALU.mult))
            link(tt(s_a[:, 4:6], s_a[:, 0:2], s_a[:, 2:4], ALU.subtract))
            link(ts(s_a[:, 0:2], s_a[:, 4:6], -1.0, None, ALU.mult))
            link(tt(s_a[:, 2:4], s_a[:, 0:2], s_a[:, 4:6], ALU.max))
            ts(s_a[:, 6:8], s_a[:, 2:4], 0.001, None, ALU.max).then_inc(setup_p, 1)
            v.wait_ge(setup_s, 2)
            link(nc.vector.reciprocal(s_a[:, 10:12], s_a[:, 8:10]))
            link(tt(s_m[:, :, :], mob, s_a[:, 10:12].unsqueeze(2).to_broadcast([128, HEADS, 4]), ALU.mult))
            xs, ys = k98("xs"), k98("ys")
            for h in range(HEADS):
                ca, cb, cc_, cd = (s_m[0:HT, h, j:j + 1] for j in range(4))
                u = [s_w[:, j, :] for j in range(8)]
                link(ts(u[0], xs, ca, cb, ALU.mult, ALU.add))
                link(ts(u[1], ys, ca, None, ALU.mult))
                link(ts(u[2], xs, cc_, cd, ALU.mult, ALU.add))
                link(ts(u[2], u[2], 1e-6, None, ALU.add))
                link(ts(u[3], ys, cc_, None, ALU.mult))
                link(tt(u[4], u[2], u[2], ALU.mult))
                link(tt(u[5], u[3], u[3], ALU.mult))
                link(tt(u[4], u[4], u[5], ALU.add))
                link(nc.vector.reciprocal(u[5], u[4]))
                link(tt(u[6], u[0], u[2], ALU.mult))
                link(tt(u[7], u[1], u[3], ALU.mult))
                link(tt(u[6], u[6], u[7], ALU.add))
                link(tt(u[6], u[6], u[5], ALU.mult))
                link(tt(u[4], u[1], u[2], ALU.mult))
                link(tt(u[7], u[0], u[3], ALU.mult))
                link(tt(u[4], u[4], u[7], ALU.subtract))
                link(tt(u[4], u[4], u[5], ALU.mult))
                link(stt(S[:, h, :], u[4], 1.3, u[6], ALU.mult, ALU.add))
                for n in range(2):
                    r = [s_rank[:, n, h, j:j + 1] for j in range(4)]
                    link(tt(u[0], S[:, h, :], k98("self", 2, N)[:, n], ALU.mult))
                    link(nc.vector.tensor_reduce(r[0], u[0], AX.X, ALU.add))
                    link(ts(u[1], S[:, h, :], r[0], None, ALU.is_lt))
                    link(ts(u[2], S[:, h, :], r[0], None, ALU.is_equal))
                    link(tt(u[2], u[2], k98("before", 2, N)[:, n], ALU.mult))
                    link(tt(u[1], u[1], u[2], ALU.add))
                    link(nc.vector.tensor_reduce(r[1], u[1], AX.X, ALU.add))
                    link(ts(PM[:, n, h, :], k98("iota196"), r[1], None, ALU.is_equal))
            nc.vector.memset(s_a[:, 12:13], 0.0).then_inc(setup, 1)
            for h in range(HEADS):
                ts(b_De[:, h, :], k98("at"), rowb[0:HT, ROW_D + h:ROW_D + h + 1], None, ALU.mult)
            v.wait_ge(setup_a, 1)
            for m in range(2):
                for h in range(HEADS):
                    tt(b_MA[:, m, h], k98("after", 2, NCH)[:, m].unsqueeze(2).to_broadcast([HT, NCH, STATE]),
                       b_A[0:HT, h * STATE:(h + 1) * STATE].unsqueeze(1).to_broadcast([HT, NCH, STATE]), ALU.mult)
            v.wait_ge(setup_pe, 2)
            for h in range(HEADS):
                last = nc.vector.tensor_copy(PT[:, :, h, :], ps[1 + h][0:HT, 0:2 * N].rearrange("p (t n) -> p t n", t=2))
            last.then_inc(setup, 1)
            for_rounds(v, [stage0, stage1, stage2, stage3], chains)


def kernel(**inputs):
    import numpy as np
    import concourse.bacc as bacc
    from concourse.bass_utils import run_bass_kernel_spmd

    f = {k: np.asarray(x) for k, x in inputs.items()}

    def halves(x):
        return np.concatenate([x, x], 0)

    def chan(x):
        return x.reshape(CC, 128, -1).transpose(1, 0, 2)

    def taps(w):
        w = np.moveaxis(w, (-3, -2, -1), (0, 1, 2))
        w = np.moveaxis(w, (1, 2), (-3, -2))
        low = np.concatenate([w[..., 0, :, :], w[..., 2, :, :]], -2)
        high = np.concatenate([w[..., 1, :, :], np.zeros_like(w[..., 2, :, :])], -2)
        return np.concatenate([low, high], 0)

    def bn_columns(names):
        cols = np.zeros((128, NBN), np.float32)
        for j, name in names.items():
            x = f[name]
            if x.size == MID:
                cols[:, j] = halves(x)
            else:
                cols[:, j:j + 2] = x.reshape(CC, 128).T
        return cols

    def bn_names(l0, l2, l3):
        return {**{BN_A1 + n: f"L0_conv_bn{n + 1}_{l0}" for n in range(3)},
                **{BN_C1 + n: f"L2_conv_bn{n + 1}_{l2}" for n in range(3)},
                **{BN_D1 + n: f"L3_conv_{l3}{n + 1}" for n in range(3)}}

    at98, c98, at128, c128, at_scan, c_scan = shape_constants()
    bias_names = {BN_C1: "L2_conv_conv1_b", BN_C2: "L2_conv_dconv_b", BN_C3: "L2_conv_conv2_b"}
    w1 = f["L0_conv_w1"].reshape(EXPERTS, MID, CC, 128).transpose(3, 0, 2, 1)
    w3 = f["L0_conv_w3"].reshape(EXPERTS, 2, 128, MID).transpose(1, 3, 0, 2)
    arrays = {
        "x": f["x"].reshape(BATCH, CH, N),
        "c98": c98, "c128": c128, "c_scan": c_scan,
        "bnp": np.stack([bn_columns(bn_names(k, k, k)) for k in "gbmv"] + [bn_columns(bias_names)], 1),
        "rows": np.concatenate([f[n].reshape(-1) for n in (
            "L1_conv_A_log", "L1_conv_Dparam", "L1_conv_mobius", "L0_conv_r1_b", "L0_conv_r2_b", "L0_conv_r3_b",
            "L1_conv_dbc_b", "L2_conv_off_b")])[None],
        "w1": w1.reshape(128, EXPERTS, CC * MID),
        "w2": taps(f["L0_conv_w2"]).reshape(128, EXPERTS, 6 * MID),
        "w3": w3.reshape(128, EXPERTS, 128),
        "r1": chan(f["L0_conv_r1_w"]),
        "r23": np.stack([f["L0_conv_r2_w"], f["L0_conv_r3_w"]], 1),
        "inw": chan(f["L1_conv_in_proj_w"].T).reshape(128, CC, 6, 128),
        "cvec": np.concatenate([f["L1_conv_in_proj_b"].reshape(6, 128).T, chan(f["L1_conv_dw_w"]).reshape(128, 6),
                                f["L1_conv_dw_b"].reshape(CC, 128).T, f["L1_conv_out_proj_b"].reshape(CC, 128).T], 1),
        "dbcw": chan(f["L1_conv_dbc_w"].T).reshape(128, CC, HEADS, DBC),
        "outw": chan(f["L1_conv_out_proj_w"].T).reshape(128, CC, 2, 128),
        "c1w": chan(f["L2_conv_conv1_w"].T),
        "offw": taps(f["L2_conv_off_w"]),
        "dcw": f["L2_conv_dconv_w"].reshape(MID, MID, TAPS).transpose(1, 2, 0).reshape(MID, TAPS * MID),
        "c2w": f["L2_conv_conv2_w"].T,
        "d1w": chan(f["L3_conv_w1"].reshape(MID, CH).T),
        "d2w": taps(f["L3_conv_w2"]),
        "d3w": f["L3_conv_w3"].reshape(CH, MID).T,
    }
    nc = bacc.Bacc("TRN2", target_bir_lowering=False, num_devices=1)
    args = {}
    for name, x in arrays.items():
        arrays[name] = x = np.ascontiguousarray(x)
        args[name] = nc.dram_tensor(f"in_{name}", x.shape, F32, kind="ExternalInput").ap()
    out = nc.dram_tensor("out_0", (BATCH, CH, N), F32, kind="ExternalOutput").ap()
    build(nc, args, out, at98, at128, at_scan)
    r = run_bass_kernel_spmd(nc, [{f"in_{k}": x for k, x in arrays.items()}], core_ids=[0])
    return r.results[0]["out_0"].reshape(BATCH, CH, HW, HW)
```

```python
from contextlib import ExitStack

import concourse.bass as bass
from concourse import mybir

ALU = mybir.AluOpType
ACT = mybir.ActivationFunctionType
AX = mybir.AxisListType
F32 = mybir.dt.float32

BATCH, CH, HW = 32, 256, 14
N = HW * HW
G = 2
GROUPS = BATCH // G
CC = CH // 128
W = G * N
MID = 64
EXPERTS = 8
TAPS = 9
HEADS, STATE = 2, 8
HD = CH // HEADS
DBC = 1 + 2 * STATE
HT = N // 2
HR = HW // 2
HS = HR * (HW + 2)
CHUNK = 14
NCH = N // CHUNK
CPT = NCH // 2
CS = NCH * STATE
PAD = HW + 2
XD = HD + DBC
GN_EPS = 1e-5
BN_EPS = 1e-5
LOG2E = 1.4426950408889634
STAGES = 4
(BN_A1, BN_A2, BN_A3, BN_C1, BN_C2, BN_C3, BN_D1, BN_D2, BN_D3) = (0, 1, 2, 4, 5, 6, 8, 9, 10)
NBN = 12
ROW_A, ROW_D, ROW_MOB = 0, HEADS * STATE, HEADS * STATE + HEADS
ROW_BC = ROW_MOB + 4 * HEADS
ROW_R = [ROW_BC + EXPERTS * i for i in range(3)]
ROW_DBC = ROW_BC + 3 * EXPERTS
ROW_OFF = ROW_DBC + HEADS * DBC
ROWS = ROW_OFF + 2 * TAPS


def shape_constants():
    import numpy as np

    f = np.float32
    u = np.arange(HT)
    tok = np.stack([u, HT + u])
    t = np.arange(N)
    i, c = u % CHUNK, u // CHUNK
    tt = np.arange(CHUNK)
    step = np.arange(HW - 1, dtype=f) / f(HW - 1)
    line = np.append(-(f(1) - step) + step, f(1)).astype(f)
    k = np.arange(TAPS)
    sample = np.arange(128)
    grid = np.zeros((128, 2, TAPS, 2), f)
    for m in range(2):
        grid[:, m, :, 0] = (sample // PAD + HR * m)[:, None] + (k // 3 - 1)[None]
        grid[:, m, :, 1] = (sample % PAD)[:, None] + (k % 3 - 1)[None]
    parts_scan = [
        ("self", np.stack([tok[m][:, None] == t[None] for m in range(2)], 1)),
        ("before", np.stack([t[None] < tok[m][:, None] for m in range(2)], 1)),
        ("iota196", np.tile(t, (HT, 1))),
        ("xs", np.tile(line[t % HW], (HT, 1))),
        ("ys", np.tile(line[t // HW], (HT, 1))),
    ]
    parts98 = [
        ("later", (c[:, None] == c[None]) & (i[:, None] > i[None])),
        ("same", c[:, None] == c[None]),
        ("upto", i[:, None] <= tt[None]),
        ("at", i[:, None] == tt[None]),
        ("chunk7", c[:, None] == np.arange(CPT)[None]),
        ("chunk14", np.stack([(tok[m] // CHUNK)[:, None] == np.arange(NCH)[None] for m in range(2)], 1)),
        ("after", np.stack([(tok[m] // CHUNK)[:, None] > np.arange(NCH)[None] for m in range(2)], 1)),
        ("tri0", tok[0][:, None] <= t[None]),
        ("tri1", tok[1][:, None] <= t[None, HT:]),
    ]
    p = np.arange(128)
    parts128 = [
        ("ident", p[:, None] == p[None]),
        ("group", (p[:, None] // 8 == p[None] // 8) / 16.0),
        ("grid", grid),
        ("iota14", np.tile(np.arange(HW), (128, 1))),
    ]
    out = []
    for parts in (parts98, parts128, parts_scan):
        where, at, cols = {}, 0, []
        for name, a in parts:
            a = np.asarray(a, f)
            a = a.reshape(a.shape[0], -1)
            where[name] = (at, at + a.shape[1])
            at += a.shape[1]
            cols.append(a)
        out += [where, np.ascontiguousarray(np.concatenate(cols, 1))]
    return out


class Signal:

    def __init__(self, sem, per=1):
        self.sem, self.per = sem, per

    def count(self, g, k=None):
        return g * self.per + (self.per if k is None else k)


class Chain:

    def __init__(self, sem, per):
        self.sem, self.per, self.at = sem, per, 0

    def step(self):
        self.at += 1
        return 1

    def count(self, g, back=0):
        return g * self.per + self.at - back

    def end(self, what):
        assert self.at == self.per, (what, self.at, self.per)
        self.at = 0


class Banks:

    def __init__(self, tiles, filled, drained, fills):
        assert fills % len(tiles) == 0
        self.tiles, self.nb, self.per = tiles, len(tiles), fills // len(tiles)
        self.sems = filled, drained

    def tile(self, f):
        return self.tiles[f % self.nb]

    def filled(self, f):
        return self.sems[0][f % self.nb]

    def drained(self, f):
        return self.sems[1][f % self.nb]

    def empty(self, g, f):
        return g * self.per + f // self.nb

    def full(self, g, f):
        return self.empty(g, f) + 1


PARTS = {
    "sync": ({0: 1, 1: 1}, {}, {}, {6: 1}),
    "tensor": ({1: 1, 2: 1, 3: 1, 5: 1, 6: 1, 8: 1, 9: 1, 10: 2},
               {1: 1, 2: 1, 4: 6, 6: 4, 7: 4, 9: 4, 10: 1, 11: 1, 12: 2, 13: 2, 15: 2},
               {1: 1, 2: 1, 3: 1, 4: 4, 5: 8, 7: 2 * TAPS, 11: 2},
               {1: 1, 2: 1, 3: 1, 4: 1, 6: 2}),
    "scalar": ({3: 1, 5: 2, 6: 1, 8: 1, 9: 1, 10: 2},
               {4: 6, 5: 2, 6: 2, 7: 2, 8: 2, 9: 3, 11: 1, 12: 1, 15: 2},
               {3: 3, 4: 2, 5: 4, 7: TAPS, 11: 3},
               {3: 2, 5: 1, 6: 2}),
    "gpsimd": ({2: 1, 10: 2},
               {2: 1, 8: 3, 10: 2, 13: 2, 15: 2},
               {2: 1, 6: 2, 11: 2},
               {2: 1}),
    "vector": ({0: 1, 1: 1, 2: 1, 3: 1, 4: EXPERTS, 5: 1, 7: EXPERTS, 8: 1, 9: EXPERTS, 10: 2},
               {0: 1, 1: 1, 2: 1, 3: 1, 5: 3, 6: 2, 7: 2, 8: 6, 9: 1, 10: 6, 12: 1, 13: 2},
               {0: 1, 1: 1, 2: 1, 3: 1, 4: 2, 5: 4, 6: 2, 7: TAPS},
               {0: 1, 1: 1, 2: 1, 3: 1, 5: 1, 6: 2}),
}
ORDER = {
    "sync": "003",
    "tensor": "002233120122232223222221201112112203211211211211222202121122122031121121102011",
    "scalar": "2220332222211020213111210112311221112021112230112221100",
    "gpsimd": "2013221111111221100",
    "vector": "030222123001010013322200000222222110132000211000020112112111321102111121130000100001100",
}
VECTOR_STEPS = (57, 26, 8, 10)
NZERO = 7


def round_parts(name, stages):
    left = [[(i, part) for i, n in steps.items() for part in range(n)] for steps in PARTS[name]]
    order = [(s, *left[s].pop(0)) for s in map(int, ORDER[name])]
    assert not any(left), (name, left)
    return [x for x in order if x[0] in stages]


def for_rounds(eng, name, steps, chains=()):

    def one(r, stages):
        for s, i, part in round_parts(name, stages):
            steps[s](i, part, r - s)
        for s in stages:
            if s in chains:
                chains[s].end((name, s))

    for r in range(STAGES):
        one(r, range(min(r + 1, STAGES)))
    with eng.Fori(STAGES, GROUPS) as r:
        one(r, range(STAGES))
    for r in range(GROUPS, GROUPS + STAGES - 1):
        one(r, range(r - GROUPS + 1, STAGES))


def build(nc, a, out, at98, at128, at_scan):
    ctx = ExitStack()
    with ctx:
        def sb(name, shape):
            return ctx.enter_context(nc.sbuf_tensor(name, shape, F32))

        def sem(name):
            return ctx.enter_context(nc.semaphore(name))

        c98 = sb("c98", [HT, a["c98"].shape[1]])
        c128 = sb("c128", [128, a["c128"].shape[1]])
        bnp = sb("bnp", [128, 5, NBN])
        bn_s = sb("bn_s", [128, NBN])
        bn_b = sb("bn_b", [128, NBN])
        bn_t = sb("bn_t", [128, NBN])
        root = sb("root", [128, NBN])
        rows = sb("rows", [1, ROWS])
        ones = sb("ones", [1, 128])
        rowb = sb("rowb", [128, ROW_BC])
        w1 = sb("w1", [128, EXPERTS, CC * MID])
        w2 = sb("w2", [128, EXPERTS, 6 * MID])
        w3 = sb("w3", [128, EXPERTS, 128])
        r1 = sb("r1", [128, CC, EXPERTS])
        r23 = sb("r23", [MID, 2, EXPERTS])
        inw = sb("inw", [128, CC, 6, 128])
        cvec = sb("cvec", [128, 16])
        dbcw = sb("dbcw", [128, CC, HEADS, DBC])
        outw = sb("outw", [128, CC, 2, 128])
        c1w = sb("c1w", [128, CC, MID])
        offw = sb("offw", [128, 6, 2 * TAPS])
        dcw = sb("dcw", [128, TAPS * MID])
        c2w = sb("c2w", [MID, CH])
        d1w = sb("d1w", [128, CC, MID])
        d2w = sb("d2w", [128, 6, MID])
        d3w = sb("d3w", [MID, CH])

        def k98(name, *dims):
            lo, hi = (at98 if name in at98 else at_scan)[name]
            v = (c98 if name in at98 else c_scan)[:, lo:hi]
            if len(dims) == 2:
                v = v.rearrange("p (x y) -> p x y", x=dims[0])
            return v

        def k128(name):
            lo, hi = at128[name]
            return c128[:, lo:hi]

        ident = k128("ident")

        X = [sb(f"x{s}", [128, CC, G, N]) for s in range(STAGES)]
        XR = sb("xr", [128, CC, G, N])
        Y = [sb(f"y{s}", [128, CC, G, N]) for s in range(STAGES)]
        OUT = sb("xo", [128, CC, G, N])
        st = [sb(f"st{s}", [128, 4, 6]) for s in range(STAGES)]
        mv = [sb(f"mv{s}", [128, 4, 2]) for s in range(STAGES)]
        gm = [sb(f"gm{s}", [128, 4]) for s in range(STAGES)]
        dm = [sb(f"dm{s}", [128, 4, 2]) for s in range(STAGES)]
        dd = [sb(f"dd{s}", [128, 4, 2]) for s in range(STAGES)]
        dq = [sb(f"dq{s}", [128, 4]) for s in range(STAGES)]
        ve = [sb(f"ve{s}", [128, 4]) for s in range(STAGES)]
        rs = [sb(f"rs{s}", [128, 4]) for s in range(STAGES)]
        gs = [None, None] + [sb(f"gs{s}", [128, 4]) for s in (2, 3)]
        a_md = sb("a_md", [128, 4])
        a_mo = sb("a_mo", [128, 4])
        a_e = sb("a_e", [128, G * EXPERTS])
        a_rw = sb("a_rw", [128, 3, G, EXPERTS])
        a_w1 = sb("a_w1", [128, G, CC, MID])
        a_w2 = sb("a_w2", [128, G, 6, MID])
        a_w3 = sb("a_w3", [128, G, 128])
        a_pad = sb("a_pad", [128, G, PAD, PAD])
        a_sum = sb("a_sum", [128, 2, G])
        a_mean = sb("a_mean", [128, 2, G])
        a_h2 = sb("a_h2", [128, G, N])
        a_t = sb("a_t", [128, CC, W])
        a_u = a_t
        b_xc = sb("b_xc", [128, CC, G, N + 2])
        b_res = sb("b_res", [128, CC, W])
        b_gate = sb("b_gate", [128, CC, W])
        b_xf = sb("b_xf", [128, CC, G, N])
        XT = sb("b_xt", [HT, 2, G, HEADS, XD])
        XP = sb("b_xp", [HT, 2, G, HEADS, XD])
        Q8 = 2 * G * HEADS
        b_ab = sb("b_ab", [HT, Q8])
        b_ex = sb("b_ex", [HT, Q8])
        b_ln = sb("b_ln", [HT, Q8])
        b_u = sb("b_u", [HT, Q8])
        b_wm = sb("b_wm", [HT, Q8])
        b_m = sb("b_m", [HT, Q8])
        b_nu = sb("b_nu", [HT, Q8])
        b_de = sb("b_de", [HT, Q8])
        b_rc = sb("b_rc", [HT, Q8])
        b_sp = sb("b_sp", [HT, Q8])
        dt = sb("b_dt", [HT, Q8])
        dB = sb("b_db", [HT, Q8, STATE])
        rD = sb("b_rd", [HT, Q8, CHUNK])
        DU0 = sb("b_du0", [HT, 4, N])
        DU1 = sb("b_du1", [HT, 4, HT])
        CD = sb("b_cd", [HT, Q8, STATE, CHUNK])
        AD = sb("b_adt", [HT, Q8, STATE, CHUNK])
        EE = sb("b_ee", [HT, Q8, STATE, CHUNK])
        M1 = M2 = AD
        MC = sb("b_mc", [HT, Q8, CHUNK])
        MC2 = sb("b_mc2", [HT, Q8, CHUNK])
        MC3 = sb("b_mc3", [HT, Q8, CHUNK])
        MB = sb("b_mb", [HT, Q8, CPT, CHUNK])
        FF = sb("b_ff", [HT, Q8, STATE])
        UL = sb("b_ul", [HT, Q8, NCH, STATE])
        CR = sb("b_cr", [HT, Q8, NCH, STATE])
        RE = sb("b_re", [CS, 4, N])
        RR = RE
        US = sb("b_us", [CS, 4, HD])
        YT = XT
        b_y1 = sb("b_y1", [128, CC, W])
        b_y2 = b_y1
        b_o = b_gate
        b_A = sb("b_A", [128, HEADS * STATE])
        b_MA = sb("b_MA", [HT, 2, HEADS, NCH, STATE])
        b_De = sb("b_De", [HT, HEADS, CHUNK])
        PM = sb("b_pm", [HT, 2, HEADS, N])
        PT = sb("b_pt", [HT, 2, HEADS, N])
        c_flat = sb("c_pad", [128, G * PAD * PAD + PAD])
        c_pad = c_flat[:, 0:G * PAD * PAD].rearrange("p (b y x) -> p b y x", b=G, y=PAD)
        c_h = sb("c_h", [128, N])
        c_py = sb("c_py", [HS, 4, 2 * TAPS])
        c_df = sb("c_df", [HS, 4 * 2 * TAPS, HW])
        c_ab = c_df
        c_te = c_df[:, :, :].rearrange("p (t b k d) v -> p t b k d v", t=2, b=G, k=TAPS)
        c_wt = sb("c_wt", [HS, 2, G, TAPS, HW, HW])
        c_wm = [sb(f"c_wm{j}", [HT, 2, N]) for j in range(2)]
        c_z = sb("c_z", [HT, 2, G, TAPS * MID])
        c_v = sb("c_v", [MID, W])
        c_o = sb("c_o", [128, CC, W])
        d_sq = sb("d_sq", [128, N])
        d_pad = sb("d_pad", [128, G, PAD, PAD])
        d_sq2 = sb("d_sq2", [128, N])
        d_h2 = sb("d_h2", [MID, W])
        d_sq3 = OUT[:, :, :, :].rearrange("p c b n -> p c (b n)")
        d_t = d_sq3
        s_a = sb("s_a", [128, 16])
        s_w = c_wt[0:HT, 0, 0].rearrange("p k y x -> p (k y x)")[:, 0:1568].rearrange("p (v n) -> p v n", n=N)
        c_scan = c_wt[0:HT, 0, 1].rearrange("p k y x -> p (k y x)")[:, 0:a["c_scan"].shape[1]]
        S = c_wt[0:HT, 1, 0].rearrange("p k y x -> p (k y x)")[:, 0:HEADS * N].rearrange("p (h n) -> p h n", h=HEADS)
        s_half = sb("s_half", [128, Q8])
        s_m = sb("s_m", [128, HEADS, 4])
        bn_r = sb("bn_r", [128, NBN])
        s_rank = sb("s_rank", [HT, 2, HEADS, 4])

        ps = [ctx.enter_context(nc.psum_tensor(f"ps{i}", [128, 512], F32)) for i in range(8)]

        def banks(name, which, fills):
            return Banks([ps[i] for i in which], [sem(f"{name}_filled{i}") for i in which],
                         [sem(f"{name}_drained{i}") for i in which], fills)

        A = banks("a", [0], 9)
        B = banks("b", [2, 3, 4], 30)
        C = banks("c", [5], 7)
        CT = banks("ct", [6, 7], 26)
        D = banks("d", [1], 6)

        def sig(name, per=1):
            return Signal(sem(name), per)

        consts_in = sem("consts_in")
        n_consts = [0]
        x_in = sig("x_in", 16 * CC)
        xr_in = sig("xr_in", 16 * CC)
        out_stored = sig("out_stored", 16 * CC)
        x_done = [None] + [sig(f"x{s}_written") for s in range(1, STAGES)] + [sig("out_written")]
        stats = [sig(f"stats{s}") for s in range(STAGES)]
        spread = [sig(f"spread{s}") for s in range(STAGES)]
        rstd = [sig(f"rstd{s}") for s in range(STAGES)]
        normed = [sig(f"normed{s}", 4) for s in range(STAGES)]
        pads_zero = sem("pads_zero")
        setup = sem("setup_done")
        setup_pe = sem("setup_pe")
        setup_v = sem("setup_v")
        setup_p = sem("setup_p")
        setup_s = sem("setup_s")
        setup_r = sem("setup_r")
        setup_a = sem("setup_a")
        b_ff = sig("b_ff_ready")

        a_md_ok = sig("a_md_ready")
        a_mix = sig("a_mixed", 3)
        norm_shift = [None, None] + [sig(f"norm_shift{s}") for s in (2, 3)]
        a_mn = sig("a_mean_ready", 2)
        a_u_ok = sig("a_u_written", 2)

        b_gate_ok = sig("b_gate_written")
        b_dw = sig("b_dwconv")
        b_xf_ok = sig("b_xf_written")
        b_abs = sig("b_abs")
        b_e = sig("b_e")
        b_u_ok = sig("b_u_ready")
        b_l = sig("b_ln")
        b_dt = sig("b_dt_ready")
        b_rd = sig("b_rD_ready")
        b_cd = sig("b_cd_ready")
        b_du = sig("b_du_ready")
        b_ee = sig("b_ee_ready")
        b_mb = sig("b_mb_ready")
        b_ul = sig("b_ul_ready")
        b_cr_ok = sig("b_cr_ready")
        b_y2_ok = sig("b_y2_ready")

        c_df_ok = sig("c_df_ready")
        c_ab_ok = sig("c_ab_ready")
        c_te_ok = sig("c_te_ready")
        c_wt_v = sig("c_wt_by_vector", 2)
        c_wt_p = sig("c_wt_by_pool", 2)

        d_h1 = sig("d_h1_written")
        d_h2_ok = sig("d_h2_written")

        xsrc = a["x"]

        def pair(t, g, c):
            v = t.rearrange("(g b) (c p) n -> c g p b n", b=G, p=128)[c]
            return v[g] if isinstance(g, int) else v[bass.ds(g, 1)].rearrange("o p b n -> (o p) b n")

        def bilinear(tt, t, b):
            te = c_te[:, t, b]
            return tt(c_wt[:, t, b], te[:, :, 0, :].unsqueeze(3).to_broadcast([HS, TAPS, HW, HW]),
                      te[:, :, 1, :].unsqueeze(2).to_broadcast([HS, TAPS, HW, HW]), ALU.mult)

        def half(b):
            return slice(b * MID, (b + 1) * MID)

        def in_rows(t):
            return t[0:HT, 0:4 * HS].rearrange("p (r x) -> p r x", x=PAD)[:, :, 0:HW]

        block = ctx.enter_context(nc.Block())
        loads = [(c98[:, :], a["c98"]), (c128[:, :], a["c128"]), (c_scan, a["c_scan"]), (bnp[:, :, :], a["bnp"]), (rows[:, :], a["rows"]),
                 (w1[:, :, :], a["w1"]), (r1[:, :, :], a["r1"]), (r23[:, :, :], a["r23"]),
                 (w2[:, :, :], a["w2"]), (w3[:, :, :], a["w3"]), (inw[:, :, :, :], a["inw"]), (cvec[:, :], a["cvec"]),
                 (dbcw[:, :, :, :], a["dbcw"]), (outw[:, :, :, :], a["outw"]), (c1w[:, :, :], a["c1w"]),
                 (offw[:, :, :], a["offw"]), (dcw[:, :], a["dcw"]), (c2w[:, :], a["c2w"]), (d1w[:, :, :], a["d1w"]),
                 (d2w[:, :, :], a["d2w"]), (d3w[:, :], a["d3w"])]
        ALL_IN = 16 * len(loads)

        @block.sync
        def _(sp):
            for dst, src in loads:
                sp.dma_start(dst, src).then_inc(consts_in, 16)

            def stage0(i, part, g):
                if i == 0:
                    sp.wait_ge(normed[0].sem, normed[0].count(g, 0))
                    for c in range(CC):
                        sp.dma_start(X[0][:, c, :, :], pair(xsrc, g, c)).then_inc(x_in.sem, 16)
                if i == 1:
                    sp.wait_ge(x_done[1].sem, x_done[1].count(g, 0))
                    for c in range(CC):
                        sp.dma_start(XR[:, c, :, :], pair(xsrc, g, c)).then_inc(xr_in.sem, 16)

            def stage3(i, part, g):
                if i == 6:
                    sp.wait_ge(x_done[4].sem, x_done[4].count(g))
                    for c in range(CC):
                        sp.dma_start(pair(out, g, c), OUT[:, c, :, :]).then_inc(out_stored.sem, 16)

            def idle(i, part, g):
                return

            for_rounds(sp, "sync", [stage0, idle, idle, stage3])
            sp.wait_ge(out_stored.sem, 16 * CC * GROUPS)

        @block.tensor
        def _(pe):
            def mm(o, l, r, start=True, stop=True):
                return nc.tensor.matmul(o, l, r, start=start, stop=stop)

            def group_mean(s, g, bank, f, rhs, ready):
                pe.wait_ge(ready.sem, ready.count(g))
                pe.wait_ge(bank.drained(f), bank.empty(g, f))
                t = bank.tile(f)
                mm(t[:, 0:4], k128("group"), rhs).then_inc(bank.filled(f), 1)

            def route(g, bank, f, mean, ws, b0):
                pe.wait_ge(bank.drained(f), bank.empty(g, f))
                t = bank.tile(f)
                bias = rows[0:1, b0:b0 + EXPERTS].unsqueeze(1).to_broadcast([1, G, EXPERTS])
                mm(t[:, 0:G * EXPERTS].rearrange("p (b e) -> p b e", b=G), ones[0:1, :], bias, stop=False)
                for b in range(G):
                    for j, w in enumerate(ws):
                        m = mean[j][:, b:b + 1]
                        last = mm(t[:, b * EXPERTS:(b + 1) * EXPERTS], m.to_broadcast([m.shape[0], 128]), w,
                                  start=False, stop=(b == G - 1 and j == len(ws) - 1))
                last.then_inc(bank.filled(f), 1)

            def conv3x3(t, wt, pad):
                for j in range(6):
                    dy, dx = 2 * (j // 3), j % 3
                    for b in range(G):
                        last = mm(t[half(b), 0:N], wt(b, j), pad[:, b, dy:dy + HW, dx:dx + HW],
                                  start=(j == 0), stop=(j == 5))
                return last

            def conv1x1(t, wt, y):
                for c in range(CC):
                    for b in range(G):
                        last = mm(t[half(b), 0:N], wt(b, c), y[:, c, b, :], start=(c == 0), stop=(c == CC - 1))
                return last

            def stage0(i, part, g):
                if i == 1:
                    group_mean(0, g, A, 0, mv[0][:, :, 0], stats[0])
                if i == 2:
                    group_mean(0, g, A, 1, dq[0][:, :], spread[0])
                if i == 3:
                    pe.wait_ge(a_md_ok.sem, a_md_ok.count(g))
                    route(g, A, 2, [a_md[:, 2 * c:2 * c + 2] for c in range(CC)],
                          [r1[:, c, :] for c in range(CC)], ROW_R[0])
                if i == 5:
                    pe.wait_ge(a_mix.sem, a_mix.count(g, 1))
                    pe.wait_ge(normed[0].sem, normed[0].count(g))
                    pe.wait_ge(A.drained(3), A.empty(g, 3))
                    conv1x1(A.tile(3), lambda b, c: a_w1[:, b, c, :], Y[0]).then_inc(A.filled(3), 1)
                if i == 6:
                    pe.wait_ge(a_mn.sem, a_mn.count(g, 1))
                    route(g, A, 4, [a_mean[0:MID, 0, :]], [r23[:, 0, :]], ROW_R[1])
                if i == 8:
                    pe.wait_ge(a_mix.sem, a_mix.count(g, 2))
                    pe.wait_ge(A.drained(3), A.full(g, 3))
                    pe.wait_ge(A.drained(5), A.empty(g, 5))
                    conv3x3(A.tile(5), lambda b, j: a_w2[:, b, j, :], a_pad).then_inc(A.filled(5), 1)
                if i == 9:
                    pe.wait_ge(a_mn.sem, a_mn.count(g, 2))
                    route(g, A, 6, [a_mean[0:MID, 1, :]], [r23[:, 1, :]], ROW_R[2])
                if i == 10:
                    if part == 0:
                        pe.wait_ge(a_mix.sem, a_mix.count(g, 3))
                        pe.wait_ge(A.drained(5), A.full(g, 5))
                    m = part
                    pe.wait_ge(A.drained(7 + m), A.empty(g, 7 + m))
                    t = A.tile(7 + m)
                    for b in range(G):
                        last = mm(t[:, b * N:(b + 1) * N], a_w3[m * MID:(m + 1) * MID, b, :],
                                  a_h2[m * MID:(m + 1) * MID, b, :])
                    last.then_inc(A.filled(7 + m), 1)

            def stage1(i, part, g):
                if i == 1:
                    group_mean(1, g, B, 0, mv[1][:, :, 0], stats[1])
                if i == 2:
                    group_mean(1, g, B, 1, dq[1][:, :], spread[1])
                if i == 4:
                    m = part
                    if m == 0:
                        pe.wait_ge(normed[1].sem, normed[1].count(g))
                    pe.wait_ge(B.drained(2 + m), B.empty(g, 2 + m))
                    t = B.tile(2 + m)
                    for c in range(CC):
                        last = mm(t[:, 0:W], inw[:, c, m, :], Y[1][:, c, :, :], start=(c == 0), stop=(c == CC - 1))
                    last.then_inc(B.filled(2 + m), 1)
                if i == 6:
                    if part == 0:
                        pe.wait_ge(b_xf_ok.sem, b_xf_ok.count(g))
                    k, tt, b = part, part // G, part % G
                    pe.wait_ge(B.drained(8 + k), B.empty(g, 8 + k))
                    t = B.tile(8 + k)
                    cols = slice(tt * HT, (tt + 1) * HT)
                    for h in range(HEADS):
                        nc.tensor.transpose(t[0:HT, h * XD:h * XD + HD], b_xf[:, h, b, cols], ident)
                    o = t[0:HT, 0:HEADS * XD].rearrange("p (h x) -> p h x", h=HEADS)[:, :, HD:XD]
                    for c in range(CC):
                        mm(o, b_xf[:, c, b, cols], dbcw[:, c, :, :], start=(c == 0), stop=False)
                    last = mm(o, ones[0:1, 0:HT], rows[0:1, ROW_DBC:ROW_DBC + HEADS * DBC]
                              .rearrange("p (h x) -> p h x", h=HEADS), start=False)
                    last.then_inc(B.filled(8 + k), 1)
                if i == 7:
                    if part == 0:
                        pe.wait_ge(B.drained(9), B.full(g, 9))
                        pe.wait_ge(B.drained(10), B.full(g, 10))
                        pe.wait_ge(B.drained(11), B.full(g, 11))
                    k, tt, b = part, part // G, part % G
                    pe.wait_ge(B.drained(12 + k), B.empty(g, 12 + k))
                    t = B.tile(12 + k)
                    for h in range(HEADS):
                        for n in range(2):
                            last = mm(t[0:HT, h * XD:(h + 1) * XD], PM[:, n, h, tt * HT:(tt + 1) * HT],
                                      XT[:, n, b, h, :], start=(n == 0), stop=(n == 1))
                    last.then_inc(B.filled(12 + k), 1)
                if i == 9 and part == 0:
                    pe.wait_ge(b_rd.sem, b_rd.count(g))
                    pe.wait_ge(B.drained(16), B.empty(g, 16))
                    t = B.tile(16)
                    last = mm(t[0:HT, 0:Q8 * CHUNK], k98("later"), rD[:, :, :].rearrange("p q t -> p (q t)"))
                    last.then_inc(B.filled(16), 1)
                if i == 9 and part in (1, 2):
                    b = part - 1
                    if b == 0:
                        pe.wait_ge(b_du.sem, b_du.count(g))
                    pe.wait_ge(B.drained(17 + b), B.empty(g, 17 + b))
                    t = B.tile(17 + b)
                    for h in range(HEADS):
                        o = t[0:CS, h * N:(h + 1) * N]
                        mm(o, b_MA[:, 0, h].rearrange("p c s -> p (c s)"), DU0[:, 2 * b + h, :], stop=False)
                        last = mm(o[:, HT:N], b_MA[:, 1, h].rearrange("p c s -> p (c s)"), DU1[:, 2 * b + h, :],
                                  start=False)
                    last.then_inc(B.filled(17 + b), 1)
                if i == 9 and part == 3:
                    pe.wait_ge(b_cd.sem, b_cd.count(g))
                    for k in range(2):
                        pe.wait_ge(B.drained(19 + k), B.empty(g, 19 + k))
                        t = B.tile(19 + k)
                        last = mm(t[0:HT, 0:448], k98("same"),
                                  CD[:, 4 * k:4 * k + 4].rearrange("p q s t -> p (q s t)"))
                        last.then_inc(B.filled(19 + k), 1)
                if i == 10:
                    pe.wait_ge(b_cr_ok.sem, b_cr_ok.count(g))
                    for b in range(G):
                        pe.wait_ge(B.drained(21 + b), B.empty(g, 21 + b))
                        t = B.tile(21 + b)
                        for h in range(HEADS):
                            for tt in range(2):
                                o = t[0:CS, h * N + tt * HT:h * N + (tt + 1) * HT]
                                last = nc.tensor.transpose(
                                    o, CR[:, tt * 4 + 2 * b + h].rearrange("p c s -> p (c s)"), ident[0:HT, 0:HT])
                        last.then_inc(B.filled(21 + b), 1)
                if i == 11:
                    pe.wait_ge(b_ul.sem, b_ul.count(g))
                    pe.wait_ge(B.drained(23), B.empty(g, 23))
                    t = B.tile(23)
                    for b in range(G):
                        for h in range(HEADS):
                            for tt in range(2):
                                q = tt * 4 + b * 2 + h
                                last = mm(t[0:CS, (2 * b + h) * HD:(2 * b + h + 1) * HD],
                                          UL[:, q].rearrange("p c s -> p (c s)"), XP[:, tt, b, h, 0:HD],
                                          start=(tt == 0), stop=(tt == 1))
                    last.then_inc(B.filled(23), 1)
                if i == 12:
                    if part == 0:
                        pe.wait_ge(b_mb.sem, b_mb.count(g))
                        pe.wait_ge(B.drained(21), B.full(g, 21))
                        pe.wait_ge(B.drained(22), B.full(g, 22))
                        pe.wait_ge(B.drained(23), B.full(g, 23))
                    tt = part
                    pe.wait_ge(B.drained(24 + tt), B.empty(g, 24 + tt))
                    t = B.tile(24 + tt)
                    for b in range(G):
                        for h in range(HEADS):
                            j = 2 * b + h
                            o = t[0:HT, j * HD:(j + 1) * HD]
                            mm(o, MB[:, tt * 4 + j].rearrange("p c t -> p (c t)"), XP[:, tt, b, h, 0:HD],
                               stop=False)
                            last = mm(o, RR[:, j, tt * HT:(tt + 1) * HT], US[:, j, :], start=False)
                    last.then_inc(B.filled(24 + tt), 1)
                if i == 13:
                    if part == 0:
                        pe.wait_ge(B.drained(24), B.full(g, 24))
                        pe.wait_ge(B.drained(25), B.full(g, 25))
                    h = part
                    pe.wait_ge(B.drained(26 + h), B.empty(g, 26 + h))
                    t = B.tile(26 + h)
                    for b in range(G):
                        for tt in range(2):
                            last = mm(t[:, b * N:(b + 1) * N], YT[:, tt, b, h, 0:HD], PT[:, tt, h, :],
                                      start=(tt == 0), stop=(tt == 1))
                    last.then_inc(B.filled(26 + h), 1)
                if i == 15:
                    if part == 0:
                        pe.wait_ge(b_y2_ok.sem, b_y2_ok.count(g))
                    m = part
                    pe.wait_ge(B.drained(28 + m), B.empty(g, 28 + m))
                    t = B.tile(28 + m)
                    for c in range(CC):
                        last = mm(t[:, 0:W], outw[:, c, m, :], b_y2[:, c, :], start=(c == 0), stop=(c == CC - 1))
                    last.then_inc(B.filled(28 + m), 1)

            def stage2(i, part, g):
                if i == 1:
                    group_mean(2, g, C, 0, mv[2][:, :, 0], stats[2])
                if i == 2:
                    group_mean(2, g, C, 1, dq[2][:, :], spread[2])
                if i == 3:
                    pe.wait_ge(normed[2].sem, normed[2].count(g))
                    pe.wait_ge(C.drained(2), C.empty(g, 2))
                    conv1x1(C.tile(2), lambda b, c: c1w[:, c, :], Y[2]).then_inc(C.filled(2), 1)
                if i == 4:
                    t = C.tile(3)
                    if part == 0:
                        pe.wait_ge(C.drained(3), C.empty(g, 3))
                        mm(t[0:HS, 0:2 * G * 2 * TAPS].rearrange("p (q j) -> p q j", q=2 * G), ones[0:1, 0:HS],
                           rows[0:1, ROW_OFF:ROW_OFF + 2 * TAPS].unsqueeze(1).to_broadcast([1, 2 * G, 2 * TAPS]),
                           stop=False)
                        pe.wait_ge(C.drained(2), C.full(g, 2))
                    tt = part // G
                    b = part % G
                    o = t[0:HS, (2 * tt + b) * 2 * TAPS:(2 * tt + b + 1) * 2 * TAPS]
                    for j in range(6):
                        at = (b * PAD + 2 * (j // 3) + HR * tt) * PAD + j % 3
                        last = mm(o, c_flat[:, at:at + HS], offw[:, j, :], start=False,
                                  stop=(tt == 1 and b == G - 1 and j == 5))
                    if part == 3:
                        last.then_inc(C.filled(3), 1)
                if i == 5:
                    k = part
                    tt, h, b = k // 4, k // 2 % 2, k % 2
                    pe.wait_ge(CT.drained(k), CT.empty(g, k))
                    t = CT.tile(k)
                    w = TAPS * MID // 2
                    last = mm(t[0:HT, 0:w], c_h[half(b), tt * HT:(tt + 1) * HT],
                              dcw[half(b), h * w:(h + 1) * w])
                    last.then_inc(CT.filled(k), 1)
                if i == 7:
                    def turn(k):
                        b, tap = k % G, k // G
                        pe.wait_ge(CT.drained(8 + k), CT.empty(g, 8 + k))
                        t = CT.tile(8 + k)
                        for m in range(2):
                            for n in range(2):
                                src = c_wt[:, n, b, tap, HR * m:HR * (m + 1), :].rearrange("p y x -> p (y x)")
                                last = nc.tensor.transpose(t[0:HT, (2 * m + n) * HS:(2 * m + n + 1) * HS], src,
                                                           ident[0:HS, 0:HS])
                        last.then_inc(CT.filled(8 + k), 1)

                    def add(tap):
                        for b in range(G):
                            pe.wait_ge(CT.drained(8 + G * tap + b), CT.full(g, 8 + G * tap + b))
                        t = C.tile(4)
                        for m in range(2):
                            for b in range(G):
                                last = mm(t[half(b), 0:N], c_z[:, m, b, tap * MID:(tap + 1) * MID],
                                          c_wm[b][:, m, :], start=(tap == 0 and m == 0),
                                          stop=(tap == TAPS - 1 and m == 1))
                        return last

                    tap = part // 2
                    if part % 2:
                        last = add(tap)
                        if tap == TAPS - 1:
                            last.then_inc(C.filled(4), 1)
                    else:
                        if tap == 0:
                            pe.wait_ge(CT.drained(6), CT.full(g, 6))
                            pe.wait_ge(CT.drained(7), CT.full(g, 7))
                            pe.wait_ge(C.drained(4), C.empty(g, 4))
                            pe.wait_ge(c_wt_v.sem, c_wt_v.count(g))
                            pe.wait_ge(c_wt_p.sem, c_wt_p.count(g))
                        for b in range(G):
                            turn(G * tap + b)
                if i == 11:
                    if part == 0:
                        pe.wait_ge(C.drained(4), C.full(g, 4))
                    m = part
                    pe.wait_ge(C.drained(5 + m), C.empty(g, 5 + m))
                    t = C.tile(5 + m)
                    mm(t[:, 0:W], c2w[:, m * 128:(m + 1) * 128], c_v[:, :]).then_inc(C.filled(5 + m), 1)

            def stage3(i, part, g):
                if i == 1:
                    group_mean(3, g, D, 0, mv[3][:, :, 0], stats[3])
                if i == 2:
                    group_mean(3, g, D, 1, dq[3][:, :], spread[3])
                if i == 3:
                    pe.wait_ge(normed[3].sem, normed[3].count(g))
                    pe.wait_ge(D.drained(2), D.empty(g, 2))
                    conv1x1(D.tile(2), lambda b, c: d1w[:, c, :], Y[3]).then_inc(D.filled(2), 1)
                if i == 4:
                    pe.wait_ge(d_h1.sem, d_h1.count(g))
                    pe.wait_ge(D.drained(3), D.empty(g, 3))
                    conv3x3(D.tile(3), lambda b, j: d2w[:, j, :], d_pad).then_inc(D.filled(3), 1)
                if i == 6:
                    if part == 0:
                        pe.wait_ge(d_h2_ok.sem, d_h2_ok.count(g))
                    m = part
                    pe.wait_ge(D.drained(4 + m), D.empty(g, 4 + m))
                    t = D.tile(4 + m)
                    mm(t[:, 0:W], d3w[:, m * 128:(m + 1) * 128], d_h2[:, :]).then_inc(D.filled(4 + m), 1)

            pe.wait_ge(consts_in, ALL_IN)
            pe.wait_ge(pads_zero, 1)
            mm(ps[0][:, 0:ROW_BC], ones[0:1, :], rows[0:1, 0:ROW_BC]).then_inc(setup_pe, 1)
            pe.wait_ge(setup, 1)
            for h in range(HEADS):
                for n in range(2):
                    for tt in range(2):
                        last = nc.tensor.transpose(ps[1 + h][0:HT, (2 * tt + n) * HT:(2 * tt + n + 1) * HT],
                                                   PM[:, n, h, tt * HT:(tt + 1) * HT], ident[0:HT, 0:HT])
            last.then_inc(setup_pe, 1)
            pe.wait_ge(setup, 2)
            for_rounds(pe, "tensor", [stage0, stage1, stage2, stage3])

        @block.scalar
        def _(act):
            def fn(o, i, f, **kw):
                return nc.scalar.activation(o, i, f, **kw)

            def halves(t, b, pad, j, sums=None):
                for h in range(2):
                    part, r0 = slice(h * MID, (h + 1) * MID), 1 - h
                    src = t[half(b), 0:N].rearrange("p (y x) -> p y x", x=HW)
                    kw = {} if sums is None or h else {"accum_out": sums[0:MID, b:b + 1]}
                    last = fn(pad[part, b, r0:r0 + HW, 1:1 + HW], src, ACT.Relu, scale=bn_s[half(b), j:j + 1],
                              bias=bn_b[half(b), j:j + 1], **kw)
                return last

            def stage0(i, part, g):
                def half_tanh(f):
                    act.wait_ge(A.filled(f), A.full(g, f))
                    t = A.tile(f)
                    fn(a_e[:, :], t[:, 0:G * EXPERTS], ACT.Tanh, scale=0.5).then_inc(A.drained(f), 1)

                if i == 3:
                    half_tanh(2)
                if i == 5:
                    if part == 0:
                        act.wait_ge(A.filled(3), A.full(g, 3))
                    last = halves(A.tile(3), part, a_pad, BN_A1, a_sum[:, 0, :])
                    if part == G - 1:
                        last.then_inc(A.drained(3), 1)
                if i == 6:
                    half_tanh(4)
                if i == 8:
                    act.wait_ge(A.filled(5), A.full(g, 5))
                    t = A.tile(5)
                    for b in range(G):
                        fn(a_h2[0:MID, b, :], t[half(b), 0:N], ACT.Relu,
                           scale=bn_s[half(b), BN_A2:BN_A2 + 1], bias=bn_b[half(b), BN_A2:BN_A2 + 1],
                           accum_out=a_sum[0:MID, 1, b:b + 1])
                        last = fn(a_h2[MID:128, b, :], t[half(b), 0:N], ACT.Relu,
                                  scale=bn_s[half(b), BN_A2:BN_A2 + 1], bias=bn_b[half(b), BN_A2:BN_A2 + 1])
                    last.then_inc(A.drained(5), 1)
                if i == 9:
                    half_tanh(6)
                if i == 10:
                    m = part
                    act.wait_ge(A.drained(7 + m), A.full(g, 7 + m))
                    fn(a_u[:, m, :], a_t[:, m, :], ACT.Relu, bias=bn_b[:, BN_A3 + m:BN_A3 + m + 1])\
                        .then_inc(a_u_ok.sem, 1)

            def stage1(i, part, g):
                if i == 4:
                    m = part
                    act.wait_ge(B.filled(2 + m), B.full(g, 2 + m))
                    t = B.tile(2 + m)
                    if m < 2:
                        o = b_xc[:, m, :, 1:1 + N]
                    else:
                        o = (b_res if m < 4 else b_gate)[:, m % 2, :].rearrange("p (b n) -> p b n", b=G)
                    fn(o, t[:, 0:W].rearrange("p (b n) -> p b n", b=G), ACT.Silu,
                                 bias=cvec[:, m:m + 1]).then_inc(B.drained(2 + m), 1)
                if i == 5 and part == 0:
                    act.wait_ge(B.drained(6), B.full(g, 6))
                    act.wait_ge(B.drained(7), B.full(g, 7))
                    fn(b_gate[:, :, :], b_gate[:, :, :], ACT.Silu).then_inc(b_gate_ok.sem, 1)
                if i == 5 and part == 1:
                    act.wait_ge(b_dw.sem, b_dw.count(g))
                    fn(b_xf[:, :, :, :], b_xf[:, :, :, :], ACT.Silu).then_inc(b_xf_ok.sem, 1)
                if i in (6, 7):
                    f, dst = ((8, XT), (12, XP))[i - 6]
                    k = 2 * part
                    act.wait_ge(B.filled(f + k), B.full(g, f + k))
                    t = B.tile(f + k)
                    fn(dst[:, k // 2, k % 2, :, :],
                                 t[0:HT, 0:HEADS * XD].rearrange("p (h x) -> p h x", h=HEADS), ACT.Copy).then_inc(B.drained(f + k), 1)
                if i == 8 and part == 0:
                    act.wait_ge(B.drained(13), B.full(g, 13))
                    act.wait_ge(B.drained(14), B.full(g, 14))
                    act.wait_ge(B.drained(15), B.full(g, 15))
                    x = XP[:, :, :, :, HD:HD + 1].rearrange("p t b h o -> p (t b h) o")
                    fn(b_ab[:, :].unsqueeze(2), x, ACT.Abs, scale=LOG2E).then_inc(b_abs.sem, 1)
                if i == 8 and part == 1:
                    act.wait_ge(b_u_ok.sem, b_u_ok.count(g))
                    fn(b_ln[:, :], b_u[:, :], ACT.Ln).then_inc(b_l.sem, 1)
                if i == 9 and part < 2:
                    b = part
                    act.wait_ge(B.filled(17 + b), B.full(g, 17 + b))
                    t = B.tile(17 + b)
                    fn(RE[:, 2 * b:2 * b + 2, :].rearrange("p h n -> p (h n)"), t[0:CS, 0:W], ACT.Exp,
                                 scale=-1.0).then_inc(B.drained(17 + b), 1)
                if i == 9 and part == 2:
                    act.wait_ge(B.drained(16), B.full(g, 16))
                    fn(EE[:, :, :, :], AD[:, :, :, :], ACT.Exp, scale=-1.0).then_inc(b_ee.sem, 1)
                if i == 11:
                    act.wait_ge(B.filled(23), B.full(g, 23))
                    t = B.tile(23)
                    fn(US[:, :, :].rearrange("p j d -> p (j d)"), t[0:CS, 0:4 * HD], ACT.Copy).then_inc(B.drained(23), 1)
                if i == 12:
                    act.wait_ge(B.filled(24), B.full(g, 24))
                    t = B.tile(24)
                    fn(YT[:, 0, :, :, 0:HD].rearrange("p b h d -> p (b h) d"),
                                 t[0:HT, 0:4 * HD].rearrange("p (j d) -> p j d", d=HD), ACT.Copy).then_inc(B.drained(24), 1)
                if i == 15:
                    m = part
                    act.wait_ge(B.filled(28 + m), B.full(g, 28 + m))
                    t = B.tile(28 + m)
                    fn(b_o[:, m, :], t[:, 0:W], ACT.Silu, bias=cvec[:, 14 + m:15 + m]).then_inc(B.drained(28 + m), 1)

            def scale_shift(s, g):
                act.wait_ge(norm_shift[s].sem, norm_shift[s].count(g))
                for c in range(CC):
                    for b in range(G):
                        j = 2 * c + b
                        fn(Y[s][:, c, b, :], X[s][:, c, b, :], ACT.Identity, scale=rs[s][:, j:j + 1],
                           bias=gs[s][:, j:j + 1]).then_inc(normed[s].sem, 1)

            def stage2(i, part, g):
                if i == 3 and part == 0:
                    scale_shift(2, g)
                if i == 3 and part == 1:
                    act.wait_ge(C.filled(2), C.full(g, 2))
                    t = C.tile(2)
                    fn(c_h[:, :], t[:, 0:N], ACT.Relu, scale=bn_s[:, BN_C1:BN_C1 + 1], bias=bn_b[:, BN_C1:BN_C1 + 1])
                if i == 3 and part == 2:
                    for b in range(G):
                        last = halves(C.tile(2), b, c_pad, BN_C1)
                    last.then_inc(C.drained(2), 1)
                if i == 4 and part == 0:
                    act.wait_ge(c_df_ok.sem, c_df_ok.count(g))
                    fn(c_ab[:, :, :], c_df[:, :, :], ACT.Abs).then_inc(c_ab_ok.sem, 1)
                if i == 4 and part == 1:
                    act.wait_ge(c_ab_ok.sem, c_ab_ok.count(g))
                    fn(c_df[:, :, :], c_ab[:, :, :], ACT.Relu,
                       bias=1.0, scale=-1.0).then_inc(c_te_ok.sem, 1)
                if i == 5:
                    k = 2 * part
                    act.wait_ge(CT.filled(k), CT.full(g, k))
                    t = CT.tile(k)
                    w = TAPS * MID // 2
                    h = k // 2 % 2
                    fn(c_z[:, k // 4, 0, h * w:(h + 1) * w], t[0:HT, 0:w], ACT.Copy).then_inc(CT.drained(k), 1)
                if i == 7:
                    k = G * part
                    act.wait_ge(CT.filled(8 + k), CT.full(g, 8 + k))
                    t = CT.tile(8 + k)
                    fn(c_wm[k % G][:, :, :].rearrange("p m (y x) -> p (m y) x", x=HW), in_rows(t),
                                  ACT.Copy).then_inc(CT.drained(8 + k), 1)
                if i == 11 and part == 0:
                    act.wait_ge(C.filled(4), C.full(g, 4))
                    t = C.tile(4)
                    for b in range(G):
                        last = fn(c_v[:, b * N:(b + 1) * N], t[half(b), 0:N], ACT.Identity,
                                  scale=bn_s[half(b), BN_C2:BN_C2 + 1], bias=bn_b[half(b), BN_C2:BN_C2 + 1])
                    last.then_inc(C.drained(4), 1)
                if i == 11 and part > 0:
                    m = part - 1
                    act.wait_ge(C.filled(5 + m), C.full(g, 5 + m))
                    t = C.tile(5 + m)
                    j = BN_C3 + m
                    fn(c_o[:, m, :], t[:, 0:W], ACT.Relu, scale=bn_s[:, j:j + 1],
                                 bias=bn_b[:, j:j + 1]).then_inc(C.drained(5 + m), 1)

            def stage3(i, part, g):
                if i == 3 and part == 0:
                    scale_shift(3, g)
                if i == 3 and part == 1:
                    act.wait_ge(D.filled(2), D.full(g, 2))
                    t = D.tile(2)
                    fn(d_sq[:, :], t[:, 0:N], ACT.Square, bias=1.0).then_inc(D.drained(2), 1)
                if i == 5:
                    act.wait_ge(D.filled(3), D.full(g, 3))
                    t = D.tile(3)
                    fn(d_sq2[:, :], t[:, 0:N], ACT.Square, bias=1.0).then_inc(D.drained(3), 1)
                if i == 6:
                    if part == 0:
                        act.wait_ge(out_stored.sem, out_stored.count(g, 0))
                    m = part
                    act.wait_ge(D.filled(4 + m), D.full(g, 4 + m))
                    t = D.tile(4 + m)
                    fn(d_sq3[:, m, :], t[:, 0:W], ACT.Square, bias=1.0).then_inc(D.drained(4 + m), 1)

            act.wait_ge(setup_r, 1)
            fn(b_A[:, :], rowb[:, ROW_A:ROW_A + HEADS * STATE], ACT.Exp).then_inc(setup_a, 1)
            act.wait_ge(setup, 2)
            act.wait_ge(pads_zero, NZERO)
            for_rounds(act, "scalar", [stage0, stage1, stage2, stage3])

        @block.gpsimd
        def _(pool):
            def tt(o, x, y, op):
                return nc.gpsimd.tensor_tensor(out=o, in0=x, in1=y, op=op)

            def rstd_of(s, i, g, bank):
                if i == 2:
                    pool.wait_ge(bank.drained(1), bank.full(g, 1))
                    tt(rs[s][:, :], ve[s][:, :], root[:, 0:4], ALU.pow).then_inc(rstd[s].sem, 1)

            def add_input(s, g, m, x, y):
                ins = tt(X[s][:, m, :, :].rearrange("p b n -> p (b n)"), x, y.rearrange("p b n -> p (b n)"), ALU.add)
                if m == CC - 1:
                    ins.then_inc(x_done[s].sem, 1)

            def stage0(i, part, g):
                rstd_of(0, i, g, A)
                if i == 10:
                    if part == 0:
                        pool.wait_ge(xr_in.sem, xr_in.count(g))
                        pool.wait_ge(x_done[2].sem, x_done[2].count(g, 0))
                    m = part
                    pool.wait_ge(a_u_ok.sem, a_u_ok.count(g, m + 1))
                    add_input(1, g, m, a_u[:, m, :], XR[:, m, :, :])

            def stage1(i, part, g):
                rstd_of(1, i, g, B)
                if i == 8 and part == 0:
                    pool.wait_ge(b_abs.sem, b_abs.count(g))
                    tt(b_ex[:, :], s_half[0:HT, :], b_ab[:, :], ALU.pow).then_inc(b_e.sem, 1)
                if i == 8 and part > 0:
                    if part == 1:
                        pool.wait_ge(B.drained(13), B.full(g, 13))
                        pool.wait_ge(B.drained(14), B.full(g, 14))
                        pool.wait_ge(B.drained(15), B.full(g, 15))
                    m = part - 1
                    ins = tt(CR[:, 4 * m:4 * m + 4],
                             XP[:, m, :, :, HD + 1 + STATE:XD].rearrange("p b h s -> p (b h) s").unsqueeze(2)
                             .to_broadcast([HT, 4, NCH, STATE]),
                             k98("after", 2, NCH)[:, m].unsqueeze(1).unsqueeze(3)
                             .to_broadcast([HT, 4, NCH, STATE]), ALU.mult)
                    if part == 2:
                        ins.then_inc(b_cr_ok.sem, 1)
                if i == 10:
                    if part == 0:
                        pool.wait_ge(b_ff.sem, b_ff.count(g))
                    m = part
                    ins = tt(UL[:, 4 * m:4 * m + 4], FF[:, 4 * m:4 * m + 4].unsqueeze(2)
                             .to_broadcast([HT, 4, NCH, STATE]),
                             k98("chunk14", 2, NCH)[:, m].unsqueeze(1).unsqueeze(3)
                             .to_broadcast([HT, 4, NCH, STATE]), ALU.mult)
                    if part == 1:
                        ins.then_inc(b_ul.sem, 1)
                if i == 13:
                    h = part
                    pool.wait_ge(B.drained(26 + h), B.full(g, 26 + h))
                    ins = tt(b_y2[:, h, :], b_y1[:, h, :], b_res[:, h, :], ALU.add)
                    if part == HEADS - 1:
                        ins.then_inc(b_y2_ok.sem, 1)
                if i == 15:
                    if part == 0:
                        pool.wait_ge(x_done[3].sem, x_done[3].count(g, 0))
                    m = part
                    pool.wait_ge(B.drained(28 + m), B.full(g, 28 + m))
                    add_input(2, g, m, b_o[:, m, :], X[1][:, m, :, :])

            def stage2(i, part, g):
                rstd_of(2, i, g, C)
                if i == 6:
                    if part == 0:
                        pool.wait_ge(c_te_ok.sem, c_te_ok.count(g))
                    t = part
                    bilinear(tt, t, 1).then_inc(c_wt_p.sem, 1)
                if i == 11:
                    if part == 0:
                        pool.wait_ge(x_done[4].sem, x_done[4].count(g, 0))
                    m = part
                    pool.wait_ge(C.drained(5 + m), C.full(g, 5 + m))
                    add_input(3, g, m, c_o[:, m, :], X[2][:, m, :, :])

            def stage3(i, part, g):
                rstd_of(3, i, g, D)

            nc.gpsimd.memset(ones[:, :], 1.0).then_inc(pads_zero, 1)
            nc.gpsimd.memset(root[:, :], -0.5).then_inc(pads_zero, 1)
            nc.gpsimd.memset(s_half[:, :], 0.5).then_inc(pads_zero, 1)
            for t in (a_pad[:, :, :, :], c_flat[:, :], d_pad[:, :, :, :]):
                nc.gpsimd.memset(t, 0.0).then_inc(pads_zero, 1)
            nc.gpsimd.memset(b_xc[:, :, :, :], 0.0).then_inc(pads_zero, 1)
            pool.wait_ge(pads_zero, NZERO)
            pool.wait_ge(setup_p, 1)
            tt(bn_r[:, :], bn_t[:, :], root[:, :], ALU.pow).then_inc(setup_s, 1)
            pool.wait_ge(setup_p, 2)
            tt(s_a[:, 8:10], s_a[:, 6:8], s_half[:, 0:2], ALU.pow).then_inc(setup_s, 1)
            pool.wait_ge(setup, 2)
            for_rounds(pool, "gpsimd", [stage0, stage1, stage2, stage3])

        @block.vector
        def _(v):
            def tt(o, x, y, op):
                return nc.vector.tensor_tensor(out=o, in0=x, in1=y, op=op)

            def ts(o, x, s1, s2, op0, op1=None):
                if op1 is None:
                    return nc.vector.tensor_scalar(o, x, s1, None, op0)
                return nc.vector.tensor_scalar(o, x, s1, s2, op0, op1)

            def stt(o, x, s, y, op0, op1):
                return nc.vector.scalar_tensor_tensor(out=o, in0=x, scalar=s, in1=y, op0=op0, op1=op1)

            chains = {s: Chain(sem(f"vector_chain{s}"), n) for s, n in enumerate(VECTOR_STEPS)}

            def norm(s, i, g, bank, ready):
                ch = chains[s]
                if i == 0:
                    v.wait_ge(ready.sem, ready.count(g))
                    for c in range(CC):
                        for b in range(G):
                            nc.vector.bn_stats(st[s][:, 2 * c + b, :], X[s][:, c, b, :]).then_inc(ch.sem, ch.step())
                    v.wait_ge(ch.sem, ch.count(g))
                    tt(mv[s][:, :, 1], st[s][:, :, 2], st[s][:, :, 5], ALU.add).then_inc(ch.sem, ch.step())
                    tt(mv[s][:, :, 0], st[s][:, :, 1], st[s][:, :, 4], ALU.add).then_inc(stats[s].sem, 1)
                if i == 1:
                    v.wait_ge(bank.filled(0), bank.full(g, 0))
                    t = bank.tile(0)
                    nc.vector.tensor_copy(gm[s][:, :], t[:, 0:4]).then_inc(ch.sem, ch.step())
                    even_odd = st[s][:, :, :].rearrange("p j (e k) -> p j e k", e=2)[:, :, :, 1]
                    tt(dm[s][:, :, :], even_odd, t[:, 0:4].unsqueeze(2).to_broadcast([128, 4, 2]),
                                    ALU.subtract).then_inc(bank.drained(0), 1)
                    v.wait_ge(bank.drained(0), bank.full(g, 0))
                    tt(dd[s][:, :, :], dm[s][:, :, :], dm[s][:, :, :], ALU.mult).then_inc(ch.sem, ch.step())
                    v.wait_ge(ch.sem, ch.count(g))
                    tt(ve[s][:, :], dd[s][:, :, 0], dd[s][:, :, 1], ALU.add).then_inc(ch.sem, ch.step())
                    v.wait_ge(ch.sem, ch.count(g))
                    stt(dq[s][:, :], mv[s][:, :, 1], 2.0 / N, ve[s][:, :], ALU.mult, ALU.add)\
                        .then_inc(spread[s].sem, 1)
                if i == 2:
                    v.wait_ge(bank.filled(1), bank.full(g, 1))
                    t = bank.tile(1)
                    ts(ve[s][:, :], t[:, 0:4], GN_EPS, None, ALU.add).then_inc(bank.drained(1), 1)
                if i == 3 and s >= 2:
                    v.wait_ge(rstd[s].sem, rstd[s].count(g))
                    stt(gs[s][:, :], gm[s][:, :], -1.0, rs[s][:, :], ALU.mult, ALU.mult)\
                        .then_inc(norm_shift[s].sem, 1)
                elif i == 3:
                    v.wait_ge(rstd[s].sem, rstd[s].count(g))
                    for c in range(CC):
                        for b in range(G):
                            j = 2 * c + b
                            ts(Y[s][:, c, b, :], X[s][:, c, b, :], gm[s][:, j:j + 1], rs[s][:, j:j + 1],
                               ALU.subtract, ALU.mult).then_inc(normed[s].sem, 1)

            def stage0(i, part, g):
                ch = chains[0]
                norm(0, i, g, A, x_in)

                def sigmoid(j, f):
                    v.wait_ge(A.drained(f), A.full(g, f))
                    ts(a_rw[:, j].rearrange("p b e -> p (b e)"), a_e[:, :], 0.5, 0.5, ALU.mult, ALU.add)\
                        .then_inc(ch.sem, ch.step())
                    v.wait_ge(ch.sem, ch.count(g))

                def mix(j, ws, outs):
                    e = part
                    for b in range(G):
                        r = a_rw[:, j, b, e:e + 1]
                        if e == 0:
                            ins = ts(outs(b), ws(e), r, None, ALU.mult)
                        else:
                            v.wait_ge(ch.sem, ch.count(g, 1))
                            ins = stt(outs(b), ws(e), r, outs(b), ALU.mult, ALU.add)
                        if e == EXPERTS - 1 and b == G - 1:
                            ins.then_inc(a_mix.sem, 1)
                        else:
                            ins.then_inc(ch.sem, ch.step())

                if i == 3:
                    tt(a_mo[:, :], dm[0][:, :, 0], dm[0][:, :, 1], ALU.add).then_inc(ch.sem, ch.step())
                    v.wait_ge(ch.sem, ch.count(g))
                    stt(a_md[:, :], a_mo[:, :], 0.5, rs[0][:, :], ALU.mult, ALU.mult).then_inc(a_md_ok.sem, 1)
                if i == 4:
                    if part == 0:
                        sigmoid(0, 2)
                    mix(0, lambda e: w1[:, e, :], lambda b: a_w1[:, b].rearrange("p c o -> p (c o)"))
                if i in (5, 8):
                    j = i // 8
                    v.wait_ge(A.drained((3, 5)[j]), A.full(g, (3, 5)[j]))
                    ts(a_mean[0:MID, j, :], a_sum[0:MID, j, :], 1.0 / N, None, ALU.mult).then_inc(a_mn.sem, 1)
                if i == 7:
                    if part == 0:
                        sigmoid(1, 4)
                    mix(1, lambda e: w2[:, e, :], lambda b: a_w2[:, b].rearrange("p j o -> p (j o)"))
                if i == 9:
                    if part == 0:
                        sigmoid(2, 6)
                    mix(2, lambda e: w3[:, e, :], lambda b: a_w3[:, b, :])
                if i == 10:
                    m = part
                    v.wait_ge(A.filled(7 + m), A.full(g, 7 + m))
                    t = A.tile(7 + m)
                    stt(a_t[:, m, :], t[:, 0:W], bn_s[:, BN_A3 + m:BN_A3 + m + 1],
                                  Y[0][:, m].rearrange("p b n -> p (b n)"), ALU.mult, ALU.add).then_inc(A.drained(7 + m), 1)

            def stage1(i, part, g):
                ch = chains[1]
                norm(1, i, g, B, x_done[1])
                if i == 5 and part == 0:
                    v.wait_ge(B.drained(2), B.full(g, 2))
                    v.wait_ge(B.drained(3), B.full(g, 3))
                    for c in range(CC):
                        w = [cvec[:, 6 + 3 * c + j:7 + 3 * c + j] for j in range(3)]
                        ts(b_xf[:, c], b_xc[:, c, :, 0:N], w[0], cvec[:, 12 + c:13 + c], ALU.mult, ALU.add).then_inc(ch.sem, ch.step())
                if i == 5 and part > 0:
                    j = part
                    for c in range(CC):
                        v.wait_ge(ch.sem, ch.count(g, 1))
                        ins = stt(b_xf[:, c], b_xc[:, c, :, j:j + N], cvec[:, 6 + 3 * c + j:7 + 3 * c + j],
                                  b_xf[:, c], ALU.mult, ALU.add)
                        if j == 1 or c == 0:
                            ins.then_inc(ch.sem, ch.step())
                    if part == 2:
                        ins.then_inc(b_dw.sem, 1)
                if i in (6, 7):
                    f, dst = ((8, XT), (12, XP))[i - 6]
                    k = 2 * part + 1
                    v.wait_ge(B.filled(f + k), B.full(g, f + k))
                    t = B.tile(f + k)
                    nc.vector.tensor_copy(
                        dst[:, k // 2, k % 2, :, :],
                        t[0:HT, 0:HEADS * XD].rearrange("p (h x) -> p h x", h=HEADS)).then_inc(B.drained(f + k), 1)
                if i == 8:
                    xp = XP[:, :, :, :, :].rearrange("p t b h x -> p (t b h) x")
                    Cm = xp[:, :, HD + 1 + STATE:XD]
                    at, upto = k98("at"), k98("upto")
                if i == 8 and part == 0:
                    v.wait_ge(B.drained(13), B.full(g, 13))
                    v.wait_ge(B.drained(14), B.full(g, 14))
                    v.wait_ge(B.drained(15), B.full(g, 15))
                    tt(CD[:, :, :, :], Cm.unsqueeze(3).to_broadcast([HT, Q8, STATE, CHUNK]),
                       at.unsqueeze(1).unsqueeze(1).to_broadcast([HT, Q8, STATE, CHUNK]), ALU.mult)\
                        .then_inc(b_cd.sem, 1)
                if i == 8 and part == 1:
                    v.wait_ge(b_e.sem, b_e.count(g))
                    ts(b_u[:, :], b_ex[:, :], 1.0, None, ALU.add).then_inc(b_u_ok.sem, 1)
                    v.wait_ge(b_u_ok.sem, b_u_ok.count(g))
                    ts(b_wm[:, :], b_u[:, :], -1.0, None, ALU.add).then_inc(ch.sem, ch.step())
                    v.wait_ge(ch.sem, ch.count(g))
                    ts(b_m[:, :], b_wm[:, :], 0.0, None, ALU.is_equal).then_inc(ch.sem, ch.step())
                    v.wait_ge(ch.sem, ch.count(g))
                    tt(b_de[:, :], b_wm[:, :], b_m[:, :], ALU.add).then_inc(ch.sem, ch.step())
                    v.wait_ge(ch.sem, ch.count(g))
                    nc.vector.reciprocal(b_rc[:, :], b_de[:, :]).then_inc(ch.sem, ch.step())
                if i == 8 and part == 2:
                    v.wait_ge(b_l.sem, b_l.count(g))
                    tt(b_nu[:, :], b_ln[:, :], b_m[:, :], ALU.add).then_inc(ch.sem, ch.step())
                    v.wait_ge(ch.sem, ch.count(g))
                    tt(b_de[:, :], b_nu[:, :], b_ex[:, :], ALU.mult).then_inc(ch.sem, ch.step())
                    v.wait_ge(ch.sem, ch.count(g))
                    tt(b_sp[:, :], b_de[:, :], b_rc[:, :], ALU.mult).then_inc(ch.sem, ch.step())
                    v.wait_ge(ch.sem, ch.count(g))
                    stt(dt[:, :].unsqueeze(2), xp[:, :, HD:HD + 1], 0.0, b_sp[:, :].unsqueeze(2), ALU.max, ALU.add).then_inc(ch.sem, ch.step())
                    v.wait_ge(ch.sem, ch.count(g))
                    tt(rD[:, :, :], dt[:, :].unsqueeze(2).to_broadcast([HT, Q8, CHUNK]),
                       upto.unsqueeze(1).to_broadcast([HT, Q8, CHUNK]), ALU.mult).then_inc(b_rd.sem, 1)
                if i == 8 and part == 3:
                    tt(DU0[:, :, :], dt[:, 0:4].unsqueeze(2).to_broadcast([HT, 4, N]),
                       k98("tri0").unsqueeze(1).to_broadcast([HT, 4, N]), ALU.mult)
                if i == 8 and part == 4:
                    tt(DU1[:, :, :], dt[:, 4:8].unsqueeze(2).to_broadcast([HT, 4, HT]),
                       k98("tri1").unsqueeze(1).to_broadcast([HT, 4, HT]), ALU.mult).then_inc(b_du.sem, 1)
                if i == 8 and part == 5:
                    tt(dB[:, :, :], xp[:, :, HD + 1:HD + 1 + STATE],
                              dt[:, :].unsqueeze(2).to_broadcast([HT, Q8, STATE]), ALU.mult).then_inc(ch.sem, ch.step())
                if i == 9:
                    v.wait_ge(B.filled(16), B.full(g, 16))
                    t = B.tile(16)
                    D3 = t[0:HT, 0:Q8 * CHUNK].rearrange("p (r h t) -> p h r t", h=HEADS, t=CHUNK)
                    for h in range(HEADS):
                        ins = tt(AD[:, :, :, :].rearrange("p (r h) s t -> p h r s t", h=HEADS)[:, h],
                                 D3[:, h].unsqueeze(2).to_broadcast([HT, 4, STATE, CHUNK]),
                                 b_A[0:HT, h * STATE:(h + 1) * STATE].unsqueeze(1).unsqueeze(3)
                                 .to_broadcast([HT, 4, STATE, CHUNK]), ALU.mult)
                    ins.then_inc(B.drained(16), 1)
                if i == 10 and part == 0:
                    v.wait_ge(b_ee.sem, b_ee.count(g))
                    v.wait_ge(ch.sem, ch.count(g))
                    tt(FF[:, :, :], EE[:, :, :, CHUNK - 1], dB[:, :, :], ALU.mult).then_inc(b_ff.sem, 1)
                if i == 10 and part == 1:
                    for k in range(2):
                        v.wait_ge(B.filled(19 + k), B.full(g, 19 + k))
                        t = B.tile(19 + k)
                        tt(M1[:, 4 * k:4 * k + 4].rearrange("p q s t -> p (q s t)"),
                                     EE[:, 4 * k:4 * k + 4].rearrange("p q s t -> p (q s t)"), t[0:HT, 0:448],
                                     ALU.mult).then_inc(B.drained(19 + k), 1)
                if i == 10 and part == 2:
                    v.wait_ge(B.drained(19), B.full(g, 19))
                    v.wait_ge(B.drained(20), B.full(g, 20))
                    tt(M2[:, :, :, :], M1[:, :, :, :],
                              dB[:, :, :].unsqueeze(3).to_broadcast([HT, Q8, STATE, CHUNK]), ALU.mult).then_inc(ch.sem, ch.step())
                    v.wait_ge(ch.sem, ch.count(g))
                    nc.vector.tensor_reduce(MC[:, :, :], M2[:, :, :, :].rearrange("p q s t -> p q t s"),
                                                   AX.X, ALU.add).then_inc(ch.sem, ch.step())
                if i == 10 and part == 3:
                    v.wait_ge(ch.sem, ch.count(g))
                    tt(MC2[:, :, :], MC[:, :, :],
                              k98("upto").unsqueeze(1).to_broadcast([HT, Q8, CHUNK]), ALU.mult).then_inc(ch.sem, ch.step())
                    v.wait_ge(ch.sem, ch.count(g))
                    tt(MC3[:, :, :].rearrange("p (r h) t -> p r (h t)", h=HEADS),
                              MC2[:, :, :].rearrange("p (r h) t -> p r (h t)", h=HEADS),
                              b_De[:, :, :].rearrange("p h t -> p (h t)").unsqueeze(1)
                              .to_broadcast([HT, 4, HEADS * CHUNK]), ALU.add).then_inc(ch.sem, ch.step())
                if i == 10 and part == 4:
                    v.wait_ge(ch.sem, ch.count(g))
                    tt(MB[:, :, :, :], MC3[:, :, :].unsqueeze(2).to_broadcast([HT, Q8, CPT, CHUNK]),
                       k98("chunk7").unsqueeze(1).unsqueeze(3).to_broadcast([HT, Q8, CPT, CHUNK]), ALU.mult)\
                        .then_inc(b_mb.sem, 1)
                if i == 10 and part == 5:
                    v.wait_ge(B.drained(17), B.full(g, 17))
                    v.wait_ge(B.drained(18), B.full(g, 18))
                    for b in range(G):
                        v.wait_ge(B.filled(21 + b), B.full(g, 21 + b))
                        t = B.tile(21 + b)
                        tt(RR[:, 2 * b:2 * b + 2, :].rearrange("p h n -> p (h n)"),
                                     RE[:, 2 * b:2 * b + 2, :].rearrange("p h n -> p (h n)"), t[0:CS, 0:W],
                                     ALU.mult).then_inc(B.drained(21 + b), 1)
                if i == 12:
                    v.wait_ge(B.filled(25), B.full(g, 25))
                    t = B.tile(25)
                    nc.vector.tensor_copy(YT[:, 1, :, :, 0:HD].rearrange("p b h d -> p (b h) d"),
                                                   t[0:HT, 0:4 * HD].rearrange("p (j d) -> p j d", d=HD)).then_inc(B.drained(25), 1)
                if i == 13:
                    if part == 0:
                        v.wait_ge(b_gate_ok.sem, b_gate_ok.count(g))
                    h = part
                    v.wait_ge(B.filled(26 + h), B.full(g, 26 + h))
                    t = B.tile(26 + h)
                    tt(b_y1[:, h, :], b_gate[:, h, :], t[:, 0:W], ALU.mult).then_inc(B.drained(26 + h), 1)

            def stage2(i, part, g):
                norm(2, i, g, C, x_done[2])
                J = 2 * TAPS
                if i == 4 and part == 0:
                    v.wait_ge(C.filled(3), C.full(g, 3))
                    t = C.tile(3)
                    tt(c_py[:, :, :].rearrange("p (m b) j -> p m b j", b=G),
                                 t[0:HS, 0:4 * J].rearrange("p (m b j) -> p m b j", m=2, b=G),
                                 k128("grid")[0:HS].rearrange("p (m j) -> p m j", m=2).unsqueeze(2)
                                 .to_broadcast([HS, 2, G, J]), ALU.add).then_inc(C.drained(3), 1)
                if i == 4 and part == 1:
                    v.wait_ge(C.drained(3), C.full(g, 3))
                    tt(c_df[:, :, :], c_py[:, :, :].rearrange("p q j -> p (q j)").unsqueeze(2)
                       .to_broadcast([HS, 4 * J, HW]),
                       k128("iota14")[0:HS].unsqueeze(1).to_broadcast([HS, 4 * J, HW]), ALU.subtract).then_inc(c_df_ok.sem, 1)
                if i == 5:
                    k = 2 * part + 1
                    v.wait_ge(CT.filled(k), CT.full(g, k))
                    t = CT.tile(k)
                    w = TAPS * MID // 2
                    h = k // 2 % 2
                    nc.vector.tensor_copy(c_z[:, k // 4, 1, h * w:(h + 1) * w], t[0:HT, 0:w]).then_inc(CT.drained(k), 1)
                if i == 6:
                    if part == 0:
                        v.wait_ge(c_te_ok.sem, c_te_ok.count(g))
                    t = part
                    bilinear(tt, t, 0).then_inc(c_wt_v.sem, 1)
                if i == 7:
                    k = G * part + 1
                    v.wait_ge(CT.filled(8 + k), CT.full(g, 8 + k))
                    t = CT.tile(8 + k)
                    nc.vector.tensor_copy(c_wm[k % G][:, :, :].rearrange("p m (y x) -> p (m y) x", x=HW),
                                                     in_rows(t)).then_inc(CT.drained(8 + k), 1)

            def stage3(i, part, g):
                ch = chains[3]
                norm(3, i, g, D, x_done[3])
                if i == 3:
                    v.wait_ge(D.drained(2), D.full(g, 2))
                    for b in range(G):
                        for h in range(2):
                            part, r0 = slice(h * MID, (h + 1) * MID), 1 - h
                            last = ts(d_pad[part, b, r0:r0 + HW, 1:1 + HW],
                                      d_sq[half(b), :].rearrange("p (y x) -> p y x", x=HW),
                                      bn_s[half(b), BN_D1:BN_D1 + 1], bn_b[half(b), BN_D1:BN_D1 + 1],
                                      ALU.mult, ALU.add)
                    last.then_inc(d_h1.sem, 1)
                if i == 5:
                    v.wait_ge(D.drained(3), D.full(g, 3))
                    for b in range(G):
                        last = ts(d_h2[:, b * N:(b + 1) * N], d_sq2[half(b), :], bn_s[half(b), BN_D2:BN_D2 + 1],
                                  bn_b[half(b), BN_D2:BN_D2 + 1], ALU.mult, ALU.add)
                    last.then_inc(d_h2_ok.sem, 1)
                if i == 6:
                    m = part
                    v.wait_ge(D.drained(4 + m), D.full(g, 4 + m))
                    j = BN_D3 + m
                    stt(d_t[:, m, :], d_sq3[:, m, :], bn_s[:, j:j + 1],
                               Y[3][:, m].rearrange("p b n -> p (b n)"), ALU.mult, ALU.add).then_inc(ch.sem, ch.step())
                    v.wait_ge(ch.sem, ch.count(g))
                    ins = stt(OUT[:, m].rearrange("p b n -> p (b n)"), d_t[:, m, :], bn_b[:, j:j + 1],
                              X[3][:, m].rearrange("p b n -> p (b n)"), ALU.add, ALU.add)
                    if part == CC - 1:
                        ins.then_inc(x_done[4].sem, 1)

            at = [0]

            def link(ins):
                ins.then_inc(setup_v, 1)
                at[0] += 1
                v.wait_ge(setup_v, at[0])

            v.wait_ge(consts_in, ALL_IN)
            ts(bn_t[:, :], bnp[:, 3, :], BN_EPS, None, ALU.add).then_inc(setup_p, 1)
            link(tt(bn_b[:, :], bnp[:, 4, :], bnp[:, 2, :], ALU.subtract))
            v.wait_ge(setup_pe, 1)
            nc.vector.tensor_copy(rowb[:, :], ps[0][:, 0:ROW_BC]).then_inc(setup_r, 1)
            v.wait_ge(setup_r, 1)
            v.wait_ge(setup_s, 1)
            link(tt(bn_s[:, :], bnp[:, 0, :], bn_r[:, :], ALU.mult))
            link(tt(bn_b[:, :], bn_b[:, :], bn_s[:, :], ALU.mult))
            link(tt(bn_b[:, :], bn_b[:, :], bnp[:, 1, :], ALU.add))
            mob = rowb[:, ROW_MOB:ROW_BC].rearrange("p (h j) -> p h j", j=4)
            link(tt(s_a[:, 0:2], mob[:, :, 0], mob[:, :, 3], ALU.mult))
            link(tt(s_a[:, 2:4], mob[:, :, 1], mob[:, :, 2], ALU.mult))
            link(tt(s_a[:, 4:6], s_a[:, 0:2], s_a[:, 2:4], ALU.subtract))
            link(ts(s_a[:, 0:2], s_a[:, 4:6], -1.0, None, ALU.mult))
            link(tt(s_a[:, 2:4], s_a[:, 0:2], s_a[:, 4:6], ALU.max))
            ts(s_a[:, 6:8], s_a[:, 2:4], 0.001, None, ALU.max).then_inc(setup_p, 1)
            v.wait_ge(setup_s, 2)
            link(nc.vector.reciprocal(s_a[:, 10:12], s_a[:, 8:10]))
            link(tt(s_m[:, :, :], mob, s_a[:, 10:12].unsqueeze(2).to_broadcast([128, HEADS, 4]), ALU.mult))
            xs, ys = k98("xs"), k98("ys")
            for h in range(HEADS):
                ca, cb, cc_, cd = (s_m[0:HT, h, j:j + 1] for j in range(4))
                u = [s_w[:, j, :] for j in range(8)]
                link(ts(u[0], xs, ca, cb, ALU.mult, ALU.add))
                link(ts(u[1], ys, ca, None, ALU.mult))
                link(ts(u[2], xs, cc_, cd, ALU.mult, ALU.add))
                link(ts(u[2], u[2], 1e-6, None, ALU.add))
                link(ts(u[3], ys, cc_, None, ALU.mult))
                link(tt(u[4], u[2], u[2], ALU.mult))
                link(tt(u[5], u[3], u[3], ALU.mult))
                link(tt(u[4], u[4], u[5], ALU.add))
                link(nc.vector.reciprocal(u[5], u[4]))
                link(tt(u[6], u[0], u[2], ALU.mult))
                link(tt(u[7], u[1], u[3], ALU.mult))
                link(tt(u[6], u[6], u[7], ALU.add))
                link(tt(u[6], u[6], u[5], ALU.mult))
                link(tt(u[4], u[1], u[2], ALU.mult))
                link(tt(u[7], u[0], u[3], ALU.mult))
                link(tt(u[4], u[4], u[7], ALU.subtract))
                link(tt(u[4], u[4], u[5], ALU.mult))
                link(stt(S[:, h, :], u[4], 1.3, u[6], ALU.mult, ALU.add))
                for n in range(2):
                    r = [s_rank[:, n, h, j:j + 1] for j in range(4)]
                    link(tt(u[0], S[:, h, :], k98("self", 2, N)[:, n], ALU.mult))
                    link(nc.vector.tensor_reduce(r[0], u[0], AX.X, ALU.add))
                    link(ts(u[1], S[:, h, :], r[0], None, ALU.is_lt))
                    link(ts(u[2], S[:, h, :], r[0], None, ALU.is_equal))
                    link(tt(u[2], u[2], k98("before", 2, N)[:, n], ALU.mult))
                    link(tt(u[1], u[1], u[2], ALU.add))
                    link(nc.vector.tensor_reduce(r[1], u[1], AX.X, ALU.add))
                    link(ts(PM[:, n, h, :], k98("iota196"), r[1], None, ALU.is_equal))
            nc.vector.memset(s_a[:, 12:13], 0.0).then_inc(setup, 1)
            for h in range(HEADS):
                ts(b_De[:, h, :], k98("at"), rowb[0:HT, ROW_D + h:ROW_D + h + 1], None, ALU.mult)
            v.wait_ge(setup_a, 1)
            for m in range(2):
                for h in range(HEADS):
                    tt(b_MA[:, m, h], k98("after", 2, NCH)[:, m].unsqueeze(2).to_broadcast([HT, NCH, STATE]),
                       b_A[0:HT, h * STATE:(h + 1) * STATE].unsqueeze(1).to_broadcast([HT, NCH, STATE]), ALU.mult)
            v.wait_ge(setup_pe, 2)
            for h in range(HEADS):
                last = nc.vector.tensor_copy(PT[:, :, h, :], ps[1 + h][0:HT, 0:2 * N].rearrange("p (t n) -> p t n", t=2))
            last.then_inc(setup, 1)
            for_rounds(v, "vector", [stage0, stage1, stage2, stage3], chains)


def kernel(**inputs):
    import numpy as np
    import concourse.bacc as bacc
    from concourse.bass_utils import run_bass_kernel_spmd

    f = {k: np.asarray(x) for k, x in inputs.items()}

    def halves(x):
        return np.concatenate([x, x], 0)

    def chan(x):
        return x.reshape(CC, 128, -1).transpose(1, 0, 2)

    def taps(w):
        w = np.moveaxis(w, (-3, -2, -1), (0, 1, 2))
        w = np.moveaxis(w, (1, 2), (-3, -2))
        low = np.concatenate([w[..., 0, :, :], w[..., 2, :, :]], -2)
        high = np.concatenate([w[..., 1, :, :], np.zeros_like(w[..., 2, :, :])], -2)
        return np.concatenate([low, high], 0)

    def bn_columns(names):
        cols = np.zeros((128, NBN), np.float32)
        for j, name in names.items():
            x = f[name]
            if x.size == MID:
                cols[:, j] = halves(x)
            else:
                cols[:, j:j + 2] = x.reshape(CC, 128).T
        return cols

    def bn_names(l0, l2, l3):
        return {**{BN_A1 + n: f"L0_conv_bn{n + 1}_{l0}" for n in range(3)},
                **{BN_C1 + n: f"L2_conv_bn{n + 1}_{l2}" for n in range(3)},
                **{BN_D1 + n: f"L3_conv_{l3}{n + 1}" for n in range(3)}}

    at98, c98, at128, c128, at_scan, c_scan = shape_constants()
    bias_names = {BN_C1: "L2_conv_conv1_b", BN_C2: "L2_conv_dconv_b", BN_C3: "L2_conv_conv2_b"}
    w1 = f["L0_conv_w1"].reshape(EXPERTS, MID, CC, 128).transpose(3, 0, 2, 1)
    w3 = f["L0_conv_w3"].reshape(EXPERTS, 2, 128, MID).transpose(1, 3, 0, 2)
    arrays = {
        "x": f["x"].reshape(BATCH, CH, N),
        "c98": c98, "c128": c128, "c_scan": c_scan,
        "bnp": np.stack([bn_columns(bn_names(k, k, k)) for k in "gbmv"] + [bn_columns(bias_names)], 1),
        "rows": np.concatenate([f[n].reshape(-1) for n in (
            "L1_conv_A_log", "L1_conv_Dparam", "L1_conv_mobius", "L0_conv_r1_b", "L0_conv_r2_b", "L0_conv_r3_b",
            "L1_conv_dbc_b", "L2_conv_off_b")])[None],
        "w1": w1.reshape(128, EXPERTS, CC * MID),
        "w2": taps(f["L0_conv_w2"]).reshape(128, EXPERTS, 6 * MID),
        "w3": w3.reshape(128, EXPERTS, 128),
        "r1": chan(f["L0_conv_r1_w"]),
        "r23": np.stack([f["L0_conv_r2_w"], f["L0_conv_r3_w"]], 1),
        "inw": chan(f["L1_conv_in_proj_w"].T).reshape(128, CC, 6, 128),
        "cvec": np.concatenate([f["L1_conv_in_proj_b"].reshape(6, 128).T, chan(f["L1_conv_dw_w"]).reshape(128, 6),
                                f["L1_conv_dw_b"].reshape(CC, 128).T, f["L1_conv_out_proj_b"].reshape(CC, 128).T], 1),
        "dbcw": chan(f["L1_conv_dbc_w"].T).reshape(128, CC, HEADS, DBC),
        "outw": chan(f["L1_conv_out_proj_w"].T).reshape(128, CC, 2, 128),
        "c1w": chan(f["L2_conv_conv1_w"].T),
        "offw": taps(f["L2_conv_off_w"]),
        "dcw": halves(f["L2_conv_dconv_w"].reshape(MID, MID, TAPS).transpose(1, 2, 0).reshape(MID, TAPS * MID)),
        "c2w": f["L2_conv_conv2_w"].T,
        "d1w": chan(f["L3_conv_w1"].reshape(MID, CH).T),
        "d2w": taps(f["L3_conv_w2"]),
        "d3w": f["L3_conv_w3"].reshape(CH, MID).T,
    }
    nc = bacc.Bacc("TRN2", target_bir_lowering=False, num_devices=1)
    args = {}
    for name, x in arrays.items():
        arrays[name] = x = np.ascontiguousarray(x)
        args[name] = nc.dram_tensor(f"in_{name}", x.shape, F32, kind="ExternalInput").ap()
    out = nc.dram_tensor("out_0", (BATCH, CH, N), F32, kind="ExternalOutput").ap()
    build(nc, args, out, at98, at128, at_scan)
    r = run_bass_kernel_spmd(nc, [{f"in_{k}": x for k, x in arrays.items()}], core_ids=[0])
    return r.results[0]["out_0"].reshape(BATCH, CH, HW, HW)
```
